# Optimizing a Trainium2 kernel written in Bass

```python
import numpy as np
import jax
import jax.numpy as jnp

def _softmax(x, axis=-1):
    return jax.nn.softmax(x, axis=axis)

def _gelu(x):
    return jax.nn.gelu(x, approximate=True)

def _silu(x):
    return jax.nn.silu(x)

def _sigmoid(x):
    return jax.nn.sigmoid(x)

def _layernorm(x, axis=-1, eps=1e-05):
    m = jnp.mean(x, axis=axis, keepdims=True)
    v = jnp.var(x, axis=axis, keepdims=True)
    return (x - m) / jnp.sqrt(v + eps)

def _scatter_add(tgt, idx, src, axis=0):
    return tgt.at[idx].add(src)

def _segment_sum(src, seg, n):
    return jax.ops.segment_sum(src, seg, n)
kernel_name = 'mk_macaron_d1_jaxref_r8_b701f2'

def setup_inputs(seed: int=0):
    np.random.seed(seed)
    _w = jnp.asarray

    def _L0_attn_setup():
        import jax, jax.numpy as jnp
        import numpy as np
        DIM = 128
        DIM_HEAD = 64
        HEADS = 8
        INNER = DIM_HEAD * HEADS
        SCALE = DIM_HEAD ** (-0.5)
        COS_SCALE = 1.0

        def layer_norm(x, w, b, eps=1e-05):
            mu = jnp.mean(x, axis=-1, keepdims=True)
            var = jnp.var(x, axis=-1, keepdims=True)
            return (x - mu) * jax.lax.rsqrt(var + eps) * w + b
        key = jax.random.key(seed)
        ks = jax.random.split(key, 6)
        x = jax.random.normal(ks[0], (4, 256, DIM), dtype=jnp.float32)
        Wq = jax.random.normal(ks[1], (DIM, INNER), dtype=jnp.float32) * DIM ** (-0.5)
        Wkv = jax.random.normal(ks[2], (DIM, 2 * DIM_HEAD), dtype=jnp.float32) * DIM ** (-0.5)
        Wo = jax.random.normal(ks[3], (INNER, DIM), dtype=jnp.float32) * INNER ** (-0.5)
        norm_w = jnp.ones((DIM,), jnp.float32)
        norm_b = jnp.zeros((DIM,), jnp.float32)
        out_norm_w = jnp.ones((DIM,), jnp.float32)
        out_norm_b = jnp.zeros((DIM,), jnp.float32)
        return {'x': x, 'Wq': Wq, 'Wkv': Wkv, 'Wo': Wo, 'norm_w': norm_w, 'norm_b': norm_b, 'out_norm_w': out_norm_w, 'out_norm_b': out_norm_b}
    _L0_attn_in = _L0_attn_setup()

    def _L0_ffn_setup():
        import jax, jax.numpy as jnp
        import numpy as np
        D_MODEL = 128
        N_HEADS = 16
        HEAD_DIM = D_MODEL // N_HEADS
        KV_LATENT = 64
        N_EXPERTS = 4
        D_HIDDEN = 4 * D_MODEL
        B, T = (2, 128)

        def rmsnorm(x, w, eps=1e-06):
            return w * (x * jax.lax.rsqrt(jnp.mean(x * x, axis=-1, keepdims=True) + eps))

        def layernorm(x, g, b, eps=1e-05):
            mu = jnp.mean(x, axis=-1, keepdims=True)
            var = jnp.mean((x - mu) ** 2, axis=-1, keepdims=True)
            return (x - mu) * jax.lax.rsqrt(var + eps) * g + b

        def apply_rope(x):
            t, d = (x.shape[2], x.shape[3])
            half = d // 2
            pos = jnp.arange(t, dtype=x.dtype)[:, None]
            inv_freq = 1.0 / 10000.0 ** (jnp.arange(half, dtype=x.dtype) / half)
            ang = pos * inv_freq[None, :]
            sin, cos = (jnp.sin(ang), jnp.cos(ang))
            x1, x2 = (x[..., :half], x[..., half:])
            return jnp.concatenate([x1 * cos - x2 * sin, x1 * sin + x2 * cos], axis=-1)

        def mla_attention(x, Wq, Wdkv, Wuk, Wuv, Wo, ln_g, ln_b):
            b, t, _ = x.shape
            q = (x @ Wq.T).reshape(b, t, N_HEADS, HEAD_DIM).transpose(0, 2, 1, 3)
            latent = layernorm(x @ Wdkv.T, ln_g, ln_b)
            k = (latent @ Wuk.T).reshape(b, t, N_HEADS, HEAD_DIM).transpose(0, 2, 1, 3)
            v = (latent @ Wuv.T).reshape(b, t, N_HEADS, HEAD_DIM).transpose(0, 2, 1, 3)
            q = apply_rope(q)
            k = apply_rope(k)
            scores = jnp.einsum('bhqd,bhkd->bhqk', q, k) / np.sqrt(HEAD_DIM)
            causal = jnp.tril(jnp.ones((t, t), dtype=bool))
            scores = jnp.where(causal, scores, -jnp.inf)
            attn = jax.nn.softmax(scores, axis=-1)
            out = jnp.einsum('bhqk,bhkd->bhqd', attn, v).transpose(0, 2, 1, 3).reshape(b, t, D_MODEL)
            return out @ Wo.T

        def moe(x, gate_w, gate_b, W1, b1, W2, b2):
            logits = x @ gate_w.T + gate_b
            top = jnp.argmax(logits, axis=-1)
            onehot = jax.nn.one_hot(top, N_EXPERTS, dtype=x.dtype)
            h = jax.nn.relu(jnp.einsum('btd,ehd->bteh', x, W1) + b1)
            y = jnp.einsum('bteh,edh->bted', h, W2) + b2
            return jnp.einsum('bted,bte->btd', y, onehot)
        key = jax.random.key(seed)
        ks = jax.random.split(key, 16)
        s = lambda fan_in: 1.0 / np.sqrt(fan_in)
        return {'x': jax.random.normal(ks[0], (B, T, D_MODEL), jnp.float32), 'norm1_w': jnp.ones((D_MODEL,), jnp.float32), 'norm2_w': jnp.ones((D_MODEL,), jnp.float32), 'Wq': jax.random.normal(ks[1], (D_MODEL, D_MODEL), jnp.float32) * s(D_MODEL), 'Wdkv': jax.random.normal(ks[2], (KV_LATENT, D_MODEL), jnp.float32) * s(D_MODEL), 'Wuk': jax.random.normal(ks[3], (D_MODEL, KV_LATENT), jnp.float32) * s(KV_LATENT), 'Wuv': jax.random.normal(ks[4], (D_MODEL, KV_LATENT), jnp.float32) * s(KV_LATENT), 'Wo': jax.random.normal(ks[5], (D_MODEL, D_MODEL), jnp.float32) * s(D_MODEL), 'ln_g': jnp.ones((KV_LATENT,), jnp.float32), 'ln_b': jnp.zeros((KV_LATENT,), jnp.float32), 'gate_w': jax.random.normal(ks[6], (N_EXPERTS, D_MODEL), jnp.float32) * s(D_MODEL), 'gate_b': jnp.zeros((N_EXPERTS,), jnp.float32), 'W1': jax.random.normal(ks[7], (N_EXPERTS, D_HIDDEN, D_MODEL), jnp.float32) * s(D_MODEL), 'b1': jnp.zeros((N_EXPERTS, D_HIDDEN), jnp.float32), 'W2': jax.random.normal(ks[8], (N_EXPERTS, D_MODEL, D_HIDDEN), jnp.float32) * s(D_HIDDEN), 'b2': jnp.zeros((N_EXPERTS, D_MODEL), jnp.float32)}
    _L0_ffn_in = _L0_ffn_setup()
    _d = {'L0_attn_x': _L0_attn_in['x'], 'L0_attn_Wq': _L0_attn_in['Wq'], 'L0_attn_Wkv': _L0_attn_in['Wkv'], 'L0_attn_Wo': _L0_attn_in['Wo'], 'L0_attn_norm_w': _L0_attn_in['norm_w'], 'L0_attn_norm_b': _L0_attn_in['norm_b'], 'L0_attn_out_norm_w': _L0_attn_in['out_norm_w'], 'L0_attn_out_norm_b': _L0_attn_in['out_norm_b'], 'L0_ffn_norm1_w': _L0_ffn_in['norm1_w'], 'L0_ffn_norm2_w': _L0_ffn_in['norm2_w'], 'L0_ffn_Wq': _L0_ffn_in['Wq'], 'L0_ffn_Wdkv': _L0_ffn_in['Wdkv'], 'L0_ffn_Wuk': _L0_ffn_in['Wuk'], 'L0_ffn_Wuv': _L0_ffn_in['Wuv'], 'L0_ffn_Wo': _L0_ffn_in['Wo'], 'L0_ffn_ln_g': _L0_ffn_in['ln_g'], 'L0_ffn_ln_b': _L0_ffn_in['ln_b'], 'L0_ffn_gate_w': _L0_ffn_in['gate_w'], 'L0_ffn_gate_b': _L0_ffn_in['gate_b'], 'L0_ffn_W1': _L0_ffn_in['W1'], 'L0_ffn_b1': _L0_ffn_in['b1'], 'L0_ffn_W2': _L0_ffn_in['W2'], 'L0_ffn_b2': _L0_ffn_in['b2']}
    _x0 = _d['L0_attn_x']
    _d['L0_attn_x'] = jax.random.normal(jax.random.fold_in(jax.random.key(seed), 1), (16, 256, 128), dtype=_x0.dtype)
    del _x0
    return _d

def reference(L0_attn_x, L0_attn_Wq, L0_attn_Wkv, L0_attn_Wo, L0_attn_norm_w, L0_attn_norm_b, L0_attn_out_norm_w, L0_attn_out_norm_b, L0_ffn_norm1_w, L0_ffn_norm2_w, L0_ffn_Wq, L0_ffn_Wdkv, L0_ffn_Wuk, L0_ffn_Wuv, L0_ffn_Wo, L0_ffn_ln_g, L0_ffn_ln_b, L0_ffn_gate_w, L0_ffn_gate_b, L0_ffn_W1, L0_ffn_b1, L0_ffn_W2, L0_ffn_b2):

    def _L0_attn_ref(x, Wq, Wkv, Wo, norm_w, norm_b, out_norm_w, out_norm_b):
        import jax, jax.numpy as jnp
        import numpy as np
        DIM = 128
        DIM_HEAD = 64
        HEADS = 8
        INNER = DIM_HEAD * HEADS
        SCALE = DIM_HEAD ** (-0.5)
        COS_SCALE = 1.0

        def layer_norm(x, w, b, eps=1e-05):
            mu = jnp.mean(x, axis=-1, keepdims=True)
            var = jnp.var(x, axis=-1, keepdims=True)
            return (x - mu) * jax.lax.rsqrt(var + eps) * w + b
        b, n, _ = x.shape
        xn = layer_norm(x, norm_w, norm_b)
        q = xn @ Wq
        kv = xn @ Wkv
        k, v = (kv[..., :DIM_HEAD], kv[..., DIM_HEAD:])
        q = q.reshape(b, n, HEADS, DIM_HEAD).transpose(0, 2, 1, 3) * SCALE
        sim = jnp.einsum('bhid,bjd->bhij', q, k) * COS_SCALE
        attn = jax.nn.softmax(sim.astype(jnp.float32), axis=-1).astype(sim.dtype)
        out = jnp.einsum('bhij,bjd->bhid', attn, v)
        out = out.transpose(0, 2, 1, 3).reshape(b, n, INNER)
        out = out @ Wo
        return layer_norm(out, out_norm_w, out_norm_b)

    def _L0_ffn_ref(x, norm1_w, norm2_w, Wq, Wdkv, Wuk, Wuv, Wo, ln_g, ln_b, gate_w, gate_b, W1, b1, W2, b2):
        import jax, jax.numpy as jnp
        import numpy as np
        D_MODEL = 128
        N_HEADS = 16
        HEAD_DIM = D_MODEL // N_HEADS
        KV_LATENT = 64
        N_EXPERTS = 4
        D_HIDDEN = 4 * D_MODEL
        B, T = (2, 128)

        def rmsnorm(x, w, eps=1e-06):
            return w * (x * jax.lax.rsqrt(jnp.mean(x * x, axis=-1, keepdims=True) + eps))

        def layernorm(x, g, b, eps=1e-05):
            mu = jnp.mean(x, axis=-1, keepdims=True)
            var = jnp.mean((x - mu) ** 2, axis=-1, keepdims=True)
            return (x - mu) * jax.lax.rsqrt(var + eps) * g + b

        def apply_rope(x):
            t, d = (x.shape[2], x.shape[3])
            half = d // 2
            pos = jnp.arange(t, dtype=x.dtype)[:, None]
            inv_freq = 1.0 / 10000.0 ** (jnp.arange(half, dtype=x.dtype) / half)
            ang = pos * inv_freq[None, :]
            sin, cos = (jnp.sin(ang), jnp.cos(ang))
            x1, x2 = (x[..., :half], x[..., half:])
            return jnp.concatenate([x1 * cos - x2 * sin, x1 * sin + x2 * cos], axis=-1)

        def mla_attention(x, Wq, Wdkv, Wuk, Wuv, Wo, ln_g, ln_b):
            b, t, _ = x.shape
            q = (x @ Wq.T).reshape(b, t, N_HEADS, HEAD_DIM).transpose(0, 2, 1, 3)
            latent = layernorm(x @ Wdkv.T, ln_g, ln_b)
            k = (latent @ Wuk.T).reshape(b, t, N_HEADS, HEAD_DIM).transpose(0, 2, 1, 3)
            v = (latent @ Wuv.T).reshape(b, t, N_HEADS, HEAD_DIM).transpose(0, 2, 1, 3)
            q = apply_rope(q)
            k = apply_rope(k)
            scores = jnp.einsum('bhqd,bhkd->bhqk', q, k) / np.sqrt(HEAD_DIM)
            causal = jnp.tril(jnp.ones((t, t), dtype=bool))
            scores = jnp.where(causal, scores, -jnp.inf)
            attn = jax.nn.softmax(scores, axis=-1)
            out = jnp.einsum('bhqk,bhkd->bhqd', attn, v).transpose(0, 2, 1, 3).reshape(b, t, D_MODEL)
            return out @ Wo.T

        def moe(x, gate_w, gate_b, W1, b1, W2, b2):
            logits = x @ gate_w.T + gate_b
            top = jnp.argmax(logits, axis=-1)
            onehot = jax.nn.one_hot(top, N_EXPERTS, dtype=x.dtype)
            h = jax.nn.relu(jnp.einsum('btd,ehd->bteh', x, W1) + b1)
            y = jnp.einsum('bteh,edh->bted', h, W2) + b2
            return jnp.einsum('bted,bte->btd', y, onehot)
        x = x + mla_attention(rmsnorm(x, norm1_w), Wq, Wdkv, Wuk, Wuv, Wo, ln_g, ln_b)
        x = x + moe(rmsnorm(x, norm2_w), gate_w, gate_b, W1, b1, W2, b2)
        return x
    x = L0_attn_x
    x = x + 0.5 * _L0_ffn_ref(_layernorm(x, axis=-1), L0_ffn_norm1_w, L0_ffn_norm2_w, L0_ffn_Wq, L0_ffn_Wdkv, L0_ffn_Wuk, L0_ffn_Wuv, L0_ffn_Wo, L0_ffn_ln_g, L0_ffn_ln_b, L0_ffn_gate_w, L0_ffn_gate_b, L0_ffn_W1, L0_ffn_b1, L0_ffn_W2, L0_ffn_b2)
    x = x + _L0_attn_ref(_layernorm(x, axis=-1), L0_attn_Wq, L0_attn_Wkv, L0_attn_Wo, L0_attn_norm_w, L0_attn_norm_b, L0_attn_out_norm_w, L0_attn_out_norm_b)
    x = x + 0.5 * _L0_ffn_ref(_layernorm(x, axis=-1), L0_ffn_norm1_w, L0_ffn_norm2_w, L0_ffn_Wq, L0_ffn_Wdkv, L0_ffn_Wuk, L0_ffn_Wuv, L0_ffn_Wo, L0_ffn_ln_g, L0_ffn_ln_b, L0_ffn_gate_w, L0_ffn_gate_b, L0_ffn_W1, L0_ffn_b1, L0_ffn_W2, L0_ffn_b2)
    return x

_drawn_inputs = setup_inputs


def setup_inputs(seed=0):
    import zlib

    import numpy as np

    out = dict(_drawn_inputs(seed))
    spreads = {'L0_attn_norm_w': (1.0, 0.2),
     'L0_attn_norm_b': (0.0, 0.1),
     'L0_attn_out_norm_w': (1.0, 0.2),
     'L0_attn_out_norm_b': (0.0, 0.1),
     'L0_ffn_norm1_w': (1.0, 0.2),
     'L0_ffn_norm2_w': (1.0, 0.2),
     'L0_ffn_ln_g': (1.0, 0.2),
     'L0_ffn_ln_b': (0.0, 0.1),
     'L0_ffn_gate_b': (0.0, 0.1),
     'L0_ffn_b1': (0.0, 0.1),
     'L0_ffn_b2': (0.0, 0.1)}
    factors = {}
    for name, (base, spread) in spreads.items():
        noise = np.random.default_rng([zlib.crc32(name.encode()), seed]).standard_normal(out[name].shape)
        drawn = base * np.exp(spread * noise) if base else spread * noise
        out[name] = jnp.asarray(drawn.astype(out[name].dtype))
    for name, factor in factors.items():
        out[name] = (out[name] * factor).astype(out[name].dtype)
    return out
```

```python
from contextlib import ExitStack

import concourse.bass as bass
import numpy as np
from concourse import mybir

F32 = mybir.dt.float32
F32R = mybir.dt.float32r
BF16 = mybir.dt.bfloat16
ALU = mybir.AluOpType
ACT = mybir.ActivationFunctionType
AX = mybir.AxisListType

P = 128
NB, SEQ, D = 16, 256, 128
NT = NB * SEQ // P
KT = SEQ // P
MH, MD = 16, 8
MW = 32
LAT = 64
NE, HID = 4, 512
HC = HID // P
AH, AD = 8, 64
EPS5, EPS6 = 1e-5, 1e-6
BIG = 1e30
GRP = 4
MSCALE = float(MD) ** -0.5
ASCALE = float(AD) ** -0.5


def is_int(v):
    return isinstance(v, int)


def due(count):
    return max(count, 0) if is_int(count) else count


def value(eng, count):
    return due(count) if is_int(count) else eng.to_reg(count)


def cols(start, size):
    return slice(start, start + size) if is_int(start) else bass.ds(start, size)


def words(view):
    return view.bitcast(F32)


class Tiles:
    pass


def setup_phase(nc, T, A, sem):
    loaded = {name: sem(f"load_{name}") for name in ("x", "small", "w1", "w2")}
    step = sem("setup_step")
    zeroed = sem("setup_zeroed")
    tiles = ExitStack()

    def own(name, shape, dt=F32):
        return tiles.enter_context(nc.sbuf_tensor(f"setup_{name}", shape, dt))

    w1 = own("w1", [D, NQ * P])
    w2 = own("w2", [P, NQ * D])
    bias = own("bias", [GR, HID + D])
    rows = own("rows", [GR, 2 + 2 * NE])
    near = own("near", [GR, HID + D], BF16)
    rest = own("rest", [GR, HID + D])
    part = own("part", [GR, HID + D], BF16)
    small = [
        (T.norm1, A["norm1"]), (T.wdkv, A["wdkv"]), (T.wq, A["wq"]), (T.wq_swap, A["wq_swap"]),
        (T.ln_g, A["ln_g"]), (T.ln_b, A["ln_b"]), (T.wuk, A["wuk"]), (T.wuk_swap, A["wuk_swap"]),
        (T.wuv, A["wuv"]), (T.wo, A["wo"]), (T.cos, A["cos"]), (T.sin, A["sin"]),
        (T.norm2, A["norm2"]), (T.gate, A["gate"]), (T.gate_b, A["gate_b"].to_broadcast([P, NE])),
        (rows, A["gate_sel"]),
        (T.awq, A["awq"]), (T.awk, A["awk"]), (T.awv, A["awv"]), (T.awo, A["awo"]),
        (T.norm_w, A["norm_w"]), (T.norm_b, A["norm_b"]),
        (T.out_w, A["out_w"].to_broadcast([P, D])), (T.out_b, A["out_b"].to_broadcast([P, D])),
    ]
    small_count = 16 * (len(small) + 6)

    with tiles, nc.Block("setup") as block:
        @block.sync
        def _(sp):
            sp.dma_start(T.X[:, :].rearrange("p (t d) -> p t d", d=D),
                         A["x"].rearrange("b (k p) d -> p (b k) d", p=P)).then_inc(loaded["x"], 16)
            sp.dma_start(w1[:, :], A["w1"]).then_inc(loaded["w1"], 16)
            sp.dma_start(w2[:, :], A["w2"]).then_inc(loaded["w2"], 16)
            sp.wait_ge(loaded["x"], 16)

        @block.scalar
        def _(act):
            for tile, array in small:
                act.dma_start(tile[:, :], array).then_inc(loaded["small"], 16)
            for p in range(3):
                act.dma_start(bias[p * NE:(p + 1) * NE, 0:HID], A["b1"]).then_inc(loaded["small"], 16)
                act.dma_start(bias[p * NE:(p + 1) * NE, HID:HID + D], A["b2"]).then_inc(loaded["small"], 16)

        @block.gpsimd
        def _(pool):
            pool.memset(T.neghalf[:, :, :], -0.5)
            pool.memset(T.ident[:, :], 0.0)
            pool.memset(T.ident_bf[:, :], 0.0)
            pool.memset(T.neg[:, :, :], 0.0).then_inc(zeroed, 1)
            pool.wait_ge(zeroed, 1)
            for m in (T.ident, T.ident_bf):
                pool.affine_select(out=m[:, :], in_=m[:, :], compare_op=ALU.not_equal, fill=1.0, base=0,
                                   pattern=[[-1, P]], channel_multiplier=1)
            pool.affine_select(out=T.neg[:, :, :], in_=T.neg[:, :, :], compare_op=ALU.is_ge, fill=-BIG, base=0,
                               pattern=[[0, 4], [-1, P]], channel_multiplier=1).then_inc(T.made, 1)
            for buf in range(2):
                pool.memset(T.kstack[buf][:, :].bitcast(F32), 0.0).then_inc(zeroed, 1)
            pool.wait_ge(zeroed, 3)
            for buf in range(2):
                pool.memset(T.kstack[buf][4 * MD:4 * MD + 2, :].bitcast(F32), 1.0)

        @block.vector
        def _(dve):
            dve.memset(T.low_rows[0:AD, :], 0.0)
            dve.memset(T.low_rows[AD:P, :], -1.0)
            for buf in range(2):
                dve.memset(T.qstack[buf][:, :].bitcast(F32), 0.0)
                dve.memset(T.va[buf][:, :, :, :], 1.0)
            dve.wait_ge(loaded["small"], small_count)
            dve.tensor_copy(near[:, :], bias[:, :]).then_inc(step, 1)
            dve.wait_ge(step, 1)
            dve.scalar_tensor_tensor(rest[:, :], near[:, :], rows[:, 0:1], bias[:, :], op0=ALU.mult, op1=ALU.add)\
                .then_inc(step, 1)
            dve.wait_ge(step, 2)
            dve.tensor_copy(near[:, :], rest[:, :]).then_inc(step, 1)
            dve.wait_ge(step, 3)
            dve.scalar_tensor_tensor(part[:, :], near[:, :], rows[:, 1:2], rest[:, :], op0=ALU.mult, op1=ALU.add)\
                .then_inc(step, 1)
            dve.wait_ge(step, 4)
            for e in range(NE):
                dve.tensor_scalar(T.gate_rows[:, e * HID:(e + 1) * HID], part[:, 0:HID],
                                  rows[:, 2 + e:3 + e], rows[:, 2 + NE + e:3 + NE + e], ALU.mult, ALU.add)
            dve.tensor_copy(T.b2_rows[:, :], part[:, HID:HID + D])
            for k, (name, w, hi, lo) in enumerate((("w1", w1, T.w1_hi, T.w1_lo), ("w2", w2, T.w2_hi, T.w2_lo))):
                dve.wait_ge(loaded[name], 16)
                dve.tensor_copy(hi[:, :], w[:, :]).then_inc(step, 1)
                dve.wait_ge(step, 5 + k)
                dve.tensor_tensor(lo[:, :], w[:, :], hi[:, :].bitcast(F32), ALU.subtract)


MISC_TURNS = [("un_t", 2), ("latent", 2), ("q", 2), ("head_t0", -1), ("latent_t", 2), ("k", 2), ("v", 2),
              ("head_t1", -1), ("out_t", -1), ("wo", -1), ("max_t", 1)]
MAX_UNITS = {3: (0, 1), 4: (2, 3), 5: (4, 5), 6: (6, 7), 7: (8, 9), 8: (10, 11)}
VALUE_SLOTS = {1: (-1, 3), 4: (0, 0), 7: (0, 1), 10: (0, 2)}
SLOTS = 12
MX_BANKS, ST_BANKS = 2, 3
RING = 6
STACK_DMAS = 9 * 16
MAXROW_DMAS = 2 * 16


class MlaSems:

    def __init__(self, sem):
        self.bn = sem("mla_bn")
        self.stats = sem("mla_stats")
        self.veps = sem("mla_veps")
        self.rnorm = sem("mla_rnorm")
        self.u = sem("mla_u")
        self.turn = {k: sem(f"mla_{k}_ready") for k, _ in MISC_TURNS}
        self.taken = {k: sem(f"mla_{k}_taken") for k, _ in MISC_TURNS}
        self.lat_bn = sem("mla_lat_bn")
        self.lat_stats = sem("mla_lat_stats")
        self.lat_veps = sem("mla_lat_veps")
        self.lat_rnorm = sem("mla_lat_rnorm")
        self.latn = sem("mla_latn")
        self.rot = sem("mla_rot")
        self.hi = sem("mla_hi")
        self.lo = sem("mla_lo")
        self.va = sem("mla_va")
        self.stack = sem("mla_stack")
        self.maxrow = sem("mla_maxrow")
        self.mt_hi = sem("mla_mt_hi")
        self.mx_full = [sem(f"mla_mx_full{v}") for v in range(MX_BANKS)]
        self.mx_done = [sem(f"mla_mx_done{v}") for v in range(MX_BANKS)]
        self.st_full = [sem(f"mla_st_full{s}") for s in range(ST_BANKS)]
        self.exp = [sem(f"mla_exp{s}") for s in range(ST_BANKS)]
        self.masked = [sem(f"mla_masked{g}") for g in range(GRP)]
        self.ov_full = [sem(f"mla_ov_full{g}") for g in range(GRP)]
        self.ov_taken = [sem(f"mla_ov_taken{g}") for g in range(GRP)]
        self.recip = [sem(f"mla_recip{k}") for k in range(KT)]


def mla_phase(nc, T, S, base):
    tiles = ExitStack()
    with tiles:
        def sb(name, shape, dt=F32):
            return tiles.enter_context(nc.sbuf_tensor(f"mla{base}_{name}", shape, dt))

        def pb(name):
            return tiles.enter_context(nc.psum_tensor(f"mla{base}_{name}", [P, 512], F32))

        st6 = sb("st6", [P, KT, 6])
        mv = sb("mv", [P, KT, 2])
        veps = sb("veps", [P, 2, KT])
        rs = sb("rs", [P, 2, KT])
        un = sb("un", [P, KT, D])
        unT = sb("unT", [D, SEQ])
        lat = sb("lat", [P, KT, LAT])
        lst6 = sb("lst6", [P, KT, 6])
        lmv = sb("lmv", [P, KT, 2])
        lveps = sb("lveps", [P, KT])
        lrs = sb("lrs", [P, KT])
        latn = sb("latn", [P, KT, LAT])
        latT = sb("latT", [LAT, SEQ])
        t_cos = sb("t_cos", [P, 2, SEQ])
        t_sin = sb("t_sin", [P, 2, SEQ])
        rot = sb("rot", [P, 2, SEQ])
        hi = sb("hi", [P, 2, SEQ], F32R)
        lo = sb("lo", [P, 2, SEQ], F32R)
        vst = sb("vst", [P, KT, MH, MD])
        mx = sb("mx", [P, KT, MH])
        mt_hi = sb("mt_hi", [MH, SEQ], F32R)
        mt_lo = sb("mt_lo", [MH, SEQ], F32R)
        pr = sb("pr", [P, RING, 512])
        ot = sb("ot", [P, 2, GRP, SEQ])
        rec = sb("rec", [P, KT, MH])
        on = sb("on", [P, KT, MH, MD])
        onT = sb("onT", [D, SEQ])
        qs, ks, va = T.qstack, T.kstack, T.va

        st = [pb(f"st{n}") for n in range(3)]
        mxp = [pb(f"mxp{n}") for n in range(2)]
        ov = [pb(f"ov{n}") for n in range(2)]
        misc = pb("misc")
        block = tiles.enter_context(nc.Block(f"mla{base}"))
        X, U = T.X, T.U

        def ok(b):
            return not is_int(b) or 0 <= b < NB

        def n(b):
            return b + (base + 1)

        def nu(b, unit, banks):
            return (b + base) * (SLOTS // banks) + (unit // banks + 1)

        def before(i, kind):
            here = [(k, i + o) for k, o in MISC_TURNS if ok(i + o)]
            at = [k for k, _ in here].index(kind)
            if at:
                return here[at - 1]
            if is_int(i):
                old = [(k, i - 1 + o) for k, o in MISC_TURNS if ok(i - 1 + o)]
                return old[-1] if old else None
            return MISC_TURNS[-1][0], i + (MISC_TURNS[-1][1] - 1)

        first = 3 if base == 0 else 1

        def run(eng, iteration):
            for i in range(-3, first):
                iteration(i, i % 2)
            pairs = (NB - 3 - first) // 2
            with eng.Fori(0, pairs) as j:
                iteration(j * 2 + first, 1)
                iteration(j * 2 + (first + 1), 0)
            for i in range(2 * pairs + first, NB + 1):
                iteration(i, i % 2)

        @block.sync
        def _(sp):
            def iteration(i, par):
                if ok(i + 1):
                    b, buf = i + 1, 1 - par
                    sp.wait_ge(S.mt_hi, due(n(b)))
                    sp.wait_ge(S.taken["max_t"], due(n(b)))
                    sp.dma_start(words(qs[buf][4 * MD:4 * MD + 1, :]), words(mt_hi[:, :])).then_inc(S.maxrow, 16)
                    sp.dma_start(words(qs[buf][4 * MD + 1:4 * MD + 2, :]), words(mt_lo[:, :])).then_inc(S.maxrow, 16)
                if ok(i + 2):
                    b, buf = i + 2, par
                    sp.wait_ge(S.hi, due(n(b)))
                    sp.wait_ge(S.lo, due(n(b)))
                    sp.wait_ge(S.st_full[(SLOTS - 1) % ST_BANKS], due(nu(b - 2, SLOTS - 1, ST_BANKS)))
                    for r, (qp, kp) in enumerate(((hi, hi), (lo, hi), (hi, lo), (lo, lo))):
                        sp.dma_start(words(qs[buf][r * MD:(r + 1) * MD, :]), words(qp[:, 0, :])).then_inc(S.stack, 16)
                        sp.dma_start(words(ks[buf][r * MD:(r + 1) * MD, :]), words(kp[:, 1, :])).then_inc(S.stack, 16)
                    sp.dma_start(words(qs[buf][4 * MD:4 * MD + 2, :]), words(ks[buf][4 * MD + 2:4 * MD + 4, :]))\
                        .then_inc(S.stack, 16)

            run(sp, iteration)

        @block.gpsimd
        def _(pool):
            def scale_factors(b):
                count0 = value(pool, n(b))
                count1 = value(pool, n(b - 1))
                pool.wait_ge(T.made, 1)
                pool.wait_ge(S.stats, count0)
                pool.wait_ge(S.u, count1)
                pool.tensor_scalar(veps[:, 0, :], mv[:, :, 1], EPS5, None, ALU.add)
                pool.tensor_scalar(veps[:, 1, :], mv[:, :, 1], 1.0 + EPS6, EPS5 * EPS6,
                                   ALU.mult, ALU.add).then_inc(S.veps, 1)
                pool.wait_ge(S.veps, due(n(b)))
                pool.tensor_tensor(rs[:, :, :], veps[:, :, :], T.neghalf[:, :, 0:KT], ALU.pow).then_inc(S.rnorm, 1)

            def latent_factors(b):
                count0 = value(pool, n(b))
                count1 = value(pool, n(b - 1))
                pool.wait_ge(T.made, 1)
                pool.wait_ge(S.lat_stats, count0)
                pool.wait_ge(S.latn, count1)
                pool.tensor_scalar(lveps[:, :], lmv[:, :, 1], EPS5, None, ALU.add).then_inc(S.lat_veps, 1)
                pool.wait_ge(S.lat_veps, due(n(b)))
                pool.tensor_tensor(lrs[:, :], lveps[:, :], T.neghalf[:, 0, 0:KT], ALU.pow).then_inc(S.lat_rnorm, 1)

            def rotate(b):
                pool.wait_ge(S.taken["q"], due(n(b)))
                pool.wait_ge(S.taken["k"], due(n(b)))
                pool.wait_ge(S.hi, due(n(b - 1)))
                pool.wait_ge(S.lo, due(n(b - 1)))
                pool.tensor_tensor(rot[:, :, :], t_cos[:, :, :], t_sin[:, :, :], ALU.add).then_inc(S.rot, 1)

            def lower(b):
                pool.wait_ge(S.hi, due(n(b)))
                pool.wait_ge(S.stack, due(n(b - 1) * STACK_DMAS))
                pool.tensor_tensor(lo[:, :, :], rot[:, :, :], hi[:, :, :].bitcast(F32),
                                   ALU.subtract).then_inc(S.lo, 1)

            def causal(b, s):
                count0 = value(pool, nu(b, s, ST_BANKS))
                pool.wait_ge(T.made, 1)
                pool.wait_ge(S.exp[s % ST_BANKS], count0)
                if s % 3 == 2:
                    view = pr[:, s % RING, :].rearrange("p (h q) -> p h q", h=4)
                else:
                    view = pr[:, s % RING, :].rearrange("p (h q) -> p h q", h=2)[:, :, 0:P]
                ins = pool.affine_select(out=view, in_=view, compare_op=ALU.is_ge, fill=0.0, base=0,
                                         pattern=[[0, view.shape[1]], [1, P]], channel_multiplier=-1)
                if s % 3 == 2:
                    ins.then_inc(S.masked[s // 3], 1)

            def iteration(i, par):
                for s in range(SLOTS):
                    if ok(i):
                        causal(i, s)
                    if s == 2 and ok(i + 2):
                        latent_factors(i + 2)
                    if s == 6 and ok(i + 2):
                        rotate(i + 2)
                    if s == 8 and ok(i + 2):
                        lower(i + 2)
                    if s == 10 and ok(i + 3):
                        scale_factors(i + 3)

            run(pool, iteration)

        @block.scalar
        def _(act):
            def copy_out(kind, b, dst, src, func=ACT.Copy, **kw):
                act.wait_ge(S.turn[kind], due(n(b)))
                act.activation(dst, src, func, **kw).then_inc(S.taken[kind], 1)

            def exponentials(b, s):
                act.wait_ge(S.st_full[s % ST_BANKS], due(nu(b, s, ST_BANKS)))
                if s >= RING:
                    act.wait_ge(S.ov_full[(s - RING) // 3], due(n(b)))
                else:
                    act.wait_ge(S.ov_full[(s + SLOTS - RING) // 3], due(n(b - 1)))
                act.activation(pr[:, s % RING, :], st[s % 3][:, :], ACT.Exp, scale=MSCALE).then_inc(S.exp[s % ST_BANKS], 1)

            def take_products(b, g, par):
                act.wait_ge(S.ov_full[g], due(n(b)))
                act.wait_ge(S.turn["head_t1"], due(n(b - 1) if g == GRP - 1 else n(b - 2)))
                act.activation(ot[:, par, g, :], ov[g % 2][:, 0:SEQ], ACT.Copy).then_inc(S.ov_taken[g], 1)

            def iteration(i, par):
                for s in range(SLOTS):
                    if ok(i):
                        exponentials(i, s)
                    if s == 0 and ok(i + 2):
                        act.wait_ge(S.turn["q"], due(n(i + 1)))
                        copy_out("un_t", i + 2, unT[:, :], misc[:, 0:SEQ], scale=T.norm1[:, 0:1])
                    if s == 2 and ok(i - 1):
                        take_products(i - 1, 3, 1 - par)
                    if s == 4 and ok(i + 2):
                        act.wait_ge(S.turn["v"], due(n(i + 1)))
                        copy_out("latent_t", i + 2, latT[:, :], misc[0:LAT, 0:SEQ], ACT.Identity,
                                 scale=T.ln_g[:, 0:1], bias=T.ln_b[:, 0:1])
                    if s == 5 and ok(i):
                        take_products(i, 0, par)
                    if s == 6 and ok(i + 2):
                        act.wait_ge(S.va, due(n(i + 1)))
                        copy_out("v", i + 2, vst[:, :, :, :].rearrange("p k h d -> p (k h d)"), misc[:, 0:SEQ])
                    if s == 7 and ok(i + 2):
                        act.wait_ge(S.rot, due(n(i + 2)))
                        act.wait_ge(S.stack, due(n(i + 1) * STACK_DMAS))
                        act.activation(hi[:, :, :], rot[:, :, :], ACT.Copy).then_inc(S.hi, 1)
                    if s == 8 and ok(i):
                        take_products(i, 1, par)
                    if s == 8 and ok(i - 1):
                        act.wait_ge(S.turn["wo"], due(n(i - 2)))
                        copy_out("out_t", i - 1, onT[:, :], misc[:, 0:SEQ])
                    if s == 10 and ok(i + 1):
                        act.wait_ge(S.turn["max_t"], due(n(i + 1)))
                        act.wait_ge(S.maxrow, due(n(i) * MAXROW_DMAS))
                        act.activation(mt_hi[:, :], misc[0:MH, 0:SEQ], ACT.Copy).then_inc(S.mt_hi, 1)
                    if s == 11 and ok(i):
                        take_products(i, 2, par)

            run(act, iteration)

        @block.vector
        def _(dve):
            def row_stats(b):
                for k in range(KT):
                    ins = dve.bn_stats(st6[:, k, :], X[:, cols(b * SEQ + k * D, D)])
                ins.then_inc(S.bn, 1)
                count0 = value(dve, n(b))
                dve.wait_ge(T.made, 1)
                dve.wait_ge(S.bn, count0)
                for k in range(KT):
                    ins = dve.bn_aggr(mv[:, k, :], st6[:, k, :])
                ins.then_inc(S.stats, 1)

            def norm_rows(b):
                dve.wait_ge(S.rnorm, due(n(b)))
                dve.wait_ge(S.turn["un_t"], due(n(b - 1)))
                for k in range(KT):
                    at = cols(b * SEQ + k * D, D)
                    dve.tensor_scalar(U[:, at], X[:, at], mv[:, k, 0:1], rs[:, 0, k:k + 1],
                                      ALU.subtract, ALU.mult)
                    ins = dve.tensor_scalar(un[:, k, :], X[:, at], mv[:, k, 0:1], rs[:, 1, k:k + 1],
                                            ALU.subtract, ALU.mult)
                ins.then_inc(S.u, 1)

            def latent_stats(b):
                dve.wait_ge(S.turn["latent"], due(n(b)))
                dve.tensor_copy(lat[:, :, :], misc[:, 0:KT * LAT].rearrange("p (k c) -> p k c", k=KT))\
                    .then_inc(S.taken["latent"], 1)
                dve.wait_ge(S.taken["latent"], due(n(b)))
                for k in range(KT):
                    ins = dve.bn_stats(lst6[:, k, :], lat[:, k, :])
                ins.then_inc(S.lat_bn, 1)
                count0 = value(dve, n(b))
                dve.wait_ge(T.made, 1)
                dve.wait_ge(S.lat_bn, count0)
                for k in range(KT):
                    ins = dve.bn_aggr(lmv[:, k, :], lst6[:, k, :])
                ins.then_inc(S.lat_stats, 1)

            def norm_latents(b):
                dve.wait_ge(S.lat_rnorm, due(n(b)))
                dve.wait_ge(S.turn["latent_t"], due(n(b - 1)))
                for k in range(KT):
                    ins = dve.tensor_scalar(latn[:, k, :], lat[:, k, :], lmv[:, k, 0:1], lrs[:, k:k + 1],
                                            ALU.subtract, ALU.mult)
                ins.then_inc(S.latn, 1)

            def rotary_products(kind, which, b):
                dve.wait_ge(S.turn[kind], due(n(b)))
                dve.wait_ge(S.rot, due(n(b - 1)))
                dve.tensor_tensor(t_cos[:, which, :], misc[:, 0:SEQ], T.cos[:, :], ALU.mult)
                dve.tensor_tensor(t_sin[:, which, :], misc[:, SEQ:2 * SEQ], T.sin[:, :], ALU.mult)\
                    .then_inc(S.taken[kind], 1)

            def place_values(b, buf):
                dve.wait_ge(S.taken["v"], due(n(b)))
                dve.wait_ge(S.ov_full[GRP - 1], due(n(b - 2)))
                dve.tensor_copy(va[buf][:, :, :, 0:MD], vst[:, :, :, :]).then_inc(S.va, 1)

            def norm_heads(b, k):
                kind = f"head_t{k}"
                heads = misc[:, :].rearrange("p (h c) -> p h c", c=MW)
                dve.wait_ge(S.turn[kind], due(n(b)))
                dve.reciprocal(rec[:, k, :], heads[:, :, MD]).then_inc(S.recip[k], 1)
                dve.wait_ge(S.recip[k], due(n(b)))
                dve.wait_ge(S.turn["out_t"], due(n(b - 1)))
                dve.tensor_tensor(on[:, k, :, :], heads[:, :, 0:MD],
                                  rec[:, k, :].unsqueeze(2).to_broadcast([P, MH, MD]), ALU.mult)\
                    .then_inc(S.taken[kind], 1)

            def maxima(b, v):
                dve.wait_ge(S.mx_full[v % MX_BANKS], due(nu(b, v, MX_BANKS)))
                if v == 0:
                    dve.wait_ge(S.turn["max_t"], due(n(b - 1)))
                nh = 4 if v < 4 else 2
                out = mx[:, 0, 4 * v:4 * v + 4] if v < 4 else mx[:, 1, 2 * (v - 4):2 * (v - 4) + 2]
                dve.tensor_reduce(out, mxp[v % 2][:, :].rearrange("p (h k) -> p h k", h=nh), AX.X, ALU.max,
                                  negate=True).then_inc(S.mx_done[v % MX_BANKS], 1)

            def iteration(i, par):
                for s in range(SLOTS):
                    if s == 1 and ok(i + 2):
                        latent_stats(i + 2)
                    if s == 2 and ok(i + 2):
                        rotary_products("q", 0, i + 2)
                        norm_latents(i + 2)
                    if s == 2 and ok(i + 1):
                        place_values(i + 1, 1 - par)
                    if s == 3 and ok(i - 1):
                        norm_heads(i - 1, 0)
                    if s == 5 and ok(i + 2):
                        rotary_products("k", 1, i + 2)
                    if s == 7 and ok(i - 1):
                        norm_heads(i - 1, 1)
                    if s == 9 and ok(i - 1):
                        b = i - 1
                        dve.wait_ge(S.turn["wo"], due(n(b)))
                        at = cols(b * SEQ, SEQ)
                        dve.tensor_tensor(U[:, at], misc[:, 0:SEQ], U[:, at], ALU.add).then_inc(S.taken["wo"], 1)
                    if s == 10 and ok(i + 1):
                        b = i + 1
                        dve.wait_ge(S.mt_hi, due(n(b)))
                        dve.wait_ge(S.maxrow, due(n(b - 1) * MAXROW_DMAS))
                        dve.tensor_tensor(mt_lo[:, :], misc[0:MH, 0:SEQ], mt_hi[:, :].bitcast(F32),
                                          ALU.subtract).then_inc(S.taken["max_t"], 1)
                    if ok(i + 1):
                        for v in MAX_UNITS.get(s, ()):
                            maxima(i + 1, v)
                    if s == 9 and ok(i + 3):
                        row_stats(i + 3)
                    if s == 11 and ok(i + 3):
                        norm_rows(i + 3)

            run(dve, iteration)

        @block.tensor
        def _(pe):
            def turn(kind, b, buf):
                if kind == "un_t":
                    pe.wait_ge(S.u, due(n(b)))
                    for k in range(KT):
                        ins = pe.transpose(misc[:, k * P:(k + 1) * P], un[:, k, :], T.ident[:, :])
                elif kind == "latent":
                    pe.wait_ge(S.taken["un_t"], due(n(b)))
                    for k in range(KT):
                        ins = pe.matmul(misc[:, k * LAT:(k + 1) * LAT], unT[:, k * P:(k + 1) * P], T.wdkv[:, :],
                                        start=True, stop=True)
                elif kind == "q":
                    for half, w in enumerate((T.wq, T.wq_swap)):
                        ins = pe.matmul(misc[:, half * SEQ:(half + 1) * SEQ], w[:, :], unT[:, :],
                                        start=True, stop=True)
                elif kind == "latent_t":
                    for k in range(KT):
                        ins = pe.transpose(misc[0:LAT, k * P:(k + 1) * P], latn[:, k, :], T.ident[:, :])
                elif kind == "k":
                    pe.wait_ge(S.taken["latent_t"], due(n(b)))
                    for half, w in enumerate((T.wuk, T.wuk_swap)):
                        ins = pe.matmul(misc[:, half * SEQ:(half + 1) * SEQ], w[:, :], latT[:, :],
                                        start=True, stop=True)
                elif kind == "v":
                    for k in range(KT):
                        ins = pe.matmul(misc[:, k * D:(k + 1) * D], latT[:, k * P:(k + 1) * P], T.wuv[:, :],
                                        start=True, stop=True)
                elif kind in ("head_t0", "head_t1"):
                    k = int(kind[-1])
                    if k == 0:
                        for g in range(GRP):
                            pe.wait_ge(S.ov_taken[g], due(n(b)))
                    for g in range(GRP):
                        ins = pe.transpose(misc[:, g * P:(g + 1) * P], ot[:, buf, g, k * P:(k + 1) * P], T.ident[:, :])
                elif kind == "out_t":
                    pe.wait_ge(S.taken["head_t0"], due(n(b)))
                    pe.wait_ge(S.taken["head_t1"], due(n(b)))
                    for k in range(KT):
                        ins = pe.transpose(misc[:, k * P:(k + 1) * P],
                                           on[:, k, :, :].rearrange("p h d -> p (h d)"), T.ident[:, :])
                elif kind == "wo":
                    pe.wait_ge(S.taken["out_t"], due(n(b)))
                    for k in range(KT):
                        ins = pe.matmul(misc[:, k * D:(k + 1) * D], onT[:, k * P:(k + 1) * P], T.wo[:, :],
                                        start=True, stop=True)
                else:
                    pe.wait_ge(S.mx_done[(SLOTS - 1) % MX_BANKS], due(nu(b, SLOTS - 1, MX_BANKS)))
                    for k in range(KT):
                        ins = pe.transpose(misc[0:MH, k * P:(k + 1) * P], mx[:, k, :], T.ident[:, :])
                return ins

            def transposed_scores(b, s, buf):
                if s == 0:
                    pe.wait_ge(S.stack, due(n(b) * STACK_DMAS))
                    pe.wait_ge(S.maxrow, due(n(b) * MAXROW_DMAS))
                pe.wait_ge(S.exp[s % ST_BANKS], due(nu(b, s, ST_BANKS) - 1))
                g, part = divmod(s, 3)
                heads = [4 * g + 2 * part, 4 * g + 2 * part + 1] if part < 2 else [4 * g + m for m in range(4)]
                t0 = 0 if part < 2 else P
                size = SEQ - t0
                for m, h in enumerate(heads):
                    ins = pe.matmul(st[s % 3][:, m * size:(m + 1) * size],
                                    ks[buf][:, h * SEQ + t0:h * SEQ + t0 + P],
                                    qs[buf][:, h * SEQ + t0:(h + 1) * SEQ],
                                    start=(m == 0), stop=(m == len(heads) - 1), skip_group_check=True)
                ins.then_inc(S.st_full[s % ST_BANKS], 1)

            def plain_scores(b, v, buf):
                if v == 0:
                    pe.wait_ge(S.stack, due(n(b) * STACK_DMAS))
                pe.wait_ge(S.mx_done[v % MX_BANKS], due(nu(b, v, MX_BANKS) - 1))
                bank = mxp[v % 2]
                t, heads = (0, range(4 * v, 4 * v + 4)) if v < 4 else (1, range(2 * v - 8, 2 * v - 6))
                size = (t + 1) * P
                for m, h in enumerate(heads):
                    pe.matmul(bank[:, m * size:(m + 1) * size], qs[buf][:, h * SEQ + t * P:h * SEQ + (t + 1) * P],
                              ks[buf][:, h * SEQ:h * SEQ + size], start=(m == 0), stop=False,
                              skip_group_check=True)
                nh = len(heads)
                pe.matmul(bank[:, :].rearrange("p (h k) -> p h k", h=nh)[:, :, size - P:size], T.ident_bf[:, :],
                          T.neg[:, 0:nh, :], start=False, stop=True, skip_group_check=True)\
                    .then_inc(S.mx_full[v % MX_BANKS], 1)

            def value_products(b, g, buf):
                if g == 0:
                    pe.wait_ge(S.va, due(n(b)))
                if g >= 2:
                    pe.wait_ge(S.ov_taken[g - 2], due(n(b)))
                else:
                    pe.wait_ge(S.ov_taken[g + 2], due(n(b - 1)))
                pe.wait_ge(S.masked[g], due(n(b)))
                for kt in range(KT):
                    for m in range(GRP):
                        h = 4 * g + m
                        s = 3 * g + (m // 2 if kt == 0 else 2)
                        size = SEQ - kt * P
                        at = (m % 2 if kt == 0 else m) * size
                        ins = pe.matmul(ov[g % 2][MW * m:MW * (m + 1), kt * P:SEQ], va[buf][:, kt, h, :],
                                        pr[:, s % RING, at:at + size], start=(kt == 0), stop=(kt == KT - 1),
                                        skip_group_check=True)
                ins.then_inc(S.ov_full[g], 1)

            def iteration(i, par):
                for s in range(SLOTS):
                    if s < len(MISC_TURNS):
                        kind, off = MISC_TURNS[s]
                        if ok(i + off):
                            prev = before(i, kind)
                            turned = value(pe, n(i + off))
                            free = value(pe, n(prev[1])) if prev else None
                            if kind == "latent_t":
                                pe.wait_ge(T.made, 1)
                            if prev:
                                pe.wait_ge(S.taken[prev[0]], free)
                            if kind == "latent_t":
                                pe.wait_ge(S.latn, turned)
                            turn(kind, i + off, (par + off) % 2).then_inc(S.turn[kind], 1)
                    if ok(i):
                        transposed_scores(i, s, par)
                    if ok(i + 1):
                        for v in MAX_UNITS.get(s, ()):
                            plain_scores(i + 1, v, 1 - par)
                    if s in VALUE_SLOTS:
                        off, g = VALUE_SLOTS[s]
                        if ok(i + off):
                            value_products(i + off, g, (par + off) % 2)

            run(pe, iteration)


CT = 4
CN = CT * P
NC = NT // CT
NQ = NE * HC
HR = 4
LAGQ = 2
GR = 3 * NE


class MoeSems:

    def __init__(self, sem):
        self.bn = sem("moe_bn")
        self.stats = sem("moe_stats")
        self.sq = sem("moe_sq")
        self.ms = sem("moe_ms")
        self.veps = sem("moe_veps")
        self.rnorm = sem("moe_rnorm")
        self.xn = sem("moe_xn")
        self.xt_ready = sem("moe_xt_ready")
        self.xt = sem("moe_xt")
        self.x_hi = sem("moe_x_hi")
        self.x_lo = sem("moe_x_lo")
        self.lg_ready = sem("moe_lg_ready")
        self.lg = sem("moe_lg")
        self.top = sem("moe_top")
        self.eq = sem("moe_eq")
        self.seen = [sem(f"moe_seen{n}") for n in range(3)]
        self.onehot = sem("moe_onehot")
        self.oht_ready = sem("moe_oht_ready")
        self.oht = sem("moe_oht")
        self.h_full = [sem(f"moe_h_full{n}") for n in range(HR)]
        self.h_hi = [sem(f"moe_h_hi{n}") for n in range(HR)]
        self.h_lo = [sem(f"moe_h_lo{n}") for n in range(HR)]
        self.h_used = [sem(f"moe_h_used{n}") for n in range(HR)]
        self.y_sb = sem("moe_y_sb")
        self.yt_ready = sem("moe_yt_ready")
        self.sum = sem("moe_sum")
        self.x = sem("moe_x")
        self.stored = sem("moe_stored")


def moe_phase(nc, T, S, base, out=None):
    tiles = ExitStack()
    with tiles:
        def sb(name, shape, dt=F32):
            return tiles.enter_context(nc.sbuf_tensor(f"moe{base}_{name}", shape, dt))

        def pb(name):
            return tiles.enter_context(nc.psum_tensor(f"moe{base}_{name}", [P, 512], F32))

        st6 = sb("st6", [P, CT, 6])
        mv = sb("mv", [P, CT, 2])
        msq = sb("msq", [P, 3, CT])
        rs = sb("rs", [P, CT])
        xn = sb("xn", [P, CT, D])
        xT = sb("xT", [D, CN])
        x_hi = [sb(f"x_hi{n}", [D, CN], F32R) for n in range(2)]
        x_lo = [sb(f"x_lo{n}", [D, CN], F32R) for n in range(2)]
        lg = sb("lg", [P, CT, NE])
        top = sb("top", [P, CT])
        eq = sb("eq", [P, CT, NE])
        seen = sb("seen", [P, CT, NE])
        onehot = sb("onehot", [P, CT, 3, NE])
        oht = [sb(f"oht{n}", [GR, CN], BF16) for n in range(2)]
        h_hi = [sb(f"h_hi{n}", [P, CN], F32R) for n in range(HR)]
        h_lo = [sb(f"h_lo{n}", [P, CN], F32R) for n in range(HR)]
        y_sb = sb("y_sb", [D, CN])
        total = sb("total", [P, CN])

        hp = [pb(f"hp{n}") for n in range(HR)]
        yp = [pb(f"yp{n}") for n in range(2)]
        amid = pb("amid")
        yt = pb("yt")
        block = tiles.enter_context(nc.Block(f"moe{base}"))
        X, U = T.X, T.U

        def ok(c):
            return not is_int(c) or 0 <= c < NC

        def n(c):
            return c + (base + 1)

        def m(c, q):
            return (c + base) * (NQ // HR) + (q // HR + 1)

        def run(eng, iteration):
            first = 3 if base == 0 else 1
            for i in range(-1, first):
                iteration(i, i % 2)
            pairs = (NC - 1 - first + 1) // 2
            with eng.Fori(0, pairs) as j:
                iteration(j * 2 + first, 1)
                iteration(j * 2 + (first + 1), 0)
            for i in range(2 * pairs + first, NC + 1):
                iteration(i, i % 2)

        @block.sync
        def _(sp):
            if out is None:
                return
            rows = out.rearrange("(c b) (k p) d -> c p (b k) d", p=P, b=NB // NC)
            for c in range(NC):
                sp.wait_ge(S.x, n(c))
                sp.dma_start(rows[c], X[:, c * CN:(c + 1) * CN].rearrange("p (t d) -> p t d", d=D))\
                    .then_inc(S.stored, 16)
            sp.wait_ge(S.stored, 16 * NC)

        @block.gpsimd
        def _(pool):
            def iteration(i, par):
                if ok(i + 1):
                    c = i + 1
                    pool.wait_ge(S.stats, due(n(c)))
                    pool.wait_ge(S.xn, due(n(c - 1)))
                    pool.tensor_tensor(msq[:, 0, :], mv[:, :, 0], mv[:, :, 0], ALU.mult).then_inc(S.sq, 1)
                    pool.wait_ge(S.sq, due(n(c)))
                    pool.tensor_tensor(msq[:, 1, :], msq[:, 0, :], mv[:, :, 1], ALU.add).then_inc(S.ms, 1)
                    count0 = value(pool, n(c))
                    pool.wait_ge(T.made, 1)
                    pool.wait_ge(S.ms, count0)
                    pool.tensor_scalar(msq[:, 2, :], msq[:, 1, :], EPS6, None, ALU.add).then_inc(S.veps, 1)
                    pool.wait_ge(S.veps, due(n(c)))
                    pool.tensor_tensor(rs[:, :], msq[:, 2, :], T.neghalf[:, :, :].rearrange("p a b -> p (a b)"),
                                       ALU.pow).then_inc(S.rnorm, 1)
                    pool.wait_ge(S.x_hi, due(n(c)))
                    pool.tensor_tensor(x_lo[1 - par][:, :], xT[:, :], x_hi[1 - par][:, :].bitcast(F32),
                                       ALU.subtract).then_inc(S.x_lo, 1)

            run(pool, iteration)

        @block.scalar
        def _(act):
            def iteration(i, par):
                for q in range(NQ):
                    if ok(i):
                        r = q % HR
                        act.wait_ge(S.h_full[r], due(m(i, q)))
                        act.wait_ge(S.h_used[r], due(m(i, q) - 1))
                        act.activation(h_hi[r][:, :], hp[r][:, :], ACT.Relu).then_inc(S.h_hi[r], 1)
                    if q == 2 and ok(i - 1):
                        c = i - 1
                        act.wait_ge(S.h_used[(NQ - 1) % HR], due(m(c, NQ - 1)))
                        act.wait_ge(S.yt_ready, due(n(c - 1)))
                        act.activation(y_sb[:, :], yp[1 - par][:, :], ACT.Copy).then_inc(S.y_sb, 1)
                    if q == 7 and ok(i + 1):
                        c = i + 1
                        act.wait_ge(S.xt, due(n(c)))
                        act.wait_ge(S.h_used[(NQ - 1) % HR], due(m(c - 2, NQ - 1)))
                        act.activation(x_hi[1 - par][:, :], xT[:, :], ACT.Copy).then_inc(S.x_hi, 1)
                    if q == 13 and ok(i + 1):
                        act.wait_ge(S.oht_ready, due(n(i + 1)))
                        act.activation(oht[1 - par][:, :], amid[0:GR, :], ACT.Copy).then_inc(S.oht, 1)

            run(act, iteration)

        @block.vector
        def _(dve):
            def norm_stats(c):
                for k in range(CT):
                    ins = dve.bn_stats(st6[:, k, :], U[:, cols(c * CN + k * D, D)])
                ins.then_inc(S.bn, 1)
                count0 = value(dve, n(c))
                dve.wait_ge(T.made, 1)
                dve.wait_ge(S.bn, count0)
                for k in range(CT):
                    ins = dve.bn_aggr(mv[:, k, :], st6[:, k, :])
                ins.then_inc(S.stats, 1)

            def norm(c):
                dve.wait_ge(S.rnorm, due(n(c)))
                dve.wait_ge(S.xt_ready, due(n(c - 1)))
                for k in range(CT):
                    ins = dve.tensor_scalar(xn[:, k, :], U[:, cols(c * CN + k * D, D)], rs[:, k:k + 1], None,
                                            ALU.mult)
                ins.then_inc(S.xn, 1)

            def weigh(c):
                dve.wait_ge(S.xt_ready, due(n(c)))
                dve.wait_ge(S.lg_ready, due(n(c - 1)))
                dve.wait_ge(S.x_lo, due(n(c - 1)))
                dve.tensor_scalar(xT[:, :], amid[:, :], T.norm2[:, 0:1], None, ALU.mult).then_inc(S.xt, 1)

            def choose(c):
                dve.wait_ge(S.lg_ready, due(n(c)))
                dve.tensor_tensor(lg[:, :, :], amid[:, 0:CT * NE].rearrange("p (k e) -> p k e", e=NE),
                                  T.gate_b[:, :].unsqueeze(1).to_broadcast([P, CT, NE]), ALU.add)\
                    .then_inc(S.lg, 1)
                dve.wait_ge(S.lg, due(n(c)))
                dve.tensor_reduce(top[:, :], lg[:, :, :], AX.X, ALU.max).then_inc(S.top, 1)
                dve.wait_ge(S.top, due(n(c)))
                dve.tensor_tensor(eq[:, :, :], lg[:, :, :], top[:, :].unsqueeze(2).to_broadcast([P, CT, NE]),
                                  ALU.is_equal).then_inc(S.eq, 1)
                dve.wait_ge(S.eq, due(n(c)))
                dve.tensor_copy(seen[:, :, 1], eq[:, :, 0]).then_inc(S.seen[0], 1)
                for e in (1, 2):
                    dve.wait_ge(S.seen[e - 1], due(n(c)))
                    dve.tensor_tensor(seen[:, :, e + 1], seen[:, :, e], eq[:, :, e], ALU.max)\
                        .then_inc(S.seen[e], 1)
                dve.wait_ge(S.seen[2], due(n(c)))
                dve.wait_ge(S.oht_ready, due(n(c - 1)))
                for part in range(3):
                    ins = dve.tensor_tensor(onehot[:, :, part, :], eq[:, :, :], seen[:, :, :], ALU.is_gt)
                ins.then_inc(S.onehot, 1)

            def finish(c):
                dve.wait_ge(S.yt_ready, due(n(c)))
                at = cols(c * CN, CN)
                dve.tensor_tensor(total[:, :], yt[:, :], U[:, at], ALU.add).then_inc(S.sum, 1)
                dve.wait_ge(S.sum, due(n(c)))
                dve.scalar_tensor_tensor(X[:, at], total[:, :], 0.5, X[:, at], op0=ALU.mult, op1=ALU.add)\
                    .then_inc(S.x, 1)

            def iteration(i, par):
                if is_int(i) and i == -1:
                    dve.memset(seen[:, :, 0], 0.0)
                for q in range(NQ):
                    if ok(i):
                        r = q % HR
                        dve.wait_ge(S.h_hi[r], due(m(i, q)))
                        dve.scalar_tensor_tensor(h_lo[r][:, :], hp[r][:, :], 0.0, h_hi[r][:, :].bitcast(F32),
                                                 op0=ALU.max, op1=ALU.subtract).then_inc(S.h_lo[r], 1)
                    if q == 0 and ok(i + 1):
                        norm_stats(i + 1)
                    if q == 3 and ok(i + 1):
                        norm(i + 1)
                    if q == 4 and ok(i - 1):
                        finish(i - 1)
                    if q == 6 and ok(i + 1):
                        weigh(i + 1)
                    if q == 9 and ok(i + 1):
                        choose(i + 1)

            run(dve, iteration)

        @block.tensor
        def _(pe):
            def block_in(c, q, buf):
                r = q % HR
                if q == 0:
                    pe.wait_ge(S.x_hi, due(n(c)))
                    pe.wait_ge(S.x_lo, due(n(c)))
                    pe.wait_ge(S.oht, due(n(c)))
                pe.wait_ge(S.h_lo[r], due(m(c, q) - 1))
                w = slice(q * P, (q + 1) * P)
                pe.matmul(hp[r][:, :], T.gate_rows[:, w], oht[buf][:, :], start=True, stop=False)
                pe.matmul(hp[r][:, :], T.w1_lo[:, w], x_hi[buf][:, :], start=False, stop=False)
                pe.matmul(hp[r][:, :], T.w1_hi[:, w], x_lo[buf][:, :], start=False, stop=False)
                pe.matmul(hp[r][:, :], T.w1_hi[:, w], x_hi[buf][:, :], start=False, stop=True)\
                    .then_inc(S.h_full[r], 1)

            def block_out(c, q, buf):
                r = q % HR
                if q == 0:
                    pe.wait_ge(S.y_sb, due(n(c - 2)))
                    pe.matmul(yp[buf][:, :], T.b2_rows[:, :], oht[buf][:, :], start=True, stop=False)
                pe.wait_ge(S.h_lo[r], due(m(c, q)))
                w = slice(q * P, (q + 1) * P)
                pe.matmul(yp[buf][:, :], T.w2_lo[:, w], h_hi[r][:, :], start=False, stop=False)
                pe.matmul(yp[buf][:, :], T.w2_hi[:, w], h_lo[r][:, :], start=False, stop=False)
                pe.matmul(yp[buf][:, :], T.w2_hi[:, w], h_hi[r][:, :], start=False, stop=(q == NQ - 1))\
                    .then_inc(S.h_used[r], 1)

            def iteration(i, par):
                for q in range(NQ):
                    if ok(i):
                        block_in(i, q, par)
                    if q >= LAGQ and ok(i):
                        block_out(i, q - LAGQ, par)
                    if q < LAGQ and ok(i - 1):
                        block_out(i - 1, q + NQ - LAGQ, 1 - par)
                    if q == 3 and ok(i - 1):
                        c = i - 1
                        pe.wait_ge(S.y_sb, due(n(c)))
                        pe.wait_ge(S.sum, due(n(c - 1)))
                        for k in range(CT):
                            ins = pe.transpose(yt[:, k * P:(k + 1) * P], y_sb[:, k * P:(k + 1) * P], T.ident[:, :])
                        ins.then_inc(S.yt_ready, 1)
                    if q == 5 and ok(i + 1):
                        c = i + 1
                        pe.wait_ge(S.xn, due(n(c)))
                        pe.wait_ge(S.oht, due(n(c - 1)))
                        for k in range(CT):
                            ins = pe.transpose(amid[:, k * P:(k + 1) * P], xn[:, k, :], T.ident[:, :])
                        ins.then_inc(S.xt_ready, 1)
                    if q == 8 and ok(i + 1):
                        c = i + 1
                        pe.wait_ge(S.xt, due(n(c)))
                        for k in range(CT):
                            ins = pe.matmul(amid[:, k * NE:(k + 1) * NE], xT[:, k * P:(k + 1) * P], T.gate[:, :],
                                            start=True, stop=True)
                        ins.then_inc(S.lg_ready, 1)
                    if q == 12 and ok(i + 1):
                        c = i + 1
                        pe.wait_ge(S.onehot, due(n(c)))
                        for k in range(CT):
                            ins = pe.transpose(amid[0:GR, k * P:(k + 1) * P],
                                               onehot[:, k, :, :].rearrange("p a e -> p (a e)"), T.ident[:, :])
                        ins.then_inc(S.oht_ready, 1)

            run(pe, iteration)


PR4 = 4
PAIRS = AH // 2
PT_LAG = 2
Q_SLOTS = {2: 0, 3: 1, 4: 2, 5: 3}
PAIR_SLOTS = {4: (0, 0), 6: (0, 1), 0: (-1, 2), 2: (-1, 3)}


class MqaSems:

    def __init__(self, sem):
        self.bn = sem("mqa_bn")
        self.stats = sem("mqa_stats")
        self.sum_eps = sem("mqa_sum_eps")
        self.veps = sem("mqa_veps")
        self.rnorm = sem("mqa_rnorm")
        self.xn = sem("mqa_xn")
        self.xt_ready = sem("mqa_xt_ready")
        self.xt = sem("mqa_xt")
        self.kv_ready = sem("mqa_kv_ready")
        self.k_hi = sem("mqa_k_hi")
        self.k_lo = sem("mqa_k_lo")
        self.q_ready = sem("mqa_q_ready")
        self.q_hi = sem("mqa_q_hi")
        self.q = sem("mqa_q")
        self.s_full = [sem(f"mqa_s_full{n}") for n in range(2)]
        self.mx = [sem(f"mqa_mx{n}") for n in range(2)]
        self.exp = [sem(f"mqa_exp{n}") for n in range(2)]
        self.rec = [sem(f"mqa_rec{n}") for n in range(2)]
        self.pn = [sem(f"mqa_pn{n}") for n in range(2)]
        self.pt_full = [sem(f"mqa_pt_full{n}") for n in range(2)]
        self.pt_sb = [sem(f"mqa_pt_sb{n}") for n in range(2)]
        self.ov_full = [sem(f"mqa_ov_full{n}") for n in range(2)]
        self.ov_sb = [sem(f"mqa_ov_sb{n}") for n in range(2)]
        self.wo_ready = sem("mqa_wo_ready")
        self.wo = sem("mqa_wo")
        self.o_bn = sem("mqa_o_bn")
        self.o_stats = sem("mqa_o_stats")
        self.o_veps = sem("mqa_o_veps")
        self.o_rnorm = sem("mqa_o_rnorm")
        self.o_norm = sem("mqa_o_norm")
        self.o_w = sem("mqa_o_w")
        self.o_b = sem("mqa_o_b")
        self.x = sem("mqa_x")


def mqa_phase(nc, T, S):
    tiles = ExitStack()
    with tiles:
        def sb(name, shape, dt=F32):
            return tiles.enter_context(nc.sbuf_tensor(f"mqa_{name}", shape, dt))

        def pb(name):
            return tiles.enter_context(nc.psum_tensor(f"mqa_{name}", [P, 512], F32))

        st6 = sb("st6", [P, KT, 6])
        mv = sb("mv", [P, KT, 2])
        veps = sb("veps", [P, 2, KT])
        rs = sb("rs", [P, KT])
        xn = sb("xn", [P, KT, D])
        xT = sb("xT", [D, SEQ])
        k_hi = [sb(f"k_hi{n}", [P, SEQ], F32R) for n in range(2)]
        k_lo = [sb(f"k_lo{n}", [P, SEQ], F32R) for n in range(2)]
        vals = [sb(f"vals{n}", [P, KT, AD]) for n in range(2)]
        q_hi = sb("q_hi", [P, 2 * SEQ], F32R)
        qst = [sb(f"qst{n}", [P, AH * SEQ], F32R) for n in range(2)]
        nmax = sb("nmax", [P, AH, KT])
        sums = sb("sums", [P, AH, KT])
        recs = sb("recs", [P, AH, KT])
        pr = sb("pr", [P, PR4, KT, SEQ])
        pt = sb("pt", [P, PR4, KT, SEQ])
        oT = sb("oT", [P, PAIRS, SEQ])
        o_sb = sb("o_sb", [P, KT, D])
        ost6 = sb("ost6", [P, KT, 6])
        omv = sb("omv", [P, KT, 2])
        oveps = sb("oveps", [P, KT])
        ors = sb("ors", [P, KT])
        o_n = sb("o_n", [P, KT, D])
        o_w = sb("o_w", [P, KT, D])
        o_b = sb("o_b", [P, KT, D])

        sp_ = [pb(f"s{n}") for n in range(2)]
        ptp = [pb(f"pt{n}") for n in range(2)]
        ovp = [pb(f"ov{n}") for n in range(2)]
        qp = pb("qp")
        misc = pb("misc")
        block = tiles.enter_context(nc.Block("mqa"))
        X = T.X

        def ok(b):
            return not is_int(b) or 0 <= b < NB

        def n(b):
            return b + 1

        def nh(b, h):
            return b * (AH // 2) + (h // 2 + 1)

        def nq(b, p):
            return b * PAIRS + (p + 1)

        def np_(b, p):
            return b * (PAIRS // 2) + (p // 2 + 1)

        def run(eng, iteration):
            first = 3
            for i in range(-2, first):
                iteration(i, i % 2)
            pairs = (NB - 2 - first) // 2
            with eng.Fori(0, pairs) as j:
                iteration(j * 2 + first, 1)
                iteration(j * 2 + (first + 1), 0)
            for i in range(2 * pairs + first, NB + 1):
                iteration(i, i % 2)

        def take(eng, copy, b, h):
            eng.wait_ge(S.pt_full[h % 2], due(nh(b, h)))
            pair = (h - PR4) // 2
            if pair >= 0:
                eng.wait_ge(S.ov_full[pair % 2], due(np_(b, pair)))
            else:
                eng.wait_ge(S.ov_full[pair % 2], due(np_(b - 1, pair + PAIRS)))
            copy(pt[:, h % PR4, :, :].rearrange("p t q -> p (t q)"), ptp[h % 2][:, :]).then_inc(S.pt_sb[h % 2], 1)

        @block.gpsimd
        def _(pool):
            def row_factors(b):
                count0 = value(pool, n(b))
                count1 = value(pool, n(b - 1))
                pool.wait_ge(T.made, 1)
                pool.wait_ge(S.stats, count0)
                pool.wait_ge(S.xn, count1)
                pool.tensor_scalar(veps[:, 0, :], mv[:, :, 1], EPS5, EPS5 * EPS5, ALU.mult, ALU.add)\
                    .then_inc(S.sum_eps, 1)
                pool.wait_ge(S.sum_eps, due(n(b)))
                pool.tensor_tensor(veps[:, 1, :], veps[:, 0, :], mv[:, :, 1], ALU.add).then_inc(S.veps, 1)
                pool.wait_ge(S.veps, due(n(b)))
                pool.tensor_tensor(rs[:, :], veps[:, 1, :], T.neghalf[:, 0, 0:KT], ALU.pow).then_inc(S.rnorm, 1)

            def out_factors(b):
                count0 = value(pool, n(b))
                pool.wait_ge(T.made, 1)
                pool.wait_ge(S.o_stats, count0)
                pool.tensor_scalar(oveps[:, :], omv[:, :, 1], EPS5, None, ALU.add).then_inc(S.o_veps, 1)
                pool.wait_ge(S.o_veps, due(n(b)))
                pool.tensor_tensor(ors[:, :], oveps[:, :], T.neghalf[:, 0, 0:KT], ALU.pow).then_inc(S.o_rnorm, 1)

            def finish(b):
                pool.wait_ge(S.o_norm, due(n(b)))
                row = lambda t: t[:, :].unsqueeze(1).to_broadcast([P, KT, D])
                pool.tensor_tensor(o_w[:, :, :], o_n[:, :, :], row(T.out_w), ALU.mult).then_inc(S.o_w, 1)
                pool.wait_ge(S.o_w, due(n(b)))
                pool.tensor_tensor(o_b[:, :, :], o_w[:, :, :], row(T.out_b), ALU.add).then_inc(S.o_b, 1)
                pool.wait_ge(S.o_b, due(n(b)))
                at = cols(b * SEQ, SEQ)
                pool.tensor_tensor(X[:, at], X[:, at], o_b[:, :, :].rearrange("p k d -> p (k d)"), ALU.add)\
                    .then_inc(S.x, 1)

            def iteration(i, par):
                if ok(i - 1):
                    out_factors(i - 1)
                    finish(i - 1)
                if ok(i + 2):
                    row_factors(i + 2)

            run(pool, iteration)

        @block.scalar
        def _(act):
            def exponentials(b, h):
                s = h % 2
                act.wait_ge(S.mx[s], due(nh(b, h)))
                if h >= PR4:
                    act.wait_ge(S.pt_full[s], due(nh(b, h - PR4)))
                else:
                    act.wait_ge(S.pt_full[s], due(nh(b - 1, h + AH - PR4)))
                for t in range(KT):
                    ins = act.activation(pr[:, h % PR4, t, :], sp_[s][:, t * SEQ:(t + 1) * SEQ], ACT.Exp,
                                         bias=nmax[:, h, t:t + 1], accum_out=sums[:, h, t:t + 1])
                ins.then_inc(S.exp[s], 1)

            def take_transposes(b, h):
                take(act, lambda dst, src: act.activation(dst, src, ACT.Copy), b, h)

            def iteration(i, par):
                for s in range(AH):
                    if ok(i):
                        exponentials(i, s)
                    h = s - PT_LAG
                    if h % 2 == 1:
                        if h >= 0 and ok(i):
                            take_transposes(i, h)
                        if h < 0 and ok(i - 1):
                            take_transposes(i - 1, h + AH)
                    if s == 0 and ok(i + 1):
                        b = i + 1
                        act.wait_ge(S.xt_ready, due(n(b)))
                        act.wait_ge(S.q_ready, due(nq(b - 1, PAIRS - 1)))
                        act.activation(xT[:, :], misc[:, 0:SEQ], ACT.Identity, scale=T.norm_w[:, 0:1],
                                       bias=T.norm_b[:, 0:1]).then_inc(S.xt, 1)
                    if s == 1 and ok(i + 1):
                        b, buf = i + 1, 1 - par
                        act.wait_ge(S.kv_ready, due(n(b)))
                        act.wait_ge(S.s_full[1], due(nh(b - 2, AH - 1)))
                        act.wait_ge(S.ov_full[1], due(np_(b - 2, PAIRS - 1)))
                        act.activation(vals[buf][:, :, :].rearrange("p k d -> p (k d)"),
                                       misc[:, SEQ:SEQ + KT * AD], ACT.Copy)
                        act.activation(k_hi[buf][:, :], misc[:, 0:SEQ], ACT.Copy, scale=ASCALE)\
                            .then_inc(S.k_hi, 1)
                    if s in Q_SLOTS and ok(i + 1):
                        b, p = i + 1, Q_SLOTS[s]
                        act.wait_ge(S.q_ready, due(nq(b, p)))
                        act.wait_ge(S.q, due(nq(b, p) - 1))
                        act.activation(q_hi[:, :], qp[:, :], ACT.Copy).then_inc(S.q_hi, 1)
                    if s in PAIR_SLOTS:
                        off, p = PAIR_SLOTS[s]
                        if ok(i + off):
                            b = i + off
                            act.wait_ge(S.ov_full[p % 2], due(np_(b, p)))
                            act.wait_ge(S.wo_ready, due(n(b - 1)))
                            act.activation(oT[:, p, :], ovp[p % 2][:, 0:SEQ], ACT.Copy).then_inc(S.ov_sb[p % 2], 1)

            run(act, iteration)

        @block.vector
        def _(dve):
            def row_stats(b):
                for k in range(KT):
                    ins = dve.bn_stats(st6[:, k, :], X[:, cols(b * SEQ + k * D, D)])
                ins.then_inc(S.bn, 1)
                count0 = value(dve, n(b))
                dve.wait_ge(T.made, 1)
                dve.wait_ge(S.bn, count0)
                for k in range(KT):
                    ins = dve.bn_aggr(mv[:, k, :], st6[:, k, :])
                ins.then_inc(S.stats, 1)

            def norm_rows(b):
                dve.wait_ge(S.rnorm, due(n(b)))
                dve.wait_ge(S.xt_ready, due(n(b - 1)))
                for k in range(KT):
                    ins = dve.tensor_scalar(xn[:, k, :], X[:, cols(b * SEQ + k * D, D)], mv[:, k, 0:1],
                                            rs[:, k:k + 1], ALU.subtract, ALU.mult)
                ins.then_inc(S.xn, 1)

            def maximum(b, h):
                s = h % 2
                dve.wait_ge(S.s_full[s], due(nh(b, h)))
                dve.wait_ge(S.exp[s], due(nh(b, h) - (AH // 2)))
                dve.tensor_reduce(nmax[:, h, :], sp_[s][:, :].rearrange("p (t k) -> p t k", t=KT), AX.X, ALU.max,
                                  negate=True).then_inc(S.mx[s], 1)

            def probabilities(b, h):
                s = h % 2
                dve.wait_ge(S.exp[s], due(nh(b, h)))
                dve.reciprocal(recs[:, h, :], sums[:, h, :]).then_inc(S.rec[s], 1)
                dve.wait_ge(S.rec[s], due(nh(b, h)))
                for t in range(KT):
                    ins = dve.tensor_scalar(pr[:, h % PR4, t, :], pr[:, h % PR4, t, :], recs[:, h, t:t + 1], None,
                                            ALU.mult)
                ins.then_inc(S.pn[s], 1)

            def out_rows(b):
                dve.wait_ge(S.wo_ready, due(n(b)))
                dve.tensor_copy(o_sb[:, :, :].rearrange("p k d -> p (k d)"), misc[:, 0:KT * D]).then_inc(S.wo, 1)
                dve.wait_ge(S.wo, due(n(b)))
                for k in range(KT):
                    ins = dve.bn_stats(ost6[:, k, :], o_sb[:, k, :])
                ins.then_inc(S.o_bn, 1)
                count0 = value(dve, n(b))
                dve.wait_ge(T.made, 1)
                dve.wait_ge(S.o_bn, count0)
                for k in range(KT):
                    ins = dve.bn_aggr(omv[:, k, :], ost6[:, k, :])
                ins.then_inc(S.o_stats, 1)

            def out_norm(b):
                dve.wait_ge(S.o_rnorm, due(n(b)))
                dve.wait_ge(S.o_w, due(n(b - 1)))
                for k in range(KT):
                    ins = dve.tensor_scalar(o_n[:, k, :], o_sb[:, k, :], omv[:, k, 0:1], ors[:, k:k + 1],
                                            ALU.subtract, ALU.mult)
                ins.then_inc(S.o_norm, 1)

            def iteration(i, par):
                for s in range(AH):
                    if ok(i):
                        maximum(i, s)
                        if s:
                            probabilities(i, s - 1)
                    if s == 0 and ok(i - 1):
                        probabilities(i - 1, AH - 1)
                    h = s - PT_LAG
                    if h % 2 == 0:
                        if h >= 0 and ok(i):
                            take(dve, dve.tensor_copy, i, h)
                        if h < 0 and ok(i - 1):
                            take(dve, dve.tensor_copy, i - 1, h + AH)
                    if s == 1 and ok(i + 1):
                        b, buf = i + 1, 1 - par
                        dve.wait_ge(S.k_hi, due(n(b)))
                        dve.scalar_tensor_tensor(k_lo[buf][:, :], misc[:, 0:SEQ], ASCALE,
                                                 k_hi[buf][:, :].bitcast(F32), op0=ALU.mult, op1=ALU.subtract)\
                            .then_inc(S.k_lo, 1)
                    if s in Q_SLOTS and ok(i + 1):
                        b, p, buf = i + 1, Q_SLOTS[s], 1 - par
                        dve.wait_ge(S.q_hi, due(nq(b, p)))
                        dve.scalar_tensor_tensor(qst[buf][:, 2 * p * SEQ:(2 * p + 2) * SEQ], q_hi[:, :].bitcast(F32),
                                                 T.low_rows[:, 0:1], qp[:, :], op0=ALU.mult, op1=ALU.add)\
                            .then_inc(S.q, 1)
                    if s == 4 and ok(i - 1):
                        out_rows(i - 1)
                    if s == 5 and ok(i + 2):
                        row_stats(i + 2)
                    if s == 6 and ok(i - 1):
                        out_norm(i - 1)
                    if s == 7 and ok(i + 2):
                        norm_rows(i + 2)

            run(dve, iteration)

        @block.tensor
        def _(pe):
            def scores(b, h, buf):
                s = h % 2
                if h == 0:
                    pe.wait_ge(S.q, due(nq(b, PAIRS - 1)))
                    pe.wait_ge(S.k_lo, due(n(b)))
                pe.wait_ge(S.exp[s], due(nh(b, h) - 1))
                for t in range(KT):
                    q = qst[buf][:, h * SEQ + t * P:h * SEQ + (t + 1) * P]
                    out = sp_[s][:, t * SEQ:(t + 1) * SEQ]
                    pe.matmul(out, q, k_lo[buf][:, :], start=(t == 0), stop=False, skip_group_check=True)
                    ins = pe.matmul(out, q, k_hi[buf][:, :], start=False, stop=(t == KT - 1),
                                    skip_group_check=True)
                ins.then_inc(S.s_full[s], 1)

            def transposes(b, h):
                s = h % 2
                pe.wait_ge(S.pn[s], due(nh(b, h)))
                pe.wait_ge(S.pt_sb[s], due(nh(b, h) - 1))
                for kt in range(KT):
                    for t in range(KT):
                        at = kt * SEQ + t * P
                        ins = pe.transpose(ptp[s][:, at:at + P], pr[:, h % PR4, t, kt * P:(kt + 1) * P],
                                           T.ident[:, :])
                ins.then_inc(S.pt_full[s], 1)

            def value_products(b, p, buf):
                for s in range(2):
                    pe.wait_ge(S.pt_sb[s], due(nh(b, 2 * p + s)))
                pe.wait_ge(S.ov_sb[p % 2], due(np_(b, p) - 1))
                for kt in range(KT):
                    for m in range(2):
                        ins = pe.matmul(ovp[p % 2][AD * m:AD * (m + 1), 0:SEQ], vals[buf][:, kt, :],
                                        pt[:, (2 * p + m) % PR4, kt, :], start=(kt == 0), stop=(kt == KT - 1),
                                        skip_group_check=True)
                ins.then_inc(S.ov_full[p % 2], 1)

            def iteration(i, par):
                for s in range(AH):
                    if ok(i):
                        scores(i, s, par)
                    if s == 0 and ok(i + 1):
                        b = i + 1
                        pe.wait_ge(S.xn, due(n(b)))
                        pe.wait_ge(S.wo, due(n(b - 3)))
                        for k in range(KT):
                            ins = pe.transpose(misc[:, k * P:(k + 1) * P], xn[:, k, :], T.ident[:, :])
                        ins.then_inc(S.xt_ready, 1)
                    if s == 1 and ok(i + 1):
                        b = i + 1
                        pe.wait_ge(S.xt, due(n(b)))
                        pe.matmul(misc[:, 0:SEQ], T.awk[:, :], xT[:, :], start=True, stop=True)
                        for k in range(KT):
                            ins = pe.matmul(misc[:, SEQ + k * AD:SEQ + (k + 1) * AD], xT[:, k * P:(k + 1) * P],
                                            T.awv[:, :], start=True, stop=True)
                        ins.then_inc(S.kv_ready, 1)
                    if s in Q_SLOTS and ok(i + 1):
                        b, p = i + 1, Q_SLOTS[s]
                        pe.wait_ge(S.q, due(nq(b, p) - 1))
                        for m in range(2):
                            h = 2 * p + m
                            ins = pe.matmul(qp[:, m * SEQ:(m + 1) * SEQ], T.awq[:, h * P:(h + 1) * P], xT[:, :],
                                            start=True, stop=True)
                        ins.then_inc(S.q_ready, 1)
                    h = s - PT_LAG
                    if h >= 0 and ok(i):
                        transposes(i, h)
                    if h < 0 and ok(i - 1):
                        transposes(i - 1, h + AH)
                    if s in PAIR_SLOTS:
                        off, p = PAIR_SLOTS[s]
                        if ok(i + off):
                            value_products(i + off, p, (par + off) % 2)
                    if s == 3 and ok(i - 1):
                        b = i - 1
                        for r in range(2):
                            pe.wait_ge(S.ov_sb[r], due(np_(b, PAIRS - 2 + r)))
                        if ok(b + 2):
                            pe.wait_ge(S.k_lo, due(n(b + 2)))
                        else:
                            pe.wait_ge(S.wo, due(n(b - 1)))
                        for k in range(KT):
                            for p in range(PAIRS):
                                ins = pe.matmul(misc[:, k * D:(k + 1) * D], oT[:, p, k * P:(k + 1) * P],
                                                T.awo[:, p * D:(p + 1) * D], start=(p == 0), stop=(p == PAIRS - 1))
                        ins.then_inc(S.wo_ready, 1)

            run(pe, iteration)


def rotary_tables():
    half = MD // 2
    inv_freq = (np.float32(1.0) / np.float32(10000.0) ** (np.arange(half, dtype=np.float32) / np.float32(half)))
    angle = np.arange(SEQ, dtype=np.float32)[:, None] * inv_freq[None, :].astype(np.float32)
    cos, sin = np.cos(angle).T, np.sin(angle).T
    cos8 = np.concatenate([cos, cos])
    sin8 = np.concatenate([-sin, sin])
    return (np.ascontiguousarray(np.repeat(cos8, MH, axis=0), dtype=np.float32),
            np.ascontiguousarray(np.repeat(sin8, MH, axis=0), dtype=np.float32))


def by_dim(w, swap=False):
    w = w.reshape(MH, MD, w.shape[1])
    if swap:
        w = np.concatenate([w[:, MD // 2:], w[:, :MD // 2]], axis=1)
    return np.ascontiguousarray(w.transpose(2, 1, 0).reshape(w.shape[2], MH * MD))


def gate_rows_select():
    out = np.zeros((GR, 2 + 2 * NE), np.float32)
    for part in range(3):
        for e in range(NE):
            row = out[part * NE + e]
            row[0] = -1.0 if part > 0 else 0.0
            row[1] = -1.0 if part > 1 else 0.0
            row[2 + e] = 1.0
            if part == 0:
                row[2 + NE:] = -BIG
                row[2 + NE + e] = 0.0
    return out


def laid_out(v):
    v = {k: np.asarray(a) for k, a in v.items()}
    cos, sin = rotary_tables()
    col = lambda a: np.ascontiguousarray(a.reshape(-1, 1))
    return {
        "x": v["L0_attn_x"],
        "wq": by_dim(v["L0_ffn_Wq"]), "wq_swap": by_dim(v["L0_ffn_Wq"], True),
        "wuk": by_dim(v["L0_ffn_Wuk"]), "wuk_swap": by_dim(v["L0_ffn_Wuk"], True),
        "wuv": np.ascontiguousarray(v["L0_ffn_Wuv"].T), "wo": np.ascontiguousarray(v["L0_ffn_Wo"].T),
        "wdkv": np.ascontiguousarray(v["L0_ffn_Wdkv"].T), "cos": cos, "sin": sin,
        "norm2": col(v["L0_ffn_norm2_w"]), "gate": np.ascontiguousarray(v["L0_ffn_gate_w"].T),
        "gate_b": v["L0_ffn_gate_b"].reshape(1, NE), "gate_sel": gate_rows_select(),
        "b1": v["L0_ffn_b1"], "b2": v["L0_ffn_b2"],
        "w1": np.ascontiguousarray(v["L0_ffn_W1"].transpose(2, 0, 1).reshape(D, NE * HID)),
        "w2": np.ascontiguousarray(v["L0_ffn_W2"].reshape(NE, D, HC, P).transpose(3, 0, 2, 1).reshape(P, NE * HC * D)),
        "awq": np.ascontiguousarray(np.repeat(v["L0_attn_Wq"].reshape(D, AH, 1, AD), 2, axis=2).reshape(D, AH * P)),
        "awk": np.ascontiguousarray(np.concatenate([v["L0_attn_Wkv"][:, :AD]] * 2, axis=1)),
        "awv": np.ascontiguousarray(v["L0_attn_Wkv"][:, AD:]),
        "awo": np.ascontiguousarray(v["L0_attn_Wo"].reshape(PAIRS, P, D).transpose(1, 0, 2).reshape(P, PAIRS * D)),
        "norm_w": col(v["L0_attn_norm_w"]), "norm_b": col(v["L0_attn_norm_b"]),
        "out_w": v["L0_attn_out_norm_w"].reshape(1, D), "out_b": v["L0_attn_out_norm_b"].reshape(1, D),
        "norm1": col(v["L0_ffn_norm1_w"]), "ln_g": col(v["L0_ffn_ln_g"]), "ln_b": col(v["L0_ffn_ln_b"]),
    }


def build(nc, A, out):
    ctx = ExitStack()
    with ctx:
        def sb(name, shape, dt=F32):
            return ctx.enter_context(nc.sbuf_tensor(name, shape, dt))

        def sem(name):
            return ctx.enter_context(nc.semaphore(name))

        T = Tiles()
        T.made = sem("made")
        T.X = sb("X", [P, NT * D])
        T.U = sb("U", [P, NT * D])
        T.wq, T.wq_swap = sb("wq", [D, P]), sb("wq_swap", [D, P])
        T.wuk, T.wuk_swap = sb("wuk", [LAT, P]), sb("wuk_swap", [LAT, P])
        T.wuv, T.wo, T.wdkv = sb("wuv", [LAT, D]), sb("wo", [D, D]), sb("wdkv", [D, LAT])
        T.cos, T.sin = sb("cos", [P, SEQ]), sb("sin", [P, SEQ])
        T.norm1, T.ln_g, T.ln_b = sb("norm1", [D, 1]), sb("ln_g", [LAT, 1]), sb("ln_b", [LAT, 1])
        T.qstack = [sb(f"qstack{n}", [P, MH * SEQ], F32R) for n in range(2)]
        T.kstack = [sb(f"kstack{n}", [P, MH * SEQ], F32R) for n in range(2)]
        T.va = [sb(f"va{n}", [P, KT, MH, MW]) for n in range(2)]
        T.norm2, T.gate, T.gate_b = sb("norm2", [D, 1]), sb("gate", [D, NE]), sb("gate_b", [P, NE])
        T.w1_hi, T.w1_lo = sb("w1_hi", [D, NQ * P], F32R), sb("w1_lo", [D, NQ * P], F32R)
        T.w2_hi, T.w2_lo = sb("w2_hi", [P, NQ * D], F32R), sb("w2_lo", [P, NQ * D], F32R)
        T.gate_rows, T.b2_rows = sb("gate_rows", [GR, NQ * P], BF16), sb("b2_rows", [GR, D], BF16)
        T.awq, T.awk, T.awv = sb("awq", [D, AH * P]), sb("awk", [D, P]), sb("awv", [D, AD])
        T.awo = sb("awo", [P, PAIRS * D])
        T.norm_w, T.norm_b = sb("norm_w", [D, 1]), sb("norm_b", [D, 1])
        T.out_w, T.out_b = sb("out_w", [P, D]), sb("out_b", [P, D])
        T.low_rows = sb("low_rows", [P, 1])
        T.neghalf = sb("neghalf", [P, 2, KT])
        T.ident, T.ident_bf = sb("ident", [P, P]), sb("ident_bf", [P, P], BF16)
        T.neg = sb("neg", [P, 4, P], BF16)

        mla, moe, mqa = MlaSems(sem), MoeSems(sem), MqaSems(sem)
        setup_phase(nc, T, A, sem)
        mla_phase(nc, T, mla, 0)
        moe_phase(nc, T, moe, 0)
        mqa_phase(nc, T, mqa)
        mla_phase(nc, T, mla, NB)
        moe_phase(nc, T, moe, NC, out)


def kernel(**inputs):
    import concourse.bacc as bacc
    from concourse.bass_utils import run_bass_kernel_spmd

    arrays = laid_out(inputs)
    nc = bacc.Bacc("TRN2", target_bir_lowering=False, num_devices=1)
    dram = {name: nc.dram_tensor(f"in_{name}", a.shape, mybir.dt.from_np(a.dtype), kind="ExternalInput").ap()
            for name, a in arrays.items()}
    out = nc.dram_tensor("out", (NB, SEQ, D), F32, kind="ExternalOutput").ap()
    build(nc, dram, out)
    result = run_bass_kernel_spmd(nc, [{f"in_{name}": a for name, a in arrays.items()}], core_ids=[0])
    return result.results[0]["out"]
```

```python
from contextlib import ExitStack

import concourse.bass as bass
import numpy as np
from concourse import mybir

F32 = mybir.dt.float32
F32R = mybir.dt.float32r
BF16 = mybir.dt.bfloat16
ALU = mybir.AluOpType
ACT = mybir.ActivationFunctionType
AX = mybir.AxisListType

P = 128
NB, SEQ, D = 16, 256, 128
NT = NB * SEQ // P
KT = SEQ // P
MH, MD = 16, 8
MW = 32
HH = MH // 2
LAT = 64
NE, HID = 4, 512
HC = HID // P
AH, AD = 8, 64
EPS5, EPS6 = 1e-5, 1e-6
BIG = 1e30
GRP = 4
MSCALE = float(MD) ** -0.5
ASCALE = float(AD) ** -0.5


def is_int(v):
    return isinstance(v, int)


def due(count):
    return max(count, 0) if is_int(count) else count


def value(eng, count):
    return due(count) if is_int(count) else eng.to_reg(count)


def cols(start, size):
    return slice(start, start + size) if is_int(start) else bass.ds(start, size)


def words(view):
    return view.bitcast(F32)


class Tiles:
    pass


def setup_phase(nc, T, A, sem):
    loaded = {name: sem(f"load_{name}") for name in ("x", "small", "w1", "w2")}
    step = sem("setup_step")
    zeroed = sem("setup_zeroed")
    tiles = ExitStack()

    def own(name, shape, dt=F32):
        return tiles.enter_context(nc.sbuf_tensor(f"setup_{name}", shape, dt))

    w1 = own("w1", [D, NQ * P])
    w2 = own("w2", [P, NQ * D])
    bias = own("bias", [GR, HID + D])
    rows = own("rows", [GR, 2 + 2 * NE])
    near = own("near", [GR, HID + D], BF16)
    rest = own("rest", [GR, HID + D])
    part = own("part", [GR, HID + D], BF16)
    small = [
        (T.norm1, A["norm1"]), (T.wdkv, A["wdkv"]), (T.wq, A["wq"]), (T.wq_swap, A["wq_swap"]),
        (T.ln_g, A["ln_g"]), (T.ln_b, A["ln_b"]), (T.wuk, A["wuk"]), (T.wuk_swap, A["wuk_swap"]),
        (T.wuv, A["wuv"]), (T.wo, A["wo"]), (T.cos, A["cos"]), (T.sin, A["sin"]),
        (T.norm2, A["norm2"]), (T.gate, A["gate"]), (T.gate_b, A["gate_b"].to_broadcast([P, NE])),
        (rows, A["gate_sel"]),
        (T.awq, A["awq"]), (T.awk, A["awk"]), (T.awv, A["awv"]), (T.awo, A["awo"]),
        (T.norm_w, A["norm_w"]), (T.norm_b, A["norm_b"]),
        (T.out_w, A["out_w"].to_broadcast([P, D])), (T.out_b, A["out_b"].to_broadcast([P, D])),
    ]
    def ones_under_keys(eng, buf):
        rows = T.stack[buf][4 * MD:4 * MD + 2, :].bitcast(F32).rearrange("p (h c) -> p h c", h=MH)
        eng.memset(rows[:, :, SEQ:2 * SEQ], 1.0)

    small_count = 16 * (len(small) + 6)

    with tiles, nc.Block("setup") as block:
        @block.sync
        def _(sp):
            sp.dma_start(T.X[:, :].rearrange("p (t d) -> p t d", d=D),
                         A["x"].rearrange("b (k p) d -> p (b k) d", p=P)).then_inc(loaded["x"], 16)
            sp.dma_start(w1[:, :], A["w1"]).then_inc(loaded["w1"], 16)
            sp.dma_start(w2[:, :], A["w2"]).then_inc(loaded["w2"], 16)
            sp.wait_ge(loaded["x"], 16)

        @block.scalar
        def _(act):
            for tile, array in small:
                act.dma_start(tile[:, :], array).then_inc(loaded["small"], 16)
            for p in range(3):
                act.dma_start(bias[p * NE:(p + 1) * NE, 0:HID], A["b1"]).then_inc(loaded["small"], 16)
                act.dma_start(bias[p * NE:(p + 1) * NE, HID:HID + D], A["b2"]).then_inc(loaded["small"], 16)

        @block.gpsimd
        def _(pool):
            pool.memset(T.neghalf[:, :, :], -0.5)
            pool.memset(T.ident[:, :], 0.0)
            pool.memset(T.ident_bf[:, :], 0.0)
            pool.memset(T.neg[:, :, :], 0.0).then_inc(zeroed, 1)
            pool.wait_ge(zeroed, 1)
            for m in (T.ident, T.ident_bf):
                pool.affine_select(out=m[:, :], in_=m[:, :], compare_op=ALU.not_equal, fill=1.0, base=0,
                                   pattern=[[-1, P]], channel_multiplier=1)
            pool.affine_select(out=T.neg[:, :, :], in_=T.neg[:, :, :], compare_op=ALU.is_ge, fill=-BIG, base=0,
                               pattern=[[0, 4], [-1, P]], channel_multiplier=1).then_inc(T.made, 1)
            pool.memset(T.stack[1][:, :].bitcast(F32), 0.0).then_inc(zeroed, 1)
            pool.wait_ge(zeroed, 2)
            ones_under_keys(pool, 1)

        @block.vector
        def _(dve):
            dve.memset(T.stack[0][:, :].bitcast(F32), 0.0).then_inc(step, 1)
            dve.wait_ge(step, 1)
            ones_under_keys(dve, 0)
            for buf in range(2):
                dve.memset(T.va[buf][:, :, :, :], 1.0)
            dve.wait_ge(loaded["small"], small_count)
            dve.tensor_copy(near[:, :], bias[:, :]).then_inc(step, 1)
            dve.wait_ge(step, 2)
            dve.scalar_tensor_tensor(rest[:, :], near[:, :], rows[:, 0:1], bias[:, :], op0=ALU.mult, op1=ALU.add)\
                .then_inc(step, 1)
            dve.wait_ge(step, 3)
            dve.tensor_copy(near[:, :], rest[:, :]).then_inc(step, 1)
            dve.wait_ge(step, 4)
            dve.scalar_tensor_tensor(part[:, :], near[:, :], rows[:, 1:2], rest[:, :], op0=ALU.mult, op1=ALU.add)\
                .then_inc(step, 1)
            dve.wait_ge(step, 5)
            for e in range(NE):
                dve.tensor_scalar(T.gate_rows[:, e * HID:(e + 1) * HID], part[:, 0:HID],
                                  rows[:, 2 + e:3 + e], rows[:, 2 + NE + e:3 + NE + e], ALU.mult, ALU.add)
            dve.tensor_copy(T.b2_rows[:, :], part[:, HID:HID + D])
            for k, (name, w, hi, lo) in enumerate((("w1", w1, T.w1_hi, T.w1_lo), ("w2", w2, T.w2_hi, T.w2_lo))):
                dve.wait_ge(loaded[name], 16)
                dve.tensor_copy(hi[:, :], w[:, :]).then_inc(step, 1)
                dve.wait_ge(step, 6 + k)
                dve.tensor_tensor(lo[:, :], w[:, :], hi[:, :].bitcast(F32), ALU.subtract)


LATENT_MISC = {0: ("un_t", 2), 1: ("latent", 2), 2: ("q", 2), 3: ("head_t0", -1), 4: ("latent_t", 2), 5: ("k", 2),
              6: ("head_t1", -1), 7: ("out_t", -1), 8: ("max_t", 1), 9: ("v", 2), 11: ("wo", -1)}
MISC_TURNS = [LATENT_MISC[s] for s in sorted(LATENT_MISC)]
UNITS = [unit for half in range(2) for unit in
         [(half * HH + 4 * m, 4, 0) for m in range(2)] + [(half * HH + 2 * m, 2, 1) for m in range(4)]]
MAX_SLOTS = {0: (0, 1), 1: (2,), 2: (3, 4), 3: (5,), 4: (6, 7), 5: (8, 9), 6: (10,), 7: (11,)}
VALUE_SLOTS = {1: (-1, 3), 4: (0, 0), 7: (0, 1), 10: (0, 2)}
SLOTS = 12
MX_BANKS, ST_BANKS = 2, 3
RING = 6
STACK_DMAS = 5 * 16
MAXROW_DMAS = 2 * 16


class MlaSems:

    def __init__(self, sem):
        self.bn = sem("mla_bn")
        self.stats = sem("mla_stats")
        self.veps = sem("mla_veps")
        self.rnorm = sem("mla_rnorm")
        self.u = sem("mla_u")
        self.turn = {k: sem(f"mla_{k}_ready") for k, _ in MISC_TURNS}
        self.taken = {k: sem(f"mla_{k}_taken") for k, _ in MISC_TURNS}
        self.lat_bn = sem("mla_lat_bn")
        self.lat_stats = sem("mla_lat_stats")
        self.lat_veps = sem("mla_lat_veps")
        self.lat_rnorm = sem("mla_lat_rnorm")
        self.latn = sem("mla_latn")
        self.rot = sem("mla_rot")
        self.hi = sem("mla_hi")
        self.lo = sem("mla_lo")
        self.va = sem("mla_va")
        self.stack = [sem(f"mla_stack{n}") for n in range(2)]
        self.maxrow = sem("mla_maxrow")
        self.mt_hi = sem("mla_mt_hi")
        self.mx_full = [sem(f"mla_mx_full{v}") for v in range(MX_BANKS)]
        self.mx_done = [sem(f"mla_mx_done{v}") for v in range(MX_BANKS)]
        self.st_full = [sem(f"mla_st_full{s}") for s in range(ST_BANKS)]
        self.exp = [sem(f"mla_exp{s}") for s in range(ST_BANKS)]
        self.masked = [sem(f"mla_masked{g}") for g in range(GRP)]
        self.ov_full = [sem(f"mla_ov_full{g}") for g in range(GRP)]
        self.ov_taken = [sem(f"mla_ov_taken{g}") for g in range(GRP)]
        self.recip = [sem(f"mla_recip{k}") for k in range(KT)]


def mla_phase(nc, T, S, base):
    tiles = ExitStack()
    with tiles:
        def sb(name, shape, dt=F32):
            return tiles.enter_context(nc.sbuf_tensor(f"mla{base}_{name}", shape, dt))

        def pb(name):
            return tiles.enter_context(nc.psum_tensor(f"mla{base}_{name}", [P, 512], F32))

        st6 = sb("st6", [P, KT, 6])
        mv = sb("mv", [P, KT, 2])
        veps = sb("veps", [P, 2, KT])
        rs = sb("rs", [P, 2, KT])
        un = sb("un", [P, KT, D])
        unT = sb("unT", [D, SEQ])
        lat = sb("lat", [P, KT, LAT])
        lst6 = sb("lst6", [P, KT, 6])
        lmv = sb("lmv", [P, KT, 2])
        lveps = sb("lveps", [P, KT])
        lrs = sb("lrs", [P, KT])
        latn = sb("latn", [P, KT, LAT])
        latT = sb("latT", [LAT, SEQ])
        t_cos = sb("t_cos", [P, 2, SEQ])
        t_sin = sb("t_sin", [P, 2, SEQ])
        rot = sb("rot", [P, 2, SEQ])
        parts = sb("parts", [P, 4, SEQ], F32R)
        hi, lo = parts[:, 0:3:2, :], parts[:, 1:4:2, :]
        vst = sb("vst", [P, KT, MH, MD])
        mx = sb("mx", [P, KT, MH])
        mt_hi = sb("mt_hi", [MH, SEQ], F32R)
        mt_lo = sb("mt_lo", [MH, SEQ], F32R)
        pr = sb("pr", [P, RING, 512])
        ot = sb("ot", [P, 2, GRP, SEQ])
        rec = sb("rec", [P, KT, MH])
        on = sb("on", [P, KT, MH, MD])
        onT = sb("onT", [D, SEQ])
        va = T.va

        st = [pb(f"st{n}") for n in range(3)]
        mxp = [pb(f"mxp{n}") for n in range(2)]
        ov = [pb(f"ov{n}") for n in range(2)]
        misc = pb("misc")
        block = tiles.enter_context(nc.Block(f"mla{base}"))
        X, U = T.X, T.U

        def queries(buf, h, first=0, size=SEQ):
            return T.stack[buf][:, h * 2 * SEQ + first:h * 2 * SEQ + first + size]

        def keys(buf, h, first=0, size=SEQ):
            return T.stack[buf][:, (h * 2 + 1) * SEQ + first:(h * 2 + 1) * SEQ + first + size]

        def query_rows(buf, row, rows, h, heads):
            return words(T.stack[buf][row:row + rows, :].rearrange("p (h c) -> p h c", h=MH)[:, h:h + heads, 0:SEQ])

        def ok(b):
            return not is_int(b) or 0 <= b < NB

        def n(b):
            return b + (base + 1)

        def nr(b, which):
            return (b + base) * 2 + (which + 1)

        def nu(b, unit, banks):
            return (b + base) * (SLOTS // banks) + (unit // banks + 1)

        def before(i, kind):
            here = [(k, i + o) for k, o in MISC_TURNS if ok(i + o)]
            at = [k for k, _ in here].index(kind)
            if at:
                return here[at - 1]
            if is_int(i):
                old = [(k, i - 1 + o) for k, o in MISC_TURNS if ok(i - 1 + o)]
                return old[-1] if old else None
            return MISC_TURNS[-1][0], i + (MISC_TURNS[-1][1] - 1)

        first = 3

        def run(eng, iteration):
            for i in range(-3, first):
                iteration(i, i % 2)
            pairs = (NB - 3 - first) // 2
            with eng.Fori(0, pairs) as j:
                iteration(j * 2 + first, 1)
                iteration(j * 2 + (first + 1), 0)
            for i in range(2 * pairs + first, NB + 1):
                iteration(i, i % 2)

        @block.sync
        def _(sp):
            def stack(b, half, buf):
                last = (SLOTS // 2) * (half + 1) - 1
                read = value(sp, nu(b - 2, last, ST_BANKS))
                passed = value(sp, nu(b - 1, half * SLOTS // 2, MX_BANKS))
                split = value(sp, nr(b, 1))
                sp.wait_ge(S.st_full[last % ST_BANKS], read)
                sp.wait_ge(S.mx_full[0], passed)
                sp.dma_start(query_rows(buf, 4 * MD, 2, half * HH, HH), query_rows(buf, 4 * MD + 2, 2, half * HH, HH))\
                    .then_inc(S.stack[half], 16)
                rows = slice(half * HH * MD, (half + 1) * HH * MD)
                at = slice(half * HH * 2 * SEQ, (half + 1) * HH * 2 * SEQ)
                for r, (q, k) in enumerate(((0, 2), (1, 2), (0, 3), (1, 3))):
                    if r < 2:
                        sp.wait_ge((S.hi, S.lo)[r], split)
                    sp.dma_start(words(T.stack[buf][r * MD:(r + 1) * MD, at]), words(parts[rows, q:k + 1:k - q, :]))\
                        .then_inc(S.stack[half], 16)

            def iteration(i, par):
                if ok(i + 2):
                    for half in range(2):
                        stack(i + 2, half, par)

            run(sp, iteration)

        @block.gpsimd
        def _(pool):
            def scale_factors(b):
                count0 = value(pool, n(b))
                count1 = value(pool, n(b - 1))
                pool.wait_ge(T.made, 1)
                pool.wait_ge(S.stats, count0)
                pool.wait_ge(S.u, count1)
                pool.tensor_scalar(veps[:, 0, :], mv[:, :, 1], EPS5, None, ALU.add)
                pool.tensor_scalar(veps[:, 1, :], mv[:, :, 1], 1.0 + EPS6, EPS5 * EPS6,
                                   ALU.mult, ALU.add).then_inc(S.veps, 1)
                pool.wait_ge(S.veps, due(n(b)))
                pool.tensor_tensor(rs[:, :, :], veps[:, :, :], T.neghalf[:, :, 0:KT], ALU.pow).then_inc(S.rnorm, 1)

            def latent_factors(b):
                count0 = value(pool, n(b))
                count1 = value(pool, n(b - 1))
                pool.wait_ge(T.made, 1)
                pool.wait_ge(S.lat_stats, count0)
                pool.wait_ge(S.latn, count1)
                pool.tensor_scalar(lveps[:, :], lmv[:, :, 1], EPS5, None, ALU.add).then_inc(S.lat_veps, 1)
                pool.wait_ge(S.lat_veps, due(n(b)))
                pool.tensor_tensor(lrs[:, :], lveps[:, :], T.neghalf[:, 0, 0:KT], ALU.pow).then_inc(S.lat_rnorm, 1)

            def rotate(b, which):
                pool.wait_ge(S.taken["qk"[which]], due(n(b)))
                pool.wait_ge(S.hi, due(nr(b - 1, which)))
                pool.wait_ge(S.lo, due(nr(b - 1, which)))
                pool.tensor_tensor(rot[:, which, :], t_cos[:, which, :], t_sin[:, which, :], ALU.add)\
                    .then_inc(S.rot, 1)

            def lower(b, which):
                pool.wait_ge(S.hi, due(nr(b, which)))
                for half in range(2):
                    pool.wait_ge(S.stack[half], due(n(b - 1) * STACK_DMAS))
                pool.tensor_tensor(lo[:, which, :], rot[:, which, :], hi[:, which, :].bitcast(F32),
                                   ALU.subtract).then_inc(S.lo, 1)

            def causal(b, s):
                count0 = value(pool, nu(b, s, ST_BANKS))
                pool.wait_ge(T.made, 1)
                pool.wait_ge(S.exp[s % ST_BANKS], count0)
                if s % 3 == 2:
                    view = pr[:, s % RING, :].rearrange("p (h q) -> p h q", h=4)
                else:
                    view = pr[:, s % RING, :].rearrange("p (h q) -> p h q", h=2)[:, :, 0:P]
                ins = pool.affine_select(out=view, in_=view, compare_op=ALU.is_ge, fill=0.0, base=0,
                                         pattern=[[0, view.shape[1]], [1, P]], channel_multiplier=-1)
                if s % 3 == 2:
                    ins.then_inc(S.masked[s // 3], 1)

            def iteration(i, par):
                for s in range(SLOTS):
                    if ok(i):
                        causal(i, s)
                    if s == 1 and ok(i + 2):
                        latent_factors(i + 2)
                    if s in (2, 5) and ok(i + 2):
                        rotate(i + 2, (2, 5).index(s))
                    if s in (4, 6) and ok(i + 2):
                        lower(i + 2, (4, 6).index(s))
                    if s == 8 and ok(i + 3):
                        scale_factors(i + 3)

            run(pool, iteration)

        @block.scalar
        def _(act):
            def copy_out(kind, b, dst, src, func=ACT.Copy, **kw):
                act.wait_ge(S.turn[kind], due(n(b)))
                act.activation(dst, src, func, **kw).then_inc(S.taken[kind], 1)

            def exponentials(b, s):
                act.wait_ge(S.st_full[s % ST_BANKS], due(nu(b, s, ST_BANKS)))
                if s >= RING:
                    act.wait_ge(S.ov_full[(s - RING) // 3], due(n(b)))
                else:
                    act.wait_ge(S.ov_full[(s + SLOTS - RING) // 3], due(n(b - 1)))
                act.activation(pr[:, s % RING, :], st[s % 3][:, :], ACT.Exp, scale=MSCALE).then_inc(S.exp[s % ST_BANKS], 1)

            def upper(b, which):
                act.wait_ge(S.rot, due(nr(b, which)))
                for half in range(2):
                    act.wait_ge(S.stack[half], due(n(b - 1) * STACK_DMAS))
                act.activation(hi[:, which, :], rot[:, which, :], ACT.Copy).then_inc(S.hi, 1)

            def take_products(b, g, par):
                act.wait_ge(S.ov_full[g], due(n(b)))
                act.wait_ge(S.turn["head_t1"], due(n(b - 1) if g == GRP - 1 else n(b - 2)))
                act.activation(ot[:, par, g, :], ov[g % 2][:, 0:SEQ], ACT.Copy).then_inc(S.ov_taken[g], 1)

            def iteration(i, par):
                for s in range(SLOTS):
                    if s == 8 and ok(i + 1):
                        act.wait_ge(S.turn["max_t"], due(n(i + 1)))
                        act.wait_ge(S.maxrow, due(n(i) * MAXROW_DMAS))
                        act.activation(mt_hi[:, :], misc[0:MH, 0:SEQ], ACT.Copy).then_inc(S.mt_hi, 1)
                    if ok(i):
                        exponentials(i, s)
                    if s == 0 and ok(i + 2):
                        act.wait_ge(S.turn["q"], due(n(i + 1)))
                        copy_out("un_t", i + 2, unT[:, :], misc[:, 0:SEQ], scale=T.norm1[:, 0:1])
                    if s == 2 and ok(i - 1):
                        take_products(i - 1, 3, 1 - par)
                    if s == 4 and ok(i + 2):
                        act.wait_ge(S.turn["v"], due(n(i + 1)))
                        copy_out("latent_t", i + 2, latT[:, :], misc[0:LAT, 0:SEQ], ACT.Identity,
                                 scale=T.ln_g[:, 0:1], bias=T.ln_b[:, 0:1])
                    if s == 5 and ok(i):
                        take_products(i, 0, par)
                    if s == 7 and ok(i - 1):
                        act.wait_ge(S.turn["wo"], due(n(i - 2)))
                        copy_out("out_t", i - 1, onT[:, :], misc[:, 0:SEQ])
                    if s in (3, 6) and ok(i + 2):
                        upper(i + 2, (3, 6).index(s))
                    if s == 9 and ok(i + 1):
                        b, buf = i + 1, 1 - par
                        act.wait_ge(S.taken["max_t"], due(n(b)))
                        act.dma_start(query_rows(buf, 4 * MD, 1, 0, MH), words(mt_hi[:, :])).then_inc(S.maxrow, 16)
                        act.dma_start(query_rows(buf, 4 * MD + 1, 1, 0, MH), words(mt_lo[:, :])).then_inc(S.maxrow, 16)
                    if s == 9 and ok(i + 2):
                        act.wait_ge(S.va, due(n(i + 1)))
                        copy_out("v", i + 2, vst[:, :, :, :].rearrange("p k h d -> p (k h d)"), misc[:, 0:SEQ])
                    if s == 8 and ok(i):
                        take_products(i, 1, par)
                    if s == 11 and ok(i):
                        take_products(i, 2, par)

            run(act, iteration)

        @block.vector
        def _(dve):
            def row_stats(b):
                for k in range(KT):
                    ins = dve.bn_stats(st6[:, k, :], X[:, cols(b * SEQ + k * D, D)])
                ins.then_inc(S.bn, 1)
                count0 = value(dve, n(b))
                dve.wait_ge(T.made, 1)
                dve.wait_ge(S.bn, count0)
                for k in range(KT):
                    ins = dve.bn_aggr(mv[:, k, :], st6[:, k, :])
                ins.then_inc(S.stats, 1)

            def norm_rows(b):
                dve.wait_ge(S.rnorm, due(n(b)))
                dve.wait_ge(S.turn["un_t"], due(n(b - 1)))
                for k in range(KT):
                    at = cols(b * SEQ + k * D, D)
                    dve.tensor_scalar(U[:, at], X[:, at], mv[:, k, 0:1], rs[:, 0, k:k + 1],
                                      ALU.subtract, ALU.mult)
                    ins = dve.tensor_scalar(un[:, k, :], X[:, at], mv[:, k, 0:1], rs[:, 1, k:k + 1],
                                            ALU.subtract, ALU.mult)
                ins.then_inc(S.u, 1)

            def latent_stats(b):
                dve.wait_ge(S.turn["latent"], due(n(b)))
                dve.tensor_copy(lat[:, :, :], misc[:, 0:KT * LAT].rearrange("p (k c) -> p k c", k=KT))\
                    .then_inc(S.taken["latent"], 1)
                dve.wait_ge(S.taken["latent"], due(n(b)))
                for k in range(KT):
                    ins = dve.bn_stats(lst6[:, k, :], lat[:, k, :])
                ins.then_inc(S.lat_bn, 1)
                count0 = value(dve, n(b))
                dve.wait_ge(T.made, 1)
                dve.wait_ge(S.lat_bn, count0)
                for k in range(KT):
                    ins = dve.bn_aggr(lmv[:, k, :], lst6[:, k, :])
                ins.then_inc(S.lat_stats, 1)

            def norm_latents(b):
                dve.wait_ge(S.lat_rnorm, due(n(b)))
                dve.wait_ge(S.turn["latent_t"], due(n(b - 1)))
                for k in range(KT):
                    ins = dve.tensor_scalar(latn[:, k, :], lat[:, k, :], lmv[:, k, 0:1], lrs[:, k:k + 1],
                                            ALU.subtract, ALU.mult)
                ins.then_inc(S.latn, 1)

            def rotary_products(kind, which, b):
                dve.wait_ge(S.turn[kind], due(n(b)))
                dve.wait_ge(S.rot, due(nr(b - 1, which)))
                dve.tensor_tensor(t_cos[:, which, :], misc[:, 0:SEQ], T.cos[:, :], ALU.mult)
                dve.tensor_tensor(t_sin[:, which, :], misc[:, SEQ:2 * SEQ], T.sin[:, :], ALU.mult)\
                    .then_inc(S.taken[kind], 1)

            def place_values(b, buf):
                dve.wait_ge(S.taken["v"], due(n(b)))
                dve.wait_ge(S.ov_full[GRP - 1], due(n(b - 2)))
                dve.tensor_copy(va[buf][:, :, :, 0:MD], vst[:, :, :, :]).then_inc(S.va, 1)

            def norm_heads(b, k):
                kind = f"head_t{k}"
                heads = misc[:, :].rearrange("p (h c) -> p h c", c=MW)
                dve.wait_ge(S.turn[kind], due(n(b)))
                dve.reciprocal(rec[:, k, :], heads[:, :, MD]).then_inc(S.recip[k], 1)
                dve.wait_ge(S.recip[k], due(n(b)))
                dve.wait_ge(S.turn["out_t"], due(n(b - 1)))
                dve.tensor_tensor(on[:, k, :, :], heads[:, :, 0:MD],
                                  rec[:, k, :].unsqueeze(2).to_broadcast([P, MH, MD]), ALU.mult)\
                    .then_inc(S.taken[kind], 1)

            def maxima(b, v):
                dve.wait_ge(S.mx_full[v % MX_BANKS], due(nu(b, v, MX_BANKS)))
                if v == 0:
                    dve.wait_ge(S.turn["max_t"], due(n(b - 1)))
                h, nh, t = UNITS[v]
                dve.tensor_reduce(mx[:, t, h:h + nh], mxp[v % 2][:, :].rearrange("p (h k) -> p h k", h=nh), AX.X, ALU.max,
                                  negate=True).then_inc(S.mx_done[v % MX_BANKS], 1)

            def iteration(i, par):
                for s in range(SLOTS):
                    if s == 0 and ok(i + 3):
                        row_stats(i + 3)
                    if s == 1 and ok(i + 2):
                        latent_stats(i + 2)
                    if s == 2 and ok(i + 2):
                        rotary_products("q", 0, i + 2)
                    if s == 7 and ok(i + 1):
                        place_values(i + 1, 1 - par)
                    if s == 3 and ok(i - 1):
                        norm_heads(i - 1, 0)
                    if s == 3 and ok(i + 2):
                        norm_latents(i + 2)
                    if s == 5 and ok(i + 2):
                        rotary_products("k", 1, i + 2)
                    if s == 6 and ok(i - 1):
                        norm_heads(i - 1, 1)
                    if s == 8 and ok(i + 1):
                        b = i + 1
                        dve.wait_ge(S.mt_hi, due(n(b)))
                        dve.wait_ge(S.maxrow, due(n(b - 1) * MAXROW_DMAS))
                        dve.tensor_tensor(mt_lo[:, :], misc[0:MH, 0:SEQ], mt_hi[:, :].bitcast(F32),
                                          ALU.subtract).then_inc(S.taken["max_t"], 1)
                    if s == 10 and ok(i + 3):
                        norm_rows(i + 3)
                    if s == 11 and ok(i - 1):
                        b = i - 1
                        dve.wait_ge(S.turn["wo"], due(n(b)))
                        at = cols(b * SEQ, SEQ)
                        dve.tensor_tensor(U[:, at], misc[:, 0:SEQ], U[:, at], ALU.add).then_inc(S.taken["wo"], 1)
                    if ok(i + 1):
                        for v in MAX_SLOTS.get(s, ()):
                            maxima(i + 1, v)

            run(dve, iteration)

        @block.tensor
        def _(pe):
            def turn(kind, b, buf):
                if kind == "un_t":
                    pe.wait_ge(S.u, due(n(b)))
                    for k in range(KT):
                        ins = pe.transpose(misc[:, k * P:(k + 1) * P], un[:, k, :], T.ident[:, :])
                elif kind == "latent":
                    pe.wait_ge(S.taken["un_t"], due(n(b)))
                    for k in range(KT):
                        ins = pe.matmul(misc[:, k * LAT:(k + 1) * LAT], unT[:, k * P:(k + 1) * P], T.wdkv[:, :],
                                        start=True, stop=True)
                elif kind == "q":
                    for half, w in enumerate((T.wq, T.wq_swap)):
                        ins = pe.matmul(misc[:, half * SEQ:(half + 1) * SEQ], w[:, :], unT[:, :],
                                        start=True, stop=True)
                elif kind == "latent_t":
                    for k in range(KT):
                        ins = pe.transpose(misc[0:LAT, k * P:(k + 1) * P], latn[:, k, :], T.ident[:, :])
                elif kind == "k":
                    pe.wait_ge(S.taken["latent_t"], due(n(b)))
                    for half, w in enumerate((T.wuk, T.wuk_swap)):
                        ins = pe.matmul(misc[:, half * SEQ:(half + 1) * SEQ], w[:, :], latT[:, :],
                                        start=True, stop=True)
                elif kind == "v":
                    for k in range(KT):
                        ins = pe.matmul(misc[:, k * D:(k + 1) * D], latT[:, k * P:(k + 1) * P], T.wuv[:, :],
                                        start=True, stop=True)
                elif kind in ("head_t0", "head_t1"):
                    k = int(kind[-1])
                    if k == 0:
                        for g in range(GRP):
                            pe.wait_ge(S.ov_taken[g], due(n(b)))
                    for g in range(GRP):
                        ins = pe.transpose(misc[:, g * P:(g + 1) * P], ot[:, buf, g, k * P:(k + 1) * P], T.ident[:, :])
                elif kind == "out_t":
                    pe.wait_ge(S.taken["head_t0"], due(n(b)))
                    pe.wait_ge(S.taken["head_t1"], due(n(b)))
                    for k in range(KT):
                        ins = pe.transpose(misc[:, k * P:(k + 1) * P],
                                           on[:, k, :, :].rearrange("p h d -> p (h d)"), T.ident[:, :])
                elif kind == "wo":
                    pe.wait_ge(S.taken["out_t"], due(n(b)))
                    for k in range(KT):
                        ins = pe.matmul(misc[:, k * D:(k + 1) * D], onT[:, k * P:(k + 1) * P], T.wo[:, :],
                                        start=True, stop=True)
                else:
                    pe.wait_ge(S.mx_done[(SLOTS - 1) % MX_BANKS], due(nu(b, SLOTS - 1, MX_BANKS)))
                    for k in range(KT):
                        ins = pe.transpose(misc[0:MH, k * P:(k + 1) * P], mx[:, k, :], T.ident[:, :])
                return ins

            def transposed_scores(b, s, buf):
                if s == 0:
                    for half in range(2):
                        pe.wait_ge(S.stack[half], due(n(b) * STACK_DMAS))
                    pe.wait_ge(S.maxrow, due(n(b) * MAXROW_DMAS))
                pe.wait_ge(S.exp[s % ST_BANKS], due(nu(b, s, ST_BANKS) - 1))
                g, part = divmod(s, 3)
                heads = [4 * g + 2 * part, 4 * g + 2 * part + 1] if part < 2 else [4 * g + m for m in range(4)]
                t0 = 0 if part < 2 else P
                size = SEQ - t0
                for m, h in enumerate(heads):
                    ins = pe.matmul(st[s % 3][:, m * size:(m + 1) * size],
                                    keys(buf, h, t0, P), queries(buf, h, t0, size),
                                    start=(m == 0), stop=(m == len(heads) - 1), skip_group_check=True)
                ins.then_inc(S.st_full[s % ST_BANKS], 1)

            def plain_scores(b, v, buf):
                h, nh, t = UNITS[v]
                if v % (SLOTS // 2) == 0:
                    pe.wait_ge(S.stack[h // HH], due(n(b) * STACK_DMAS))
                pe.wait_ge(S.mx_done[v % MX_BANKS], due(nu(b, v, MX_BANKS) - 1))
                bank = mxp[v % 2]
                size = (t + 1) * P
                for m in range(nh):
                    pe.matmul(bank[:, m * size:(m + 1) * size], queries(buf, h + m, t * P, P),
                              keys(buf, h + m, 0, size), start=(m == 0), stop=False, skip_group_check=True)
                pe.matmul(bank[:, :].rearrange("p (h k) -> p h k", h=nh)[:, :, size - P:size], T.ident_bf[:, :],
                          T.neg[:, 0:nh, :], start=False, stop=True, skip_group_check=True)\
                    .then_inc(S.mx_full[v % MX_BANKS], 1)

            def value_products(b, g, buf):
                if g == 0:
                    pe.wait_ge(S.va, due(n(b)))
                if g >= 2:
                    pe.wait_ge(S.ov_taken[g - 2], due(n(b)))
                else:
                    pe.wait_ge(S.ov_taken[g + 2], due(n(b - 1)))
                pe.wait_ge(S.masked[g], due(n(b)))
                for kt in range(KT):
                    for m in range(GRP):
                        h = 4 * g + m
                        s = 3 * g + (m // 2 if kt == 0 else 2)
                        size = SEQ - kt * P
                        at = (m % 2 if kt == 0 else m) * size
                        ins = pe.matmul(ov[g % 2][MW * m:MW * (m + 1), kt * P:SEQ], va[buf][:, kt, h, :],
                                        pr[:, s % RING, at:at + size], start=(kt == 0), stop=(kt == KT - 1),
                                        skip_group_check=True)
                ins.then_inc(S.ov_full[g], 1)

            def iteration(i, par):
                for s in range(SLOTS):
                    if ok(i):
                        transposed_scores(i, s, par)
                    if s in LATENT_MISC:
                        kind, off = LATENT_MISC[s]
                        if ok(i + off):
                            prev = before(i, kind)
                            turned = value(pe, n(i + off))
                            free = value(pe, n(prev[1])) if prev else None
                            if kind == "latent_t":
                                pe.wait_ge(T.made, 1)
                            if prev:
                                pe.wait_ge(S.taken[prev[0]], free)
                            if kind == "latent_t":
                                pe.wait_ge(S.latn, turned)
                            turn(kind, i + off, (par + off) % 2).then_inc(S.turn[kind], 1)
                    if ok(i + 1):
                        for v in MAX_SLOTS.get(s, ()):
                            plain_scores(i + 1, v, 1 - par)
                    if s in VALUE_SLOTS:
                        off, g = VALUE_SLOTS[s]
                        if ok(i + off):
                            value_products(i + off, g, (par + off) % 2)

            run(pe, iteration)


CT = 4
CN = CT * P
NC = NT // CT
NQ = NE * HC
HR = 4
LAGQ = 2
PICK = 6
GR = 3 * NE


class MoeSems:

    def __init__(self, sem):
        self.bn = sem("moe_bn")
        self.stats = sem("moe_stats")
        self.sq = sem("moe_sq")
        self.ms = sem("moe_ms")
        self.veps = sem("moe_veps")
        self.rnorm = sem("moe_rnorm")
        self.xn = sem("moe_xn")
        self.xt_ready = sem("moe_xt_ready")
        self.xt = sem("moe_xt")
        self.x_hi = sem("moe_x_hi")
        self.x_lo = sem("moe_x_lo")
        self.lg_ready = sem("moe_lg_ready")
        self.pick = sem("moe_pick")
        self.onehot = sem("moe_onehot")
        self.oht_ready = sem("moe_oht_ready")
        self.oht = sem("moe_oht")
        self.h_full = [sem(f"moe_h_full{n}") for n in range(HR)]
        self.h_hi = [sem(f"moe_h_hi{n}") for n in range(HR)]
        self.h_lo = [sem(f"moe_h_lo{n}") for n in range(HR)]
        self.h_used = [sem(f"moe_h_used{n}") for n in range(HR)]
        self.y_sb = sem("moe_y_sb")
        self.yt_ready = sem("moe_yt_ready")
        self.sum = sem("moe_sum")
        self.x = sem("moe_x")
        self.stored = sem("moe_stored")


def moe_phase(nc, T, S, base, out=None):
    tiles = ExitStack()
    with tiles:
        def sb(name, shape, dt=F32):
            return tiles.enter_context(nc.sbuf_tensor(f"moe{base}_{name}", shape, dt))

        def pb(name):
            return tiles.enter_context(nc.psum_tensor(f"moe{base}_{name}", [P, 512], F32))

        st6 = sb("st6", [P, CT, 6])
        mv = sb("mv", [P, CT, 2])
        msq = sb("msq", [P, 3, CT])
        rs = sb("rs", [P, CT])
        xn = sb("xn", [P, CT, D])
        xT = sb("xT", [D, CN])
        x_hi = [sb(f"x_hi{n}", [D, CN], F32R) for n in range(2)]
        x_lo = [sb(f"x_lo{n}", [D, CN], F32R) for n in range(2)]
        lg = sb("lg", [P, CT, NE])
        top = sb("top", [P, CT])
        eq = sb("eq", [P, CT, NE])
        seen = sb("seen", [P, CT, NE])
        onehot = sb("onehot", [P, CT, 3, NE])
        oht = [sb(f"oht{n}", [GR, CN], BF16) for n in range(2)]
        h_hi = [sb(f"h_hi{n}", [P, CN], F32R) for n in range(HR)]
        h_lo = [sb(f"h_lo{n}", [P, CN], F32R) for n in range(HR)]
        y_sb = sb("y_sb", [D, CN])
        total = sb("total", [P, CN])

        hp = [pb(f"hp{n}") for n in range(HR)]
        yp = [pb(f"yp{n}") for n in range(2)]
        amid = pb("amid")
        yt = pb("yt")
        block = tiles.enter_context(nc.Block(f"moe{base}"))
        X, U = T.X, T.U

        def ok(c):
            return not is_int(c) or 0 <= c < NC

        def n(c):
            return c + (base + 1)

        def m(c, q):
            return (c + base) * (NQ // HR) + (q // HR + 1)

        def run(eng, iteration):
            first = 3 if base == 0 else 1
            for i in range(-1, first):
                iteration(i, i % 2)
            pairs = (NC - 1 - first + 1) // 2
            with eng.Fori(0, pairs) as j:
                iteration(j * 2 + first, 1)
                iteration(j * 2 + (first + 1), 0)
            for i in range(2 * pairs + first, NC + 1):
                iteration(i, i % 2)

        @block.sync
        def _(sp):
            if out is None:
                return
            rows = out.rearrange("(c b) (k p) d -> c p (b k) d", p=P, b=NB // NC)
            for c in range(NC):
                sp.wait_ge(S.x, n(c))
                sp.dma_start(rows[c], X[:, c * CN:(c + 1) * CN].rearrange("p (t d) -> p t d", d=D))\
                    .then_inc(S.stored, 16)
            sp.wait_ge(S.stored, 16 * NC)

        @block.gpsimd
        def _(pool):
            def iteration(i, par):
                if ok(i + 1):
                    c = i + 1
                    pool.wait_ge(S.stats, due(n(c)))
                    pool.wait_ge(S.xn, due(n(c - 1)))
                    pool.tensor_tensor(msq[:, 0, :], mv[:, :, 0], mv[:, :, 0], ALU.mult).then_inc(S.sq, 1)
                    pool.wait_ge(S.sq, due(n(c)))
                    pool.tensor_tensor(msq[:, 1, :], msq[:, 0, :], mv[:, :, 1], ALU.add).then_inc(S.ms, 1)
                    count0 = value(pool, n(c))
                    pool.wait_ge(T.made, 1)
                    pool.wait_ge(S.ms, count0)
                    pool.tensor_scalar(msq[:, 2, :], msq[:, 1, :], EPS6, None, ALU.add).then_inc(S.veps, 1)
                    pool.wait_ge(S.veps, due(n(c)))
                    pool.tensor_tensor(rs[:, :], msq[:, 2, :], T.neghalf[:, :, :].rearrange("p a b -> p (a b)"),
                                       ALU.pow).then_inc(S.rnorm, 1)
                    pool.wait_ge(S.x_hi, due(n(c)))
                    pool.tensor_tensor(x_lo[1 - par][:, :], xT[:, :], x_hi[1 - par][:, :].bitcast(F32),
                                       ALU.subtract).then_inc(S.x_lo, 1)

            run(pool, iteration)

        @block.scalar
        def _(act):
            def iteration(i, par):
                for q in range(NQ):
                    if ok(i):
                        r = q % HR
                        act.wait_ge(S.h_full[r], due(m(i, q)))
                        act.wait_ge(S.h_used[r], due(m(i, q) - 1))
                        act.activation(h_hi[r][:, :], hp[r][:, :], ACT.Relu).then_inc(S.h_hi[r], 1)
                    if q == 2 and ok(i - 1):
                        c = i - 1
                        act.wait_ge(S.h_used[(NQ - 1) % HR], due(m(c, NQ - 1)))
                        act.wait_ge(S.yt_ready, due(n(c - 1)))
                        act.activation(y_sb[:, :], yp[1 - par][:, :], ACT.Copy).then_inc(S.y_sb, 1)
                    if q == 7 and ok(i + 1):
                        c = i + 1
                        act.wait_ge(S.xt, due(n(c)))
                        act.wait_ge(S.h_used[(NQ - 1) % HR], due(m(c - 2, NQ - 1)))
                        act.activation(x_hi[1 - par][:, :], xT[:, :], ACT.Copy).then_inc(S.x_hi, 1)
                    if q == 13 and ok(i + 1):
                        act.wait_ge(S.oht_ready, due(n(i + 1)))
                        act.activation(oht[1 - par][:, :], amid[0:GR, :], ACT.Copy).then_inc(S.oht, 1)

            run(act, iteration)

        @block.vector
        def _(dve):
            def norm_stats(c):
                for k in range(CT):
                    ins = dve.bn_stats(st6[:, k, :], U[:, cols(c * CN + k * D, D)])
                ins.then_inc(S.bn, 1)
                count0 = value(dve, n(c))
                dve.wait_ge(T.made, 1)
                dve.wait_ge(S.bn, count0)
                for k in range(CT):
                    ins = dve.bn_aggr(mv[:, k, :], st6[:, k, :])
                ins.then_inc(S.stats, 1)

            def norm(c):
                dve.wait_ge(S.rnorm, due(n(c)))
                dve.wait_ge(S.xt_ready, due(n(c - 1)))
                for k in range(CT):
                    ins = dve.tensor_scalar(xn[:, k, :], U[:, cols(c * CN + k * D, D)], rs[:, k:k + 1], None,
                                            ALU.mult)
                ins.then_inc(S.xn, 1)

            def weigh(c):
                dve.wait_ge(S.xt_ready, due(n(c)))
                dve.wait_ge(S.lg_ready, due(n(c - 1)))
                dve.wait_ge(S.x_lo, due(n(c - 1)))
                dve.tensor_scalar(xT[:, :], amid[:, :], T.norm2[:, 0:1], None, ALU.mult).then_inc(S.xt, 1)

            def choose(c):
                def step(k):
                    return (c + base) * PICK + k

                dve.wait_ge(S.lg_ready, due(n(c)))
                dve.tensor_tensor(lg[:, :, :], amid[:, 0:CT * NE].rearrange("p (k e) -> p k e", e=NE),
                                  T.gate_b[:, :].unsqueeze(1).to_broadcast([P, CT, NE]), ALU.add)\
                    .then_inc(S.pick, 1)
                dve.wait_ge(S.pick, step(1))
                dve.tensor_reduce(top[:, :], lg[:, :, :], AX.X, ALU.max).then_inc(S.pick, 1)
                dve.wait_ge(S.pick, step(2))
                dve.tensor_tensor(eq[:, :, :], lg[:, :, :], top[:, :].unsqueeze(2).to_broadcast([P, CT, NE]),
                                  ALU.is_equal).then_inc(S.pick, 1)
                dve.wait_ge(S.pick, step(3))
                dve.tensor_copy(seen[:, :, 1], eq[:, :, 0]).then_inc(S.pick, 1)
                for e in (1, 2):
                    dve.wait_ge(S.pick, step(3 + e))
                    dve.tensor_tensor(seen[:, :, e + 1], seen[:, :, e], eq[:, :, e], ALU.max)\
                        .then_inc(S.pick, 1)
                dve.wait_ge(S.pick, step(6))
                dve.wait_ge(S.oht_ready, due(n(c - 1)))
                for part in range(3):
                    ins = dve.tensor_tensor(onehot[:, :, part, :], eq[:, :, :], seen[:, :, :], ALU.is_gt)
                ins.then_inc(S.onehot, 1)

            def finish(c):
                dve.wait_ge(S.yt_ready, due(n(c)))
                at = cols(c * CN, CN)
                dve.tensor_tensor(total[:, :], yt[:, :], U[:, at], ALU.add).then_inc(S.sum, 1)
                dve.wait_ge(S.sum, due(n(c)))
                dve.scalar_tensor_tensor(X[:, at], total[:, :], 0.5, X[:, at], op0=ALU.mult, op1=ALU.add)\
                    .then_inc(S.x, 1)

            def iteration(i, par):
                if is_int(i) and i == -1:
                    dve.memset(seen[:, :, 0], 0.0)
                for q in range(NQ):
                    if ok(i):
                        r = q % HR
                        dve.wait_ge(S.h_hi[r], due(m(i, q)))
                        dve.scalar_tensor_tensor(h_lo[r][:, :], hp[r][:, :], 0.0, h_hi[r][:, :].bitcast(F32),
                                                 op0=ALU.max, op1=ALU.subtract).then_inc(S.h_lo[r], 1)
                    if q == 0 and ok(i + 1):
                        norm_stats(i + 1)
                    if q == 3 and ok(i + 1):
                        norm(i + 1)
                    if q == 4 and ok(i - 1):
                        finish(i - 1)
                    if q == 6 and ok(i + 1):
                        weigh(i + 1)
                    if q == 9 and ok(i + 1):
                        choose(i + 1)

            run(dve, iteration)

        @block.tensor
        def _(pe):
            def block_in(c, q, buf):
                r = q % HR
                if q == 0:
                    pe.wait_ge(S.x_hi, due(n(c)))
                    pe.wait_ge(S.x_lo, due(n(c)))
                    pe.wait_ge(S.oht, due(n(c)))
                pe.wait_ge(S.h_lo[r], due(m(c, q) - 1))
                w = slice(q * P, (q + 1) * P)
                pe.matmul(hp[r][:, :], T.gate_rows[:, w], oht[buf][:, :], start=True, stop=False)
                pe.matmul(hp[r][:, :], T.w1_lo[:, w], x_hi[buf][:, :], start=False, stop=False)
                pe.matmul(hp[r][:, :], T.w1_hi[:, w], x_lo[buf][:, :], start=False, stop=False)
                pe.matmul(hp[r][:, :], T.w1_hi[:, w], x_hi[buf][:, :], start=False, stop=True)\
                    .then_inc(S.h_full[r], 1)

            def block_out(c, q, buf):
                r = q % HR
                if q == 0:
                    pe.wait_ge(S.y_sb, due(n(c - 2)))
                    pe.matmul(yp[buf][:, :], T.b2_rows[:, :], oht[buf][:, :], start=True, stop=False)
                pe.wait_ge(S.h_lo[r], due(m(c, q)))
                w = slice(q * P, (q + 1) * P)
                pe.matmul(yp[buf][:, :], T.w2_lo[:, w], h_hi[r][:, :], start=False, stop=False)
                pe.matmul(yp[buf][:, :], T.w2_hi[:, w], h_lo[r][:, :], start=False, stop=False)
                pe.matmul(yp[buf][:, :], T.w2_hi[:, w], h_hi[r][:, :], start=False, stop=(q == NQ - 1))\
                    .then_inc(S.h_used[r], 1)

            def iteration(i, par):
                for q in range(NQ):
                    if ok(i):
                        block_in(i, q, par)
                    if q >= LAGQ and ok(i):
                        block_out(i, q - LAGQ, par)
                    if q < LAGQ and ok(i - 1):
                        block_out(i - 1, q + NQ - LAGQ, 1 - par)
                    if q == 3 and ok(i - 1):
                        c = i - 1
                        pe.wait_ge(S.y_sb, due(n(c)))
                        pe.wait_ge(S.sum, due(n(c - 1)))
                        for k in range(CT):
                            ins = pe.transpose(yt[:, k * P:(k + 1) * P], y_sb[:, k * P:(k + 1) * P], T.ident[:, :])
                        ins.then_inc(S.yt_ready, 1)
                    if q == 5 and ok(i + 1):
                        c = i + 1
                        pe.wait_ge(S.xn, due(n(c)))
                        pe.wait_ge(S.oht, due(n(c - 1)))
                        for k in range(CT):
                            ins = pe.transpose(amid[:, k * P:(k + 1) * P], xn[:, k, :], T.ident[:, :])
                        ins.then_inc(S.xt_ready, 1)
                    if q == 8 and ok(i + 1):
                        c = i + 1
                        pe.wait_ge(S.xt, due(n(c)))
                        for k in range(CT):
                            ins = pe.matmul(amid[:, k * NE:(k + 1) * NE], xT[:, k * P:(k + 1) * P], T.gate[:, :],
                                            start=True, stop=True)
                        ins.then_inc(S.lg_ready, 1)
                    if q == 12 and ok(i + 1):
                        c = i + 1
                        pe.wait_ge(S.onehot, due(n(c)))
                        for k in range(CT):
                            ins = pe.transpose(amid[0:GR, k * P:(k + 1) * P],
                                               onehot[:, k, :, :].rearrange("p a e -> p (a e)"), T.ident[:, :])
                        ins.then_inc(S.oht_ready, 1)

            run(pe, iteration)


PR4 = 4
PAIRS = AH // 2
PT_LAG = 2
Q_SLOTS = {3: 0, 5: 1, 6: 2, 7: 3}
PAIR_SLOTS = {4: (0, 0), 6: (0, 1), 0: (-1, 2), 2: (-1, 3)}
MULTI_MISC = {0: ("xt", 1), 2: ("kv", 1), 4: ("wo", -1)}
MISC_ORDER = [MULTI_MISC[s] for s in sorted(MULTI_MISC)]


class MqaSems:

    def __init__(self, sem):
        self.bn = sem("mqa_bn")
        self.stats = sem("mqa_stats")
        self.sum_eps = sem("mqa_sum_eps")
        self.veps = sem("mqa_veps")
        self.rnorm = sem("mqa_rnorm")
        self.xn = sem("mqa_xn")
        self.turn = {k: sem(f"mqa_{k}_ready") for k, _ in MISC_ORDER}
        self.taken = {k: sem(f"mqa_{k}_taken") for k, _ in MISC_ORDER}
        self.k_hi = sem("mqa_k_hi")
        self.vals = sem("mqa_vals")
        self.q_ready = sem("mqa_q_ready")
        self.q_hi = sem("mqa_q_hi")
        self.q = sem("mqa_q")
        self.s_full = [sem(f"mqa_s_full{n}") for n in range(2)]
        self.mx = [sem(f"mqa_mx{n}") for n in range(2)]
        self.exp = [sem(f"mqa_exp{n}") for n in range(2)]
        self.pt_full = [sem(f"mqa_pt_full{n}") for n in range(2)]
        self.pt_sb = [sem(f"mqa_pt_sb{n}") for n in range(2)]
        self.ov_full = [sem(f"mqa_ov_full{n}") for n in range(2)]
        self.ov_sb = [sem(f"mqa_ov_sb{n}") for n in range(2)]
        self.rec = [sem(f"mqa_rec{n}") for n in range(2)]
        self.pn = [sem(f"mqa_pn{n}") for n in range(2)]
        self.o_bn = sem("mqa_o_bn")
        self.o_stats = sem("mqa_o_stats")
        self.o_veps = sem("mqa_o_veps")
        self.o_rnorm = sem("mqa_o_rnorm")
        self.o_norm = sem("mqa_o_norm")
        self.o_w = sem("mqa_o_w")
        self.o_b = sem("mqa_o_b")
        self.x = sem("mqa_x")


def mqa_phase(nc, T, S):
    tiles = ExitStack()
    with tiles:
        def sb(name, shape, dt=F32):
            return tiles.enter_context(nc.sbuf_tensor(f"mqa_{name}", shape, dt))

        def pb(name):
            return tiles.enter_context(nc.psum_tensor(f"mqa_{name}", [P, 512], F32))

        st6 = sb("st6", [P, KT, 6])
        mv = sb("mv", [P, KT, 2])
        veps = sb("veps", [P, 2, KT])
        rs = sb("rs", [P, KT])
        xn = sb("xn", [P, KT, D])
        xT = sb("xT", [D, SEQ])
        k_hi = [sb(f"k_hi{n}", [P, SEQ], F32R) for n in range(2)]
        k_lo = [sb(f"k_lo{n}", [P, SEQ], F32R) for n in range(2)]
        vals = [sb(f"vals{n}", [P, KT, AD]) for n in range(2)]
        q_all = [sb(f"q_all{n}", [AD, 2 * SEQ]) for n in range(2)]
        qst = [sb(f"qst{n}", [P, AH * SEQ], F32R) for n in range(2)]
        nmax = sb("nmax", [P, AH, KT])
        sums = sb("sums", [P, AH, KT])
        recs = sb("recs", [P, AH, KT])
        pr = sb("pr", [P, PR4, KT, SEQ])
        pt = sb("pt", [P, PR4, KT, SEQ])
        oT = sb("oT", [P, PAIRS, SEQ])
        o_sb = sb("o_sb", [P, KT, D])
        ost6 = sb("ost6", [P, KT, 6])
        omv = sb("omv", [P, KT, 2])
        oveps = sb("oveps", [P, KT])
        ors = sb("ors", [P, KT])
        o_n = sb("o_n", [P, KT, D])
        o_w = sb("o_w", [P, KT, D])
        o_b = sb("o_b", [P, KT, D])

        sp_ = [pb(f"s{n}") for n in range(2)]
        ptp = pb("ptp")
        ovp = [pb(f"ov{n}") for n in range(2)]
        qp = [pb(f"q{n}") for n in range(2)]
        misc = pb("misc")
        block = tiles.enter_context(nc.Block("mqa"))
        X = T.X

        def ok(b):
            return not is_int(b) or 0 <= b < NB

        def n(b):
            return b + 1

        def nh(b, h):
            return b * (AH // 2) + (h // 2 + 1)

        def nq(b, p):
            return b * PAIRS + (p + 1)

        def np_(b, p):
            return b * (PAIRS // 2) + (p // 2 + 1)

        def before(i, kind):
            here = [(k, i + o) for k, o in MISC_ORDER if ok(i + o)]
            at = [k for k, _ in here].index(kind)
            if at:
                return here[at - 1]
            if is_int(i):
                old = [(k, i - 1 + o) for k, o in MISC_ORDER if ok(i - 1 + o)]
                return old[-1] if old else None
            return MISC_ORDER[-1][0], i + (MISC_ORDER[-1][1] - 1)

        def run(eng, iteration):
            first = 3
            for i in range(-2, first):
                iteration(i, i % 2)
            pairs = (NB - 2 - first) // 2
            with eng.Fori(0, pairs) as j:
                iteration(j * 2 + first, 1)
                iteration(j * 2 + (first + 1), 0)
            for i in range(2 * pairs + first, NB + 2):
                iteration(i, i % 2)

        def take(eng, copy, b, h):
            eng.wait_ge(S.pt_full[h % 2], due(nh(b, h)))
            if h >= PR4:
                eng.wait_ge(S.ov_full[(h - PR4) // 2 % 2], due(np_(b, (h - PR4) // 2)))
            else:
                eng.wait_ge(S.ov_full[(h + AH - PR4) // 2 % 2], due(np_(b - 1, (h + AH - PR4) // 2)))
            copy(pt[:, h % PR4, :, :].rearrange("p t q -> p (t q)"), ptp[:, :]).then_inc(S.pt_sb[h % 2], 1)

        @block.gpsimd
        def _(pool):
            def row_factors(b):
                count0 = value(pool, n(b))
                count1 = value(pool, n(b - 1))
                pool.wait_ge(T.made, 1)
                pool.wait_ge(S.stats, count0)
                pool.wait_ge(S.xn, count1)
                pool.tensor_scalar(veps[:, 0, :], mv[:, :, 1], EPS5, EPS5 * EPS5, ALU.mult, ALU.add)\
                    .then_inc(S.sum_eps, 1)
                pool.wait_ge(S.sum_eps, due(n(b)))
                pool.tensor_tensor(veps[:, 1, :], veps[:, 0, :], mv[:, :, 1], ALU.add).then_inc(S.veps, 1)
                pool.wait_ge(S.veps, due(n(b)))
                pool.tensor_tensor(rs[:, :], veps[:, 1, :], T.neghalf[:, 0, 0:KT], ALU.pow).then_inc(S.rnorm, 1)

            def out_factors(b):
                count0 = value(pool, n(b))
                pool.wait_ge(T.made, 1)
                pool.wait_ge(S.o_stats, count0)
                pool.tensor_scalar(oveps[:, :], omv[:, :, 1], EPS5, None, ALU.add).then_inc(S.o_veps, 1)
                pool.wait_ge(S.o_veps, due(n(b)))
                pool.tensor_tensor(ors[:, :], oveps[:, :], T.neghalf[:, 0, 0:KT], ALU.pow).then_inc(S.o_rnorm, 1)

            def finish(b):
                pool.wait_ge(S.o_norm, due(n(b)))
                row = lambda t: t[:, :].unsqueeze(1).to_broadcast([P, KT, D])
                pool.tensor_tensor(o_w[:, :, :], o_n[:, :, :], row(T.out_w), ALU.mult).then_inc(S.o_w, 1)
                pool.wait_ge(S.o_w, due(n(b)))
                pool.tensor_tensor(o_b[:, :, :], o_w[:, :, :], row(T.out_b), ALU.add).then_inc(S.o_b, 1)
                pool.wait_ge(S.o_b, due(n(b)))
                at = cols(b * SEQ, SEQ)
                pool.tensor_tensor(X[:, at], X[:, at], o_b[:, :, :].rearrange("p k d -> p (k d)"), ALU.add)\
                    .then_inc(S.x, 1)

            def lower_queries(b, p, buf):
                pool.wait_ge(S.q_hi, due(nq(b, p)))
                low = qst[buf][0:AD, 2 * p * SEQ:(2 * p + 2) * SEQ]
                pool.tensor_tensor(low, q_all[p % 2][:, :], low.bitcast(F32), ALU.subtract).then_inc(S.q, 1)

            def iteration(i, par):
                for s in range(AH):
                    if s == 0 and ok(i):
                        lower_queries(i, PAIRS - 1, par)
                    if s - 1 in Q_SLOTS and ok(i + 1):
                        lower_queries(i + 1, Q_SLOTS[s - 1], 1 - par)
                    if s == 4 and ok(i + 2):
                        row_factors(i + 2)
                    if s == 6 and ok(i - 1):
                        out_factors(i - 1)
                    if s == 1 and ok(i - 2):
                        finish(i - 2)

            run(pool, iteration)

        @block.scalar
        def _(act):
            def exponentials(b, h):
                s = h % 2
                act.wait_ge(S.mx[s], due(nh(b, h)))
                if h >= PR4:
                    act.wait_ge(S.pt_full[s], due(nh(b, h - PR4)))
                else:
                    act.wait_ge(S.pt_full[s], due(nh(b - 1, h + AH - PR4)))
                for t in range(KT):
                    ins = act.activation(pr[:, h % PR4, t, :], sp_[s][:, t * SEQ:(t + 1) * SEQ], ACT.Exp,
                                         bias=nmax[:, h, t:t + 1], accum_out=sums[:, h, t:t + 1])
                ins.then_inc(S.exp[s], 1)

            def take_transposes(b, h):
                take(act, lambda dst, src: act.activation(dst, src, ACT.Copy), b, h)

            def upper_queries(b, p, buf):
                act.wait_ge(S.q_ready, due(nq(b, p)))
                act.wait_ge(S.s_full[1], due(nh(b - 2, 2 * p + 1)))
                act.activation(qst[buf][:, 2 * p * SEQ:(2 * p + 2) * SEQ], qp[p % 2][:, :], ACT.Copy)
                act.wait_ge(S.q, due(nq(b, p) - 2))
                act.activation(q_all[p % 2][:, :], qp[p % 2][0:AD, :], ACT.Copy).then_inc(S.q_hi, 1)

            def take_pair(b, p):
                act.wait_ge(S.ov_full[p % 2], due(np_(b, p)))
                act.wait_ge(S.turn["wo"], due(n(b - 1)))
                act.activation(oT[:, p, :], ovp[p % 2][:, 0:SEQ], ACT.Copy).then_inc(S.ov_sb[p % 2], 1)

            def iteration(i, par):
                for s in range(AH):
                    if s == 0 and ok(i):
                        upper_queries(i, PAIRS - 1, par)
                    if s - 1 in Q_SLOTS and ok(i + 1):
                        upper_queries(i + 1, Q_SLOTS[s - 1], 1 - par)
                    h = s - PT_LAG
                    if h % 2 == 1:
                        if h >= 0 and ok(i):
                            take_transposes(i, h)
                        if h < 0 and ok(i - 1):
                            take_transposes(i - 1, h + AH)
                    if ok(i):
                        exponentials(i, s)
                    if s == 0 and ok(i + 1):
                        b = i + 1
                        act.wait_ge(S.turn["xt"], due(n(b)))
                        act.wait_ge(S.q_ready, due(nq(b - 1, PAIRS - 1)))
                        act.activation(xT[:, :], misc[:, 0:SEQ], ACT.Identity, scale=T.norm_w[:, 0:1],
                                       bias=T.norm_b[:, 0:1]).then_inc(S.taken["xt"], 1)
                    if s == 2 and ok(i + 1):
                        b, buf = i + 1, 1 - par
                        act.wait_ge(S.turn["kv"], due(n(b)))
                        act.wait_ge(S.s_full[1], due(nh(b - 2, AH - 1)))
                        act.wait_ge(S.ov_full[1], due(np_(b - 2, PAIRS - 1)))
                        act.activation(k_hi[buf][:, :], misc[:, 0:SEQ], ACT.Copy, scale=ASCALE)\
                            .then_inc(S.k_hi, 1)
                        act.activation(vals[buf][:, :, :].rearrange("p k d -> p (k d)"),
                                       misc[:, SEQ:SEQ + KT * AD], ACT.Copy).then_inc(S.vals, 1)
                    if s in PAIR_SLOTS:
                        off, p = PAIR_SLOTS[s]
                        if ok(i + off):
                            take_pair(i + off, p)

            run(act, iteration)

        @block.vector
        def _(dve):
            def row_stats(b):
                for k in range(KT):
                    ins = dve.bn_stats(st6[:, k, :], X[:, cols(b * SEQ + k * D, D)])
                ins.then_inc(S.bn, 1)
                count0 = value(dve, n(b))
                dve.wait_ge(T.made, 1)
                dve.wait_ge(S.bn, count0)
                for k in range(KT):
                    ins = dve.bn_aggr(mv[:, k, :], st6[:, k, :])
                ins.then_inc(S.stats, 1)

            def norm_rows(b):
                dve.wait_ge(S.rnorm, due(n(b)))
                dve.wait_ge(S.turn["xt"], due(n(b - 1)))
                for k in range(KT):
                    ins = dve.tensor_scalar(xn[:, k, :], X[:, cols(b * SEQ + k * D, D)], mv[:, k, 0:1],
                                            rs[:, k:k + 1], ALU.subtract, ALU.mult)
                ins.then_inc(S.xn, 1)

            def maximum(b, h):
                s = h % 2
                dve.wait_ge(S.s_full[s], due(nh(b, h)))
                dve.wait_ge(S.exp[s], due(nh(b, h) - (AH // 2)))
                dve.tensor_reduce(nmax[:, h, :], sp_[s][:, :].rearrange("p (t k) -> p t k", t=KT), AX.X, ALU.max,
                                  negate=True).then_inc(S.mx[s], 1)

            def probabilities(b, h):
                s = h % 2
                dve.wait_ge(S.exp[s], due(nh(b, h)))
                dve.reciprocal(recs[:, h, :], sums[:, h, :]).then_inc(S.rec[s], 1)
                dve.wait_ge(S.rec[s], due(nh(b, h)))
                for t in range(KT):
                    ins = dve.tensor_scalar(pr[:, h % PR4, t, :], pr[:, h % PR4, t, :], recs[:, h, t:t + 1], None,
                                            ALU.mult)
                ins.then_inc(S.pn[s], 1)

            def out_rows(b):
                dve.wait_ge(S.turn["wo"], due(n(b)))
                dve.tensor_copy(o_sb[:, :, :].rearrange("p k d -> p (k d)"), misc[:, 0:KT * D])\
                    .then_inc(S.taken["wo"], 1)
                dve.wait_ge(S.taken["wo"], due(n(b)))
                for k in range(KT):
                    ins = dve.bn_stats(ost6[:, k, :], o_sb[:, k, :])
                ins.then_inc(S.o_bn, 1)
                count0 = value(dve, n(b))
                dve.wait_ge(T.made, 1)
                dve.wait_ge(S.o_bn, count0)
                for k in range(KT):
                    ins = dve.bn_aggr(omv[:, k, :], ost6[:, k, :])
                ins.then_inc(S.o_stats, 1)

            def out_norm(b):
                dve.wait_ge(S.o_rnorm, due(n(b)))
                dve.wait_ge(S.o_w, due(n(b - 1)))
                for k in range(KT):
                    ins = dve.tensor_scalar(o_n[:, k, :], o_sb[:, k, :], omv[:, k, 0:1], ors[:, k:k + 1],
                                            ALU.subtract, ALU.mult)
                ins.then_inc(S.o_norm, 1)

            def iteration(i, par):
                for s in range(AH):
                    if ok(i):
                        maximum(i, s)
                    if s == 3 and ok(i + 1):
                        b, buf = i + 1, 1 - par
                        dve.wait_ge(S.k_hi, due(n(b)))
                        dve.wait_ge(S.vals, due(n(b)))
                        dve.scalar_tensor_tensor(k_lo[buf][:, :], misc[:, 0:SEQ], ASCALE,
                                                 k_hi[buf][:, :].bitcast(F32), op0=ALU.mult, op1=ALU.subtract)\
                            .then_inc(S.taken["kv"], 1)
                    if s and ok(i):
                        probabilities(i, s - 1)
                    if s == 0 and ok(i - 1):
                        probabilities(i - 1, AH - 1)
                    h = s - PT_LAG
                    if h % 2 == 0:
                        if h >= 0 and ok(i):
                            take(dve, dve.tensor_copy, i, h)
                        if h < 0 and ok(i - 1):
                            take(dve, dve.tensor_copy, i - 1, h + AH)
                    if s == 5 and ok(i - 1):
                        out_rows(i - 1)
                    if s == 7 and ok(i - 1):
                        out_norm(i - 1)
                    if s == 3 and ok(i + 2):
                        row_stats(i + 2)
                    if s == 6 and ok(i + 2):
                        norm_rows(i + 2)

            run(dve, iteration)

        @block.tensor
        def _(pe):
            def scores(b, h, buf):
                s = h % 2
                pe.wait_ge(S.q, due(nq(b, h // 2)))
                if h == 0:
                    pe.wait_ge(S.taken["kv"], due(n(b)))
                pe.wait_ge(S.exp[s], due(nh(b, h) - 1))
                for t in range(KT):
                    q = qst[buf][:, h * SEQ + t * P:h * SEQ + (t + 1) * P]
                    out = sp_[s][:, t * SEQ:(t + 1) * SEQ]
                    pe.matmul(out, q, k_lo[buf][:, :], start=(t == 0), stop=False, skip_group_check=True)
                    ins = pe.matmul(out, q, k_hi[buf][:, :], start=False, stop=(t == KT - 1),
                                    skip_group_check=True)
                ins.then_inc(S.s_full[s], 1)

            def transposes(b, h):
                s = h % 2
                pe.wait_ge(S.pn[s], due(nh(b, h)))
                pe.wait_ge(S.pt_sb[1 - s], due(nh(b, h - 1) if h else nh(b - 1, AH - 1)))
                for kt in range(KT):
                    for t in range(KT):
                        at = kt * SEQ + t * P
                        ins = pe.transpose(ptp[:, at:at + P], pr[:, h % PR4, t, kt * P:(kt + 1) * P],
                                           T.ident[:, :])
                ins.then_inc(S.pt_full[s], 1)

            def value_products(b, p, buf):
                for s in range(2):
                    pe.wait_ge(S.pt_sb[s], due(nh(b, 2 * p + s)))
                pe.wait_ge(S.ov_sb[p % 2], due(np_(b, p) - 1))
                for kt in range(KT):
                    for m in range(2):
                        ins = pe.matmul(ovp[p % 2][AD * m:AD * (m + 1), 0:SEQ], vals[buf][:, kt, :],
                                        pt[:, (2 * p + m) % PR4, kt, :], start=(kt == 0), stop=(kt == KT - 1),
                                        skip_group_check=True)
                ins.then_inc(S.ov_full[p % 2], 1)

            def turn(kind, b):
                if kind == "xt":
                    pe.wait_ge(S.xn, due(n(b)))
                    for k in range(KT):
                        ins = pe.transpose(misc[:, k * P:(k + 1) * P], xn[:, k, :], T.ident[:, :])
                elif kind == "kv":
                    pe.matmul(misc[:, 0:SEQ], T.awk[:, :], xT[:, :], start=True, stop=True)
                    for k in range(KT):
                        ins = pe.matmul(misc[:, SEQ + k * AD:SEQ + (k + 1) * AD], xT[:, k * P:(k + 1) * P],
                                        T.awv[:, :], start=True, stop=True)
                else:
                    for r in range(2):
                        pe.wait_ge(S.ov_sb[r], due(np_(b, PAIRS - 2 + r)))
                    for k in range(KT):
                        for p in range(PAIRS):
                            ins = pe.matmul(misc[:, k * D:(k + 1) * D], oT[:, p, k * P:(k + 1) * P],
                                            T.awo[:, p * D:(p + 1) * D], start=(p == 0), stop=(p == PAIRS - 1))
                return ins

            def iteration(i, par):
                for s in range(AH):
                    if ok(i):
                        scores(i, s, par)
                    if s in MULTI_MISC:
                        kind, off = MULTI_MISC[s]
                        if ok(i + off):
                            prev = before(i, kind)
                            if prev:
                                pe.wait_ge(S.taken[prev[0]], due(n(prev[1])))
                            turn(kind, i + off).then_inc(S.turn[kind], 1)
                    if s in Q_SLOTS and ok(i + 1):
                        b, p = i + 1, Q_SLOTS[s]
                        pe.wait_ge(S.taken["xt"], due(n(b)))
                        pe.wait_ge(S.q_hi, due(nq(b, p) - 2))
                        for m in range(2):
                            h2 = 2 * p + m
                            ins = pe.matmul(qp[p % 2][:, m * SEQ:(m + 1) * SEQ], T.awq[:, h2 * P:(h2 + 1) * P],
                                            xT[:, :], start=True, stop=True)
                        ins.then_inc(S.q_ready, 1)
                    h = s - PT_LAG
                    if h >= 0 and ok(i):
                        transposes(i, h)
                    if h < 0 and ok(i - 1):
                        transposes(i - 1, h + AH)
                    if s in PAIR_SLOTS:
                        off, p = PAIR_SLOTS[s]
                        if ok(i + off):
                            value_products(i + off, p, (par + off) % 2)

            run(pe, iteration)


def rotary_tables():
    half = MD // 2
    inv_freq = (np.float32(1.0) / np.float32(10000.0) ** (np.arange(half, dtype=np.float32) / np.float32(half)))
    angle = np.arange(SEQ, dtype=np.float32)[:, None] * inv_freq[None, :].astype(np.float32)
    cos, sin = np.cos(angle).T, np.sin(angle).T
    cos8 = np.concatenate([cos, cos])
    sin8 = np.concatenate([-sin, sin])
    rows = lambda a: np.ascontiguousarray(np.tile(np.repeat(a, HH, axis=0), (2, 1)), dtype=np.float32)
    return rows(cos8), rows(sin8)


def by_dim(w, swap=False):
    w = w.reshape(MH, MD, w.shape[1])
    if swap:
        w = np.concatenate([w[:, MD // 2:], w[:, :MD // 2]], axis=1)
    w = w.reshape(2, HH, MD, w.shape[2])
    return np.ascontiguousarray(w.transpose(3, 0, 2, 1).reshape(w.shape[3], MH * MD))


def gate_rows_select():
    out = np.zeros((GR, 2 + 2 * NE), np.float32)
    for part in range(3):
        for e in range(NE):
            row = out[part * NE + e]
            row[0] = -1.0 if part > 0 else 0.0
            row[1] = -1.0 if part > 1 else 0.0
            row[2 + e] = 1.0
            if part == 0:
                row[2 + NE:] = -BIG
                row[2 + NE + e] = 0.0
    return out


def laid_out(v):
    v = {k: np.asarray(a) for k, a in v.items()}
    cos, sin = rotary_tables()
    col = lambda a: np.ascontiguousarray(a.reshape(-1, 1))
    return {
        "x": v["L0_attn_x"],
        "wq": by_dim(v["L0_ffn_Wq"]), "wq_swap": by_dim(v["L0_ffn_Wq"], True),
        "wuk": by_dim(v["L0_ffn_Wuk"]), "wuk_swap": by_dim(v["L0_ffn_Wuk"], True),
        "wuv": np.ascontiguousarray(v["L0_ffn_Wuv"].T), "wo": np.ascontiguousarray(v["L0_ffn_Wo"].T),
        "wdkv": np.ascontiguousarray(v["L0_ffn_Wdkv"].T), "cos": cos, "sin": sin,
        "norm2": col(v["L0_ffn_norm2_w"]), "gate": np.ascontiguousarray(v["L0_ffn_gate_w"].T),
        "gate_b": v["L0_ffn_gate_b"].reshape(1, NE), "gate_sel": gate_rows_select(),
        "b1": v["L0_ffn_b1"], "b2": v["L0_ffn_b2"],
        "w1": np.ascontiguousarray(v["L0_ffn_W1"].transpose(2, 0, 1).reshape(D, NE * HID)),
        "w2": np.ascontiguousarray(v["L0_ffn_W2"].reshape(NE, D, HC, P).transpose(3, 0, 2, 1).reshape(P, NE * HC * D)),
        "awq": np.ascontiguousarray(np.repeat(v["L0_attn_Wq"].reshape(D, AH, 1, AD), 2, axis=2).reshape(D, AH * P)),
        "awk": np.ascontiguousarray(np.concatenate([v["L0_attn_Wkv"][:, :AD]] * 2, axis=1)),
        "awv": np.ascontiguousarray(v["L0_attn_Wkv"][:, AD:]),
        "awo": np.ascontiguousarray(v["L0_attn_Wo"].reshape(PAIRS, P, D).transpose(1, 0, 2).reshape(P, PAIRS * D)),
        "norm_w": col(v["L0_attn_norm_w"]), "norm_b": col(v["L0_attn_norm_b"]),
        "out_w": v["L0_attn_out_norm_w"].reshape(1, D), "out_b": v["L0_attn_out_norm_b"].reshape(1, D),
        "norm1": col(v["L0_ffn_norm1_w"]), "ln_g": col(v["L0_ffn_ln_g"]), "ln_b": col(v["L0_ffn_ln_b"]),
    }


def build(nc, A, out):
    ctx = ExitStack()
    with ctx:
        def sb(name, shape, dt=F32):
            return ctx.enter_context(nc.sbuf_tensor(name, shape, dt))

        def sem(name):
            return ctx.enter_context(nc.semaphore(name))

        T = Tiles()
        T.made = sem("made")
        T.X = sb("X", [P, NT * D])
        T.U = sb("U", [P, NT * D])
        T.wq, T.wq_swap = sb("wq", [D, P]), sb("wq_swap", [D, P])
        T.wuk, T.wuk_swap = sb("wuk", [LAT, P]), sb("wuk_swap", [LAT, P])
        T.wuv, T.wo, T.wdkv = sb("wuv", [LAT, D]), sb("wo", [D, D]), sb("wdkv", [D, LAT])
        T.cos, T.sin = sb("cos", [P, SEQ]), sb("sin", [P, SEQ])
        T.norm1, T.ln_g, T.ln_b = sb("norm1", [D, 1]), sb("ln_g", [LAT, 1]), sb("ln_b", [LAT, 1])
        T.stack = [sb(f"stack{n}", [P, MH * 2 * SEQ], F32R) for n in range(2)]
        T.va = [sb(f"va{n}", [P, KT, MH, MW]) for n in range(2)]
        T.norm2, T.gate, T.gate_b = sb("norm2", [D, 1]), sb("gate", [D, NE]), sb("gate_b", [P, NE])
        T.w1_hi, T.w1_lo = sb("w1_hi", [D, NQ * P], F32R), sb("w1_lo", [D, NQ * P], F32R)
        T.w2_hi, T.w2_lo = sb("w2_hi", [P, NQ * D], F32R), sb("w2_lo", [P, NQ * D], F32R)
        T.gate_rows, T.b2_rows = sb("gate_rows", [GR, NQ * P], BF16), sb("b2_rows", [GR, D], BF16)
        T.awq, T.awk, T.awv = sb("awq", [D, AH * P]), sb("awk", [D, P]), sb("awv", [D, AD])
        T.awo = sb("awo", [P, PAIRS * D])
        T.norm_w, T.norm_b = sb("norm_w", [D, 1]), sb("norm_b", [D, 1])
        T.out_w, T.out_b = sb("out_w", [P, D]), sb("out_b", [P, D])
        T.neghalf = sb("neghalf", [P, 2, KT])
        T.ident, T.ident_bf = sb("ident", [P, P]), sb("ident_bf", [P, P], BF16)
        T.neg = sb("neg", [P, 4, P], BF16)

        mla, moe, mqa = MlaSems(sem), MoeSems(sem), MqaSems(sem)
        setup_phase(nc, T, A, sem)
        mla_phase(nc, T, mla, 0)
        moe_phase(nc, T, moe, 0)
        mqa_phase(nc, T, mqa)
        mla_phase(nc, T, mla, NB)
        moe_phase(nc, T, moe, NC, out)


def kernel(**inputs):
    import concourse.bacc as bacc
    from concourse.bass_utils import run_bass_kernel_spmd

    arrays = laid_out(inputs)
    nc = bacc.Bacc("TRN2", target_bir_lowering=False, num_devices=1)
    dram = {name: nc.dram_tensor(f"in_{name}", a.shape, mybir.dt.from_np(a.dtype), kind="ExternalInput").ap()
            for name, a in arrays.items()}
    out = nc.dram_tensor("out", (NB, SEQ, D), F32, kind="ExternalOutput").ap()
    build(nc, dram, out)
    result = run_bass_kernel_spmd(nc, [{f"in_{name}": a for name, a in arrays.items()}], core_ids=[0])
    return result.results[0]["out"]
```

```python
from contextlib import ExitStack

import concourse.bass as bass
import numpy as np
from concourse import mybir

F32 = mybir.dt.float32
F32R = mybir.dt.float32r
BF16 = mybir.dt.bfloat16
ALU = mybir.AluOpType
ACT = mybir.ActivationFunctionType
AX = mybir.AxisListType

P = 128
NB, SEQ, D = 16, 256, 128
NT = NB * SEQ // P
KT = SEQ // P
MH, MD = 16, 8
MW = 32
HH = MH // 2
LAT = 64
NE, HID = 4, 512
HC = HID // P
AH, AD = 8, 64
PAIRS = AH // 2
EPS5, EPS6 = 1e-5, 1e-6
BIG = 1e30
GRP = 4
MSCALE = float(MD) ** -0.5
ASCALE = float(AD) ** -0.5


def is_int(v):
    return isinstance(v, int)


def due(count):
    return max(count, 0) if is_int(count) else count


def value(eng, count):
    return due(count) if is_int(count) else eng.to_reg(count)


def cols(start, size):
    return slice(start, start + size) if is_int(start) else bass.ds(start, size)


def words(view):
    return view.bitcast(F32)


LATENT_WEIGHTS = {"wdkv": LAT, "wq": P, "wq_swap": P, "wo": D, "cos": SEQ, "sin": SEQ, "norm1": 1}
LATENT_ROWS = {"wuk": P, "wuk_swap": P, "wuv": D, "ln_g": 1, "ln_b": 1}
WEIGHTS = {"norm2": 1, "b1": NE * HID // P, "b2": NE, "gate": NE, "awq": AH * P, "awk": P, "awv": AD,
           "awo": PAIRS * D, "norm_w": 1, "norm_b": 1}
SPREAD = {"gate_b": NE, "out_w": D, "out_b": D}
SPREAD_W = sum(SPREAD.values())


class Tiles:
    pass


X_FIRST = 4
SLICES = 4


class LoadSems:

    def __init__(self, sem):
        self.first = sem("load_first")
        self.x = sem("load_x")
        self.w1 = sem("load_w1")
        self.w2 = sem("load_w2")
        self.rest = sem("load_rest")
        self.upper = sem("weights_upper")
        self.zeroed = sem("setup_zeroed")


def setup_phase(nc, T, A, L):
    def mark_stack(eng, buf):
        halves = T.stack[buf][:, :].bitcast(F32).rearrange("p (h k t) -> p h k t", h=MH, k=2)
        eng.memset(halves[:, :, 0, :], 0.0)
        eng.memset(halves[:, :, 1, :], 1.0)

    tokens = A["x"].rearrange("b (k p) d -> p (b k) d", p=P)
    X = T.X[:, :].rearrange("p (t d) -> p t d", d=D)
    cut = X_FIRST * KT

    with nc.Block("setup") as block:
        @block.sync
        def _(sp):
            sp.dma_start(X[:, 0:cut, :], tokens[:, 0:cut, :]).then_inc(L.first, 16)
            sp.dma_start(T.latent_weights[:, :], A["latent_weights"]).then_inc(L.first, 16)
            sp.dma_start(T.latent_rows[:, :], A["latent_rows"]).then_inc(L.first, 16)
            sp.dma_start(X[:, cut:NT, :], tokens[:, cut:NT, :]).then_inc(L.x, 16)
            sp.dma_start(T.w1_raw[:, :], A["w1"]).then_inc(L.w1, 16)
            sp.dma_start(T.weights[:, :], A["weights"]).then_inc(L.rest, 16)
            sp.dma_start(T.spread[:, :], A["spread"].to_broadcast([P, SPREAD_W])).then_inc(L.rest, 16)
            sp.wait_ge(L.first, 3 * 16)

        @block.gpsimd
        def _(pool):
            pool.memset(T.neghalf[:, :, :], -0.5)
            pool.memset(T.ident[:, :], 0.0)
            pool.memset(T.ident_bf[:, :], 0.0)
            pool.memset(T.neg[:, :, :], 0.0).then_inc(L.zeroed, 1)
            pool.wait_ge(L.zeroed, 1)
            for m in (T.ident, T.ident_bf):
                pool.affine_select(out=m[:, :], in_=m[:, :], compare_op=ALU.not_equal, fill=1.0, base=0,
                                   pattern=[[-1, P]], channel_multiplier=1)
            pool.affine_select(out=T.neg[:, :, :], in_=T.neg[:, :, :], compare_op=ALU.is_ge, fill=-BIG, base=0,
                               pattern=[[0, 4], [-1, P]], channel_multiplier=1).then_inc(T.made, 1)
            mark_stack(pool, 1)

        @block.vector
        def _(dve):
            mark_stack(dve, 0)
            for buf in range(2):
                dve.memset(T.va[buf][:, :, :, :], 1.0)


def upper_slice(act, T, L, w, k):
    raw, hi = (T.w1_raw, T.w2_raw)[w], (T.w1_hi, T.w2_hi)[w]
    at = slice(k * NQ * P // SLICES, (k + 1) * NQ * P // SLICES)
    act.wait_ge((L.w1, L.w2)[w], 16)
    act.activation(hi[:, at], raw[:, at], ACT.Copy).then_inc(L.upper, 1)


def lower_slice(dve, T, L, w, k):
    raw, hi, lo = (T.w1_raw, T.w2_raw)[w], (T.w1_hi, T.w2_hi)[w], (T.w1_lo, T.w2_lo)[w]
    at = slice(k * NQ * P // SLICES, (k + 1) * NQ * P // SLICES)
    dve.wait_ge(L.upper, w * SLICES + k + 1)
    dve.tensor_tensor(lo[:, at], raw[:, at], hi[:, at].bitcast(F32), ALU.subtract)


LATENT_MISC = {0: ("un_t", 2), 1: ("latent", 2), 2: ("q", 2), 3: ("head_t0", -1), 4: ("latent_t", 2), 5: ("k", 2),
              6: ("head_t1", -1), 7: ("out_t", -1), 8: ("max_t", 1), 9: ("v", 2), 11: ("wo", -1)}
MISC_TURNS = [LATENT_MISC[s] for s in sorted(LATENT_MISC)]
UNITS = [unit for half in range(2) for unit in
         [(half * HH + 4 * m, 4, 0) for m in range(2)] + [(half * HH + 2 * m, 2, 1) for m in range(4)]]
MAX_SLOTS = {0: (0, 1), 1: (2,), 2: (3,), 3: (4, 5), 4: (6, 7), 5: (8, 9), 6: (10,), 7: (11,)}
VALUE_SLOTS = {2: (-1, 3), 4: (0, 0), 8: (0, 1), 11: (0, 2)}
SLOTS = 12
MX_BANKS, ST_BANKS = 2, 3
RING = 6
STACK_DMAS = 5 * 16
MAXROW_DMAS = 2 * 16


class MlaSems:

    def __init__(self, sem):
        self.bn = sem("mla_bn")
        self.stats = sem("mla_stats")
        self.veps = sem("mla_veps")
        self.rnorm = sem("mla_rnorm")
        self.u = sem("mla_u")
        self.turn = {k: sem(f"mla_{k}_ready") for k, _ in MISC_TURNS}
        self.taken = {k: sem(f"mla_{k}_taken") for k, _ in MISC_TURNS}
        self.lat_bn = sem("mla_lat_bn")
        self.lat_stats = sem("mla_lat_stats")
        self.lat_veps = sem("mla_lat_veps")
        self.lat_rnorm = sem("mla_lat_rnorm")
        self.latn = sem("mla_latn")
        self.rot = sem("mla_rot")
        self.hi = sem("mla_hi")
        self.lo = sem("mla_lo")
        self.va = sem("mla_va")
        self.stack = [sem(f"mla_stack{n}") for n in range(2)]
        self.maxrow = sem("mla_maxrow")
        self.mt_hi = sem("mla_mt_hi")
        self.mx_full = [sem(f"mla_mx_full{v}") for v in range(MX_BANKS)]
        self.mx_done = [sem(f"mla_mx_done{v}") for v in range(MX_BANKS)]
        self.st_full = [sem(f"mla_st_full{s}") for s in range(ST_BANKS)]
        self.exp = [sem(f"mla_exp{s}") for s in range(ST_BANKS)]
        self.masked = [sem(f"mla_masked{g}") for g in range(GRP)]
        self.ov_full = [sem(f"mla_ov_full{g}") for g in range(GRP)]
        self.ov_taken = [sem(f"mla_ov_taken{g}") for g in range(GRP)]
        self.recip = [sem(f"mla_recip{k}") for k in range(KT)]


def mla_phase(nc, T, S, base, L=None, A=None):
    tiles = ExitStack()
    with tiles:
        def sb(name, shape, dt=F32):
            return tiles.enter_context(nc.sbuf_tensor(f"mla{base}_{name}", shape, dt))

        def pb(name):
            return tiles.enter_context(nc.psum_tensor(f"mla{base}_{name}", [P, 512], F32))

        st6 = sb("st6", [P, KT, 6])
        mv = sb("mv", [P, KT, 2])
        veps = sb("veps", [P, 2, KT])
        rs = sb("rs", [P, 2, KT])
        un = sb("un", [P, KT, D])
        unT = sb("unT", [D, SEQ])
        lat = sb("lat", [P, KT, LAT])
        lst6 = sb("lst6", [P, KT, 6])
        lmv = sb("lmv", [P, KT, 2])
        lveps = sb("lveps", [P, KT])
        lrs = sb("lrs", [P, KT])
        latn = sb("latn", [P, KT, LAT])
        latT = sb("latT", [LAT, SEQ])
        t_cos = sb("t_cos", [P, 2, SEQ])
        t_sin = sb("t_sin", [P, 2, SEQ])
        rot = sb("rot", [P, 2, SEQ])
        parts = sb("parts", [P, 4, SEQ], F32R)
        hi, lo = parts[:, 0:3:2, :], parts[:, 1:4:2, :]
        vst = sb("vst", [P, KT, MH, MD])
        mx = sb("mx", [P, KT, MH])
        mt_hi = sb("mt_hi", [MH, SEQ], F32R)
        mt_lo = sb("mt_lo", [MH, SEQ], F32R)
        pr = sb("pr", [P, RING, 512])
        ot = sb("ot", [P, 2, GRP, SEQ])
        rec = sb("rec", [P, KT, MH])
        on = sb("on", [P, KT, MH, MD])
        onT = sb("onT", [D, SEQ])
        if L:
            T.w2_raw = sb("w2_raw", [P, NQ * D])
        va = T.va

        st = [pb(f"st{n}") for n in range(3)]
        mxp = [pb(f"mxp{n}") for n in range(2)]
        ov = [pb(f"ov{n}") for n in range(2)]
        misc = pb("misc")
        block = tiles.enter_context(nc.Block(f"mla{base}"))
        X, U = T.X, T.U

        def queries(buf, h, first=0, size=SEQ):
            return T.stack[buf][:, h * 2 * SEQ + first:h * 2 * SEQ + first + size]

        def keys(buf, h, first=0, size=SEQ):
            return T.stack[buf][:, (h * 2 + 1) * SEQ + first:(h * 2 + 1) * SEQ + first + size]

        def query_rows(buf, row, rows, h, heads):
            return words(T.stack[buf][row:row + rows, :].rearrange("p (h c) -> p h c", h=MH)[:, h:h + heads, 0:SEQ])

        def ok(b):
            return not is_int(b) or 0 <= b < NB

        def n(b):
            return b + (base + 1)

        def nr(b, which):
            return (b + base) * 2 + (which + 1)

        def nu(b, unit, banks):
            return (b + base) * (SLOTS // banks) + (unit // banks + 1)

        def before(i, kind):
            here = [(k, i + o) for k, o in MISC_TURNS if ok(i + o)]
            at = [k for k, _ in here].index(kind)
            if at:
                return here[at - 1]
            if is_int(i):
                old = [(k, i - 1 + o) for k, o in MISC_TURNS if ok(i - 1 + o)]
                return old[-1] if old else None
            return MISC_TURNS[-1][0], i + (MISC_TURNS[-1][1] - 1)

        first = 3

        def run(eng, iteration):
            for i in range(-3, first):
                iteration(i, i % 2)
            pairs = (NB - 3 - first) // 2
            with eng.Fori(0, pairs) as j:
                iteration(j * 2 + first, 1)
                iteration(j * 2 + (first + 1), 0)
            for i in range(2 * pairs + first, NB + 1):
                iteration(i, i % 2)

        @block.sync
        def _(sp):
            def stack(b, half, buf):
                last = (SLOTS // 2) * (half + 1) - 1
                read = value(sp, nu(b - 2, last, ST_BANKS))
                passed = value(sp, nu(b - 1, half * SLOTS // 2, MX_BANKS))
                split = value(sp, nr(b, 1))
                sp.wait_ge(S.st_full[last % ST_BANKS], read)
                sp.wait_ge(S.mx_full[0], passed)
                sp.dma_start(query_rows(buf, 4 * MD, 2, half * HH, HH), query_rows(buf, 4 * MD + 2, 2, half * HH, HH))\
                    .then_inc(S.stack[half], 16)
                rows = slice(half * HH * MD, (half + 1) * HH * MD)
                at = slice(half * HH * 2 * SEQ, (half + 1) * HH * 2 * SEQ)
                for r, (q, k) in enumerate(((0, 2), (1, 2), (0, 3), (1, 3))):
                    if r < 2:
                        sp.wait_ge((S.hi, S.lo)[r], split)
                    sp.dma_start(words(T.stack[buf][r * MD:(r + 1) * MD, at]), words(parts[rows, q:k + 1:k - q, :]))\
                        .then_inc(S.stack[half], 16)

            def iteration(i, par):
                if ok(i + 2):
                    stack(i + 2, 0, par)
                if ok(i + 1):
                    b, buf = i + 1, 1 - par
                    there = value(sp, n(b))
                    sp.wait_ge(S.mt_hi, there)
                    sp.dma_start(query_rows(buf, 4 * MD, 1, 0, MH), words(mt_hi[:, :])).then_inc(S.maxrow, 16)
                    sp.wait_ge(S.taken["max_t"], there)
                    sp.dma_start(query_rows(buf, 4 * MD + 1, 1, 0, MH), words(mt_lo[:, :])).then_inc(S.maxrow, 16)
                if ok(i + 2):
                    stack(i + 2, 1, par)

            if L:
                sp.dma_start(T.w2_raw[:, :], A["w2"]).then_inc(L.w2, 16)

            run(sp, iteration)
            if L:
                sp.wait_ge(L.rest, 2 * 16)

        @block.gpsimd
        def _(pool):
            def scale_factors(b):
                count0 = value(pool, n(b))
                count1 = value(pool, n(b - 1))
                pool.wait_ge(T.made, 1)
                pool.wait_ge(S.stats, count0)
                pool.wait_ge(S.u, count1)
                pool.tensor_scalar(veps[:, 0, :], mv[:, :, 1], EPS5, None, ALU.add)
                pool.tensor_scalar(veps[:, 1, :], mv[:, :, 1], 1.0 + EPS6, EPS5 * EPS6,
                                   ALU.mult, ALU.add).then_inc(S.veps, 1)
                pool.wait_ge(S.veps, due(n(b)))
                pool.tensor_tensor(rs[:, :, :], veps[:, :, :], T.neghalf[:, :, 0:KT], ALU.pow).then_inc(S.rnorm, 1)

            def latent_factors(b):
                count0 = value(pool, n(b))
                count1 = value(pool, n(b - 1))
                pool.wait_ge(T.made, 1)
                pool.wait_ge(S.lat_stats, count0)
                pool.wait_ge(S.latn, count1)
                pool.tensor_scalar(lveps[:, :], lmv[:, :, 1], EPS5, None, ALU.add).then_inc(S.lat_veps, 1)
                pool.wait_ge(S.lat_veps, due(n(b)))
                pool.tensor_tensor(lrs[:, :], lveps[:, :], T.neghalf[:, 0, 0:KT], ALU.pow).then_inc(S.lat_rnorm, 1)

            def rotate(b, which):
                pool.wait_ge(S.taken["qk"[which]], due(n(b)))
                pool.wait_ge(S.hi, due(nr(b - 1, which)))
                pool.wait_ge(S.lo, due(nr(b - 1, which)))
                pool.tensor_tensor(rot[:, which, :], t_cos[:, which, :], t_sin[:, which, :], ALU.add)\
                    .then_inc(S.rot, 1)

            def lower(b, which):
                pool.wait_ge(S.hi, due(nr(b, which)))
                for half in range(2):
                    pool.wait_ge(S.stack[half], due(n(b - 1) * STACK_DMAS))
                pool.tensor_tensor(lo[:, which, :], rot[:, which, :], hi[:, which, :].bitcast(F32),
                                   ALU.subtract).then_inc(S.lo, 1)

            def causal(b, s):
                count0 = value(pool, nu(b, s, ST_BANKS))
                pool.wait_ge(T.made, 1)
                pool.wait_ge(S.exp[s % ST_BANKS], count0)
                if s % 3 == 2:
                    view = pr[:, s % RING, :].rearrange("p (h q) -> p h q", h=4)
                else:
                    view = pr[:, s % RING, :].rearrange("p (h q) -> p h q", h=2)[:, :, 0:P]
                ins = pool.affine_select(out=view, in_=view, compare_op=ALU.is_ge, fill=0.0, base=0,
                                         pattern=[[0, view.shape[1]], [1, P]], channel_multiplier=-1)
                if s % 3 == 2:
                    ins.then_inc(S.masked[s // 3], 1)

            def iteration(i, par):
                for s in range(SLOTS):
                    if ok(i):
                        causal(i, s)
                    if s in (4, 6) and ok(i + 2):
                        lower(i + 2, (4, 6).index(s))
                    if s in (2, 5) and ok(i + 2):
                        rotate(i + 2, (2, 5).index(s))
                    if s == 0 and ok(i + 2):
                        latent_factors(i + 2)
                    if s == 7 and ok(i + 3):
                        scale_factors(i + 3)

            run(pool, iteration)

        @block.scalar
        def _(act):
            def copy_out(kind, b, dst, src, func=ACT.Copy, **kw):
                act.wait_ge(S.turn[kind], due(n(b)))
                act.activation(dst, src, func, **kw).then_inc(S.taken[kind], 1)

            def exponentials(b, s):
                act.wait_ge(S.st_full[s % ST_BANKS], due(nu(b, s, ST_BANKS)))
                if s >= RING:
                    act.wait_ge(S.ov_full[(s - RING) // 3], due(n(b)))
                else:
                    act.wait_ge(S.ov_full[(s + SLOTS - RING) // 3], due(n(b - 1)))
                act.activation(pr[:, s % RING, :], st[s % 3][:, :], ACT.Exp, scale=MSCALE)\
                    .then_inc(S.exp[s % ST_BANKS], 1)

            def upper(b, which):
                act.wait_ge(S.rot, due(nr(b, which)))
                for half in range(2):
                    act.wait_ge(S.stack[half], due(n(b - 1) * STACK_DMAS))
                act.activation(hi[:, which, :], rot[:, which, :], ACT.Copy).then_inc(S.hi, 1)

            def take_products(b, g, par):
                act.wait_ge(S.ov_full[g], due(n(b)))
                act.wait_ge(S.turn["head_t1"], due(n(b - 1) if g == GRP - 1 else n(b - 2)))
                act.activation(ot[:, par, g, :], ov[g % 2][:, 0:SEQ], ACT.Copy).then_inc(S.ov_taken[g], 1)

            def iteration(i, par):
                for s in range(SLOTS):
                    if L and is_int(i) and i in (1, 2) and s % 3 == 0:
                        upper_slice(act, T, L, i - 1, s // 3)
                    if s == 8 and ok(i + 1):
                        act.wait_ge(S.turn["max_t"], due(n(i + 1)))
                        act.wait_ge(S.maxrow, due(n(i) * MAXROW_DMAS))
                        act.activation(mt_hi[:, :], misc[0:MH, 0:SEQ], ACT.Copy).then_inc(S.mt_hi, 1)
                    if ok(i):
                        exponentials(i, s)
                    if s == 0 and ok(i + 2):
                        act.wait_ge(S.turn["q"], due(n(i + 1)))
                        copy_out("un_t", i + 2, unT[:, :], misc[:, 0:SEQ], scale=T.norm1[:, 0:1])
                    if s == 4 and ok(i + 2):
                        act.wait_ge(S.turn["v"], due(n(i + 1)))
                        copy_out("latent_t", i + 2, latT[:, :], misc[0:LAT, 0:SEQ], ACT.Identity,
                                 scale=T.ln_g[:, 0:1], bias=T.ln_b[:, 0:1])
                    if s == 2 and ok(i - 1):
                        take_products(i - 1, 3, 1 - par)
                    if s == 7 and ok(i - 1):
                        act.wait_ge(S.turn["wo"], due(n(i - 2)))
                        copy_out("out_t", i - 1, onT[:, :], misc[:, 0:SEQ])
                    if s in (3, 6) and ok(i + 2):
                        upper(i + 2, (3, 6).index(s))
                    if s == 6 and ok(i):
                        take_products(i, 0, par)
                    if s == 9 and ok(i + 2):
                        act.wait_ge(S.va, due(n(i + 1)))
                        copy_out("v", i + 2, vst[:, :, :, :].rearrange("p k h d -> p (k h d)"), misc[:, 0:SEQ])
                    if s == 9 and ok(i):
                        take_products(i, 1, par)
                    if s == 11 and ok(i):
                        take_products(i, 2, par)

            run(act, iteration)

        @block.vector
        def _(dve):
            def row_stats(b):
                for k in range(KT):
                    ins = dve.bn_stats(st6[:, k, :], X[:, cols(b * SEQ + k * D, D)])
                ins.then_inc(S.bn, 1)
                count0 = value(dve, n(b))
                dve.wait_ge(T.made, 1)
                dve.wait_ge(S.bn, count0)
                for k in range(KT):
                    ins = dve.bn_aggr(mv[:, k, :], st6[:, k, :])
                ins.then_inc(S.stats, 1)

            def norm_rows(b):
                dve.wait_ge(S.rnorm, due(n(b)))
                dve.wait_ge(S.turn["un_t"], due(n(b - 1)))
                for k in range(KT):
                    at = cols(b * SEQ + k * D, D)
                    dve.tensor_scalar(U[:, at], X[:, at], mv[:, k, 0:1], rs[:, 0, k:k + 1],
                                      ALU.subtract, ALU.mult)
                    ins = dve.tensor_scalar(un[:, k, :], X[:, at], mv[:, k, 0:1], rs[:, 1, k:k + 1],
                                            ALU.subtract, ALU.mult)
                ins.then_inc(S.u, 1)

            def latent_stats(b):
                dve.wait_ge(S.turn["latent"], due(n(b)))
                dve.tensor_copy(lat[:, :, :], misc[:, 0:KT * LAT].rearrange("p (k c) -> p k c", k=KT))\
                    .then_inc(S.taken["latent"], 1)
                dve.wait_ge(S.taken["latent"], due(n(b)))
                for k in range(KT):
                    ins = dve.bn_stats(lst6[:, k, :], lat[:, k, :])
                ins.then_inc(S.lat_bn, 1)
                count0 = value(dve, n(b))
                dve.wait_ge(T.made, 1)
                dve.wait_ge(S.lat_bn, count0)
                for k in range(KT):
                    ins = dve.bn_aggr(lmv[:, k, :], lst6[:, k, :])
                ins.then_inc(S.lat_stats, 1)

            def norm_latents(b):
                dve.wait_ge(S.lat_rnorm, due(n(b)))
                dve.wait_ge(S.turn["latent_t"], due(n(b - 1)))
                for k in range(KT):
                    ins = dve.tensor_scalar(latn[:, k, :], lat[:, k, :], lmv[:, k, 0:1], lrs[:, k:k + 1],
                                            ALU.subtract, ALU.mult)
                ins.then_inc(S.latn, 1)

            def rotary_products(kind, which, b):
                dve.wait_ge(S.turn[kind], due(n(b)))
                dve.wait_ge(S.rot, due(nr(b - 1, which)))
                dve.tensor_tensor(t_cos[:, which, :], misc[:, 0:SEQ], T.cos[:, :], ALU.mult)
                dve.tensor_tensor(t_sin[:, which, :], misc[:, SEQ:2 * SEQ], T.sin[:, :], ALU.mult)\
                    .then_inc(S.taken[kind], 1)

            def place_values(b, buf):
                dve.wait_ge(S.taken["v"], due(n(b)))
                dve.wait_ge(S.ov_full[GRP - 1], due(n(b - 2)))
                dve.tensor_copy(va[buf][:, :, :, 0:MD], vst[:, :, :, :]).then_inc(S.va, 1)

            def norm_heads(b, k):
                kind = f"head_t{k}"
                heads = misc[:, :].rearrange("p (h c) -> p h c", c=MW)
                dve.wait_ge(S.turn[kind], due(n(b)))
                dve.reciprocal(rec[:, k, :], heads[:, :, MD]).then_inc(S.recip[k], 1)
                dve.wait_ge(S.recip[k], due(n(b)))
                dve.wait_ge(S.turn["out_t"], due(n(b - 1)))
                dve.tensor_tensor(on[:, k, :, :], heads[:, :, 0:MD],
                                  rec[:, k, :].unsqueeze(2).to_broadcast([P, MH, MD]), ALU.mult)\
                    .then_inc(S.taken[kind], 1)

            def maxima(b, v):
                dve.wait_ge(S.mx_full[v % MX_BANKS], due(nu(b, v, MX_BANKS)))
                if v == 0:
                    dve.wait_ge(S.turn["max_t"], due(n(b - 1)))
                h, nh, t = UNITS[v]
                dve.tensor_reduce(mx[:, t, h:h + nh], mxp[v % 2][:, :].rearrange("p (h k) -> p h k", h=nh), AX.X,
                                  ALU.max, negate=True).then_inc(S.mx_done[v % MX_BANKS], 1)

            def iteration(i, par):
                for s in range(SLOTS):
                    if s == 1 and ok(i + 2):
                        latent_stats(i + 2)
                    if L and is_int(i) and i in (1, 2) and s >= SLOTS - SLICES:
                        lower_slice(dve, T, L, i - 1, s - (SLOTS - SLICES))
                    if s == 8 and ok(i + 1):
                        place_values(i + 1, 1 - par)
                    if s == 0 and ok(i + 3):
                        if L and is_int(i) and i + 3 == X_FIRST:
                            dve.wait_ge(L.x, 16)
                        row_stats(i + 3)
                    if s == 2 and ok(i + 2):
                        rotary_products("q", 0, i + 2)
                    if s == 2 and ok(i + 2):
                        norm_latents(i + 2)
                    if s == 6 and ok(i - 1):
                        norm_heads(i - 1, 1)
                    if s == 3 and ok(i - 1):
                        norm_heads(i - 1, 0)
                    if s == 5 and ok(i + 2):
                        rotary_products("k", 1, i + 2)
                    if s == 8 and ok(i + 1):
                        b = i + 1
                        dve.wait_ge(S.mt_hi, due(n(b)))
                        dve.wait_ge(S.maxrow, due(n(b - 1) * MAXROW_DMAS))
                        dve.tensor_tensor(mt_lo[:, :], misc[0:MH, 0:SEQ], mt_hi[:, :].bitcast(F32),
                                          ALU.subtract).then_inc(S.taken["max_t"], 1)
                    if s == 9 and ok(i + 3):
                        norm_rows(i + 3)
                    if ok(i + 1):
                        for v in MAX_SLOTS.get(s, ()):
                            maxima(i + 1, v)
                    if s == 10 and ok(i - 1):
                        b = i - 1
                        dve.wait_ge(S.turn["wo"], due(n(b)))
                        at = cols(b * SEQ, SEQ)
                        dve.tensor_tensor(U[:, at], misc[:, 0:SEQ], U[:, at], ALU.add).then_inc(S.taken["wo"], 1)

            run(dve, iteration)

        @block.tensor
        def _(pe):
            def turn(kind, b, buf):
                if kind == "un_t":
                    pe.wait_ge(S.u, due(n(b)))
                    for k in range(KT):
                        ins = pe.transpose(misc[:, k * P:(k + 1) * P], un[:, k, :], T.ident[:, :])
                elif kind == "latent":
                    pe.wait_ge(S.taken["un_t"], due(n(b)))
                    for k in range(KT):
                        ins = pe.matmul(misc[:, k * LAT:(k + 1) * LAT], unT[:, k * P:(k + 1) * P], T.wdkv[:, :],
                                        start=True, stop=True)
                elif kind == "q":
                    for half, w in enumerate((T.wq, T.wq_swap)):
                        ins = pe.matmul(misc[:, half * SEQ:(half + 1) * SEQ], w[:, :], unT[:, :],
                                        start=True, stop=True)
                elif kind == "latent_t":
                    for k in range(KT):
                        ins = pe.transpose(misc[0:LAT, k * P:(k + 1) * P], latn[:, k, :], T.ident[:, :])
                elif kind == "k":
                    pe.wait_ge(S.taken["latent_t"], due(n(b)))
                    for half, w in enumerate((T.wuk, T.wuk_swap)):
                        ins = pe.matmul(misc[:, half * SEQ:(half + 1) * SEQ], w[:, :], latT[:, :],
                                        start=True, stop=True)
                elif kind == "v":
                    for k in range(KT):
                        ins = pe.matmul(misc[:, k * D:(k + 1) * D], latT[:, k * P:(k + 1) * P], T.wuv[:, :],
                                        start=True, stop=True)
                elif kind in ("head_t0", "head_t1"):
                    k = int(kind[-1])
                    if k == 0:
                        for g in range(GRP):
                            pe.wait_ge(S.ov_taken[g], due(n(b)))
                    for g in range(GRP):
                        ins = pe.transpose(misc[:, g * P:(g + 1) * P], ot[:, buf, g, k * P:(k + 1) * P], T.ident[:, :])
                elif kind == "out_t":
                    pe.wait_ge(S.taken["head_t0"], due(n(b)))
                    pe.wait_ge(S.taken["head_t1"], due(n(b)))
                    for k in range(KT):
                        ins = pe.transpose(misc[:, k * P:(k + 1) * P],
                                           on[:, k, :, :].rearrange("p h d -> p (h d)"), T.ident[:, :])
                elif kind == "wo":
                    pe.wait_ge(S.taken["out_t"], due(n(b)))
                    for k in range(KT):
                        ins = pe.matmul(misc[:, k * D:(k + 1) * D], onT[:, k * P:(k + 1) * P], T.wo[:, :],
                                        start=True, stop=True)
                else:
                    pe.wait_ge(S.mx_done[(SLOTS - 1) % MX_BANKS], due(nu(b, SLOTS - 1, MX_BANKS)))
                    for k in range(KT):
                        ins = pe.transpose(misc[0:MH, k * P:(k + 1) * P], mx[:, k, :], T.ident[:, :])
                return ins

            def transposed_scores(b, s, buf):
                if s == 0:
                    for half in range(2):
                        pe.wait_ge(S.stack[half], due(n(b) * STACK_DMAS))
                    pe.wait_ge(S.maxrow, due(n(b) * MAXROW_DMAS))
                pe.wait_ge(S.exp[s % ST_BANKS], due(nu(b, s, ST_BANKS) - 1))
                g, part = divmod(s, 3)
                heads = [4 * g + 2 * part, 4 * g + 2 * part + 1] if part < 2 else [4 * g + m for m in range(4)]
                t0 = 0 if part < 2 else P
                size = SEQ - t0
                for m, h in enumerate(heads):
                    ins = pe.matmul(st[s % 3][:, m * size:(m + 1) * size],
                                    keys(buf, h, t0, P), queries(buf, h, t0, size),
                                    start=(m == 0), stop=(m == len(heads) - 1), skip_group_check=True)
                ins.then_inc(S.st_full[s % ST_BANKS], 1)

            def plain_scores(b, v, buf):
                h, nh, t = UNITS[v]
                if v % (SLOTS // 2) == 0:
                    pe.wait_ge(S.stack[h // HH], due(n(b) * STACK_DMAS))
                pe.wait_ge(S.mx_done[v % MX_BANKS], due(nu(b, v, MX_BANKS) - 1))
                bank = mxp[v % 2]
                size = (t + 1) * P
                for m in range(nh):
                    pe.matmul(bank[:, m * size:(m + 1) * size], queries(buf, h + m, t * P, P),
                              keys(buf, h + m, 0, size), start=(m == 0), stop=False, skip_group_check=True)
                pe.matmul(bank[:, :].rearrange("p (h k) -> p h k", h=nh)[:, :, size - P:size], T.ident_bf[:, :],
                          T.neg[:, 0:nh, :], start=False, stop=True, skip_group_check=True)\
                    .then_inc(S.mx_full[v % MX_BANKS], 1)

            def value_products(b, g, buf):
                if g == 0:
                    pe.wait_ge(S.va, due(n(b)))
                if g >= 2:
                    pe.wait_ge(S.ov_taken[g - 2], due(n(b)))
                else:
                    pe.wait_ge(S.ov_taken[g + 2], due(n(b - 1)))
                pe.wait_ge(S.masked[g], due(n(b)))
                for kt in range(KT):
                    for m in range(GRP):
                        h = 4 * g + m
                        s = 3 * g + (m // 2 if kt == 0 else 2)
                        size = SEQ - kt * P
                        at = (m % 2 if kt == 0 else m) * size
                        ins = pe.matmul(ov[g % 2][MW * m:MW * (m + 1), kt * P:SEQ], va[buf][:, kt, h, :],
                                        pr[:, s % RING, at:at + size], start=(kt == 0), stop=(kt == KT - 1),
                                        skip_group_check=True)
                ins.then_inc(S.ov_full[g], 1)

            def iteration(i, par):
                for s in range(SLOTS):
                    if ok(i):
                        transposed_scores(i, s, par)
                    if s in LATENT_MISC:
                        kind, off = LATENT_MISC[s]
                        if ok(i + off):
                            prev = before(i, kind)
                            turned = value(pe, n(i + off))
                            free = value(pe, n(prev[1])) if prev else None
                            if kind == "latent_t":
                                pe.wait_ge(T.made, 1)
                            if prev:
                                pe.wait_ge(S.taken[prev[0]], free)
                            if kind == "latent_t":
                                pe.wait_ge(S.latn, turned)
                            turn(kind, i + off, (par + off) % 2).then_inc(S.turn[kind], 1)
                    if s in VALUE_SLOTS:
                        off, g = VALUE_SLOTS[s]
                        if ok(i + off):
                            value_products(i + off, g, (par + off) % 2)
                    if ok(i + 1):
                        for v in MAX_SLOTS.get(s, ()):
                            plain_scores(i + 1, v, 1 - par)

            run(pe, iteration)


CT = 4
CN = CT * P
NC = NT // CT
NQ = NE * HC
HR = 4
LAGQ = 3
PICK = 6
OUT_SLOTS = {3: (-1, 3), 7: (0, 0), 10: (0, 1), 15: (0, 2)}
BACK_SLOTS = {1: (-1, 2), 6: (-1, 3), 9: (0, 0), 13: (0, 1)}
ADD_SLOTS = {3: (-1, 2), 6: (-1, 3), 11: (0, 0), 15: (0, 1)}


class MoeSems:

    def __init__(self, sem):
        self.bn = sem("moe_bn")
        self.stats = sem("moe_stats")
        self.sq = sem("moe_sq")
        self.ms = sem("moe_ms")
        self.veps = sem("moe_veps")
        self.rnorm = sem("moe_rnorm")
        self.xn = sem("moe_xn")
        self.xt_ready = sem("moe_xt_ready")
        self.xt = sem("moe_xt")
        self.x_hi = sem("moe_x_hi")
        self.x_lo = sem("moe_x_lo")
        self.lg_ready = sem("moe_lg_ready")
        self.pick = sem("moe_pick")
        self.onehot = sem("moe_onehot")
        self.h_full = [sem(f"moe_h_full{n}") for n in range(HR)]
        self.h_hi = [sem(f"moe_h_hi{n}") for n in range(HR)]
        self.h = [sem(f"moe_h{n}") for n in range(HR)]
        self.h_lo = [sem(f"moe_h_lo{n}") for n in range(HR)]
        self.h_used = [sem(f"moe_h_used{n}") for n in range(HR)]
        self.y_sb = sem("moe_y_sb")
        self.yt_ready = sem("moe_yt_ready")
        self.acc = sem("moe_acc")
        self.x = sem("moe_x")
        self.stored = sem("moe_stored")


def moe_phase(nc, T, S, base, out=None):
    tiles = ExitStack()
    with tiles:
        def sb(name, shape, dt=F32):
            return tiles.enter_context(nc.sbuf_tensor(f"moe{base}_{name}", shape, dt))

        def pb(name):
            return tiles.enter_context(nc.psum_tensor(f"moe{base}_{name}", [P, 512], F32))

        st6 = sb("st6", [P, CT, 6])
        mv = sb("mv", [P, CT, 2])
        msq = sb("msq", [P, 3, CT])
        rs = sb("rs", [P, CT])
        xn = sb("xn", [P, CT, D])
        xT = sb("xT", [D, CN])
        x_hi = [sb(f"x_hi{n}", [D, CN], F32R) for n in range(2)]
        x_lo = [sb(f"x_lo{n}", [D, CN], F32R) for n in range(2)]
        lg = sb("lg", [P, CT, NE])
        top = sb("top", [P, CT])
        eq = sb("eq", [P, CT, NE])
        seen = sb("seen", [P, CT, NE])
        onehot = [sb(f"onehot{n}", [P, CT, NE]) for n in range(2)]
        h_hi = [sb(f"h_hi{n}", [P, CN], F32R) for n in range(HR)]
        h = [sb(f"h{n}", [P, CN]) for n in range(HR)]
        h_lo = [sb(f"h_lo{n}", [P, CN], F32R) for n in range(HR)]
        y_sb = [sb(f"y_sb{n}", [D, CN]) for n in range(2)]
        acc = sb("acc", [P, CN])

        hp = [pb(f"hp{n}") for n in range(HR)]
        yp = [pb(f"yp{n}") for n in range(2)]
        amid = pb("amid")
        yt = pb("yt")
        block = tiles.enter_context(nc.Block(f"moe{base}"))
        X, U = T.X, T.U

        def ok(c):
            return not is_int(c) or 0 <= c < NC

        def n(c):
            return c + (base + 1)

        def ne(c, e):
            return (c + base) * NE + (e + 1)

        def m(c, q):
            return (c + base) * (NQ // HR) + (q // HR + 1)

        def run(eng, iteration):
            first = 3 if base == 0 else 1
            for i in range(-1, first):
                iteration(i, i % 2)
            pairs = (NC - 1 - first + 1) // 2
            with eng.Fori(0, pairs) as j:
                iteration(j * 2 + first, 1)
                iteration(j * 2 + (first + 1), 0)
            for i in range(2 * pairs + first, NC + 1):
                iteration(i, i % 2)

        @block.sync
        def _(sp):
            if out is None:
                return
            rows = out.rearrange("(c b) (k p) d -> c p (b k) d", p=P, b=NB // NC)
            for c in range(NC):
                sp.wait_ge(S.x, n(c))
                sp.dma_start(rows[c], X[:, c * CN:(c + 1) * CN].rearrange("p (t d) -> p t d", d=D))\
                    .then_inc(S.stored, 16)
            sp.wait_ge(S.stored, 16 * NC)

        @block.gpsimd
        def _(pool):
            def scale_factors(c):
                pool.wait_ge(S.stats, due(n(c)))
                pool.wait_ge(S.xn, due(n(c - 1)))
                pool.tensor_tensor(msq[:, 0, :], mv[:, :, 0], mv[:, :, 0], ALU.mult).then_inc(S.sq, 1)
                pool.wait_ge(S.sq, due(n(c)))
                pool.tensor_tensor(msq[:, 1, :], msq[:, 0, :], mv[:, :, 1], ALU.add).then_inc(S.ms, 1)
                count0 = value(pool, n(c))
                pool.wait_ge(T.made, 1)
                pool.wait_ge(S.ms, count0)
                pool.tensor_scalar(msq[:, 2, :], msq[:, 1, :], EPS6, None, ALU.add).then_inc(S.veps, 1)
                pool.wait_ge(S.veps, due(n(c)))
                pool.tensor_tensor(rs[:, :], msq[:, 2, :], T.neghalf[:, :, :].rearrange("p a b -> p (a b)"),
                                   ALU.pow).then_inc(S.rnorm, 1)

            def lower_input(c, buf):
                pool.wait_ge(S.x_hi, due(n(c)))
                pool.tensor_tensor(x_lo[buf][:, :], xT[:, :], x_hi[buf][:, :].bitcast(F32),
                                   ALU.subtract).then_inc(S.x_lo, 1)

            def iteration(i, par):
                for q in range(NQ):
                    if q == 7 and ok(i + 1):
                        lower_input(i + 1, 1 - par)
                    if q == 1 and ok(i + 1):
                        scale_factors(i + 1)
                    r = q % HR
                    if r < HR - 1 and ok(i):
                        pool.wait_ge(S.h_hi[r], due(m(i, q)))
                        pool.tensor_tensor(h_lo[r][:, :], h[r][:, :], h_hi[r][:, :].bitcast(F32), ALU.subtract)\
                            .then_inc(S.h_lo[r], 1)

            run(pool, iteration)

        @block.scalar
        def _(act):
            def iteration(i, par):
                for q in range(NQ):
                    if q == 8 and ok(i + 1):
                        c = i + 1
                        act.wait_ge(S.xt, due(n(c)))
                        act.wait_ge(S.h_used[(NQ - 1) % HR], due(m(c - 2, NQ - 1)))
                        act.activation(x_hi[1 - par][:, :], xT[:, :], ACT.Copy).then_inc(S.x_hi, 1)

                    if ok(i):
                        r = q % HR
                        if r == HR - 1:
                            act.wait_ge(S.h_full[r], due(m(i, q)))
                            act.wait_ge(S.h_lo[r], due(m(i, q) - 1))
                            act.activation(h[r][:, :], hp[r][:, :], ACT.Relu, bias=T.b1[:, q:q + 1])\
                                .then_inc(S.h[r], 1)
                        act.wait_ge(S.h[r], due(m(i, q)))
                        act.wait_ge(S.h_used[r], due(m(i, q) - 1))
                        act.activation(h_hi[r][:, :], h[r][:, :], ACT.Copy).then_inc(S.h_hi[r], 1)
                    if q in OUT_SLOTS:
                        off, e = OUT_SLOTS[q]
                        if ok(i + off):
                            c = i + off
                            act.wait_ge(S.h_used[HR - 1], due(m(c, (e + 1) * HC - 1)))
                            act.wait_ge(S.yt_ready, due(ne(c, e) - 2))
                            act.activation(y_sb[e % 2][:, :], yp[e % 2][:, :], ACT.Identity, bias=T.b2[:, e:e + 1])\
                                .then_inc(S.y_sb, 1)
            run(act, iteration)

        @block.vector
        def _(dve):
            def norm_stats(c):
                for k in range(CT):
                    ins = dve.bn_stats(st6[:, k, :], U[:, cols(c * CN + k * D, D)])
                ins.then_inc(S.bn, 1)
                count0 = value(dve, n(c))
                dve.wait_ge(T.made, 1)
                dve.wait_ge(S.bn, count0)
                for k in range(CT):
                    ins = dve.bn_aggr(mv[:, k, :], st6[:, k, :])
                ins.then_inc(S.stats, 1)

            def norm(c):
                dve.wait_ge(S.rnorm, due(n(c)))
                dve.wait_ge(S.xt_ready, due(n(c - 1)))
                for k in range(CT):
                    ins = dve.tensor_scalar(xn[:, k, :], U[:, cols(c * CN + k * D, D)], rs[:, k:k + 1], None,
                                            ALU.mult)
                ins.then_inc(S.xn, 1)

            def weigh(c):
                dve.wait_ge(S.xt_ready, due(n(c)))
                dve.wait_ge(S.lg_ready, due(n(c - 1)))
                dve.wait_ge(S.x_lo, due(n(c - 1)))
                dve.tensor_scalar(xT[:, :], amid[:, :], T.norm2[:, 0:1], None, ALU.mult).then_inc(S.xt, 1)

            def choose(c, buf):
                def step(k):
                    return (c + base) * PICK + k

                dve.wait_ge(S.lg_ready, due(n(c)))
                dve.tensor_tensor(lg[:, :, :], amid[:, 0:CT * NE].rearrange("p (k e) -> p k e", e=NE),
                                  T.gate_b[:, :].unsqueeze(1).to_broadcast([P, CT, NE]), ALU.add)\
                    .then_inc(S.pick, 1)
                dve.wait_ge(S.pick, step(1))
                dve.tensor_reduce(top[:, :], lg[:, :, :], AX.X, ALU.max).then_inc(S.pick, 1)
                dve.wait_ge(S.pick, step(2))
                dve.tensor_tensor(eq[:, :, :], lg[:, :, :], top[:, :].unsqueeze(2).to_broadcast([P, CT, NE]),
                                  ALU.is_equal).then_inc(S.pick, 1)
                dve.wait_ge(S.pick, step(3))
                dve.tensor_copy(seen[:, :, 1], eq[:, :, 0]).then_inc(S.pick, 1)
                for e in (1, 2):
                    dve.wait_ge(S.pick, step(3 + e))
                    dve.tensor_tensor(seen[:, :, e + 1], seen[:, :, e], eq[:, :, e], ALU.max)\
                        .then_inc(S.pick, 1)
                dve.wait_ge(S.pick, step(6))
                dve.wait_ge(S.acc, due(ne(c - 2, NE - 1)))
                dve.tensor_tensor(onehot[buf][:, :, :], eq[:, :, :], seen[:, :, :], ALU.is_gt).then_inc(S.onehot, 1)

            def add_expert(c, e, buf):
                dve.wait_ge(S.yt_ready, due(ne(c, e)))
                dve.wait_ge(S.onehot, due(n(c)))
                dve.wait_ge(S.acc, due(ne(c, e) - 1))
                if e == 0:
                    dve.wait_ge(S.x, due(n(c - 1)))
                for k in range(CT):
                    so_far = U[:, cols(c * CN + k * D, D)] if e == 0 else acc[:, k * D:(k + 1) * D]
                    ins = dve.scalar_tensor_tensor(acc[:, k * D:(k + 1) * D], yt[:, k * P:(k + 1) * P],
                                                   onehot[buf][:, k, e:e + 1], so_far, op0=ALU.mult, op1=ALU.add)
                ins.then_inc(S.acc, 1)

            def finish(c):
                dve.wait_ge(S.acc, due(ne(c, NE - 1)))
                at = cols(c * CN, CN)
                dve.scalar_tensor_tensor(X[:, at], acc[:, :], 0.5, X[:, at], op0=ALU.mult, op1=ALU.add)\
                    .then_inc(S.x, 1)

            def iteration(i, par):
                if is_int(i) and i == -1:
                    dve.memset(seen[:, :, 0], 0.0)
                for q in range(NQ):
                    r = q % HR
                    if r < HR - 1 and ok(i):
                        dve.wait_ge(S.h_full[r], due(m(i, q)))
                        dve.wait_ge(S.h_lo[r], due(m(i, q) - 1))
                        dve.tensor_scalar(h[r][:, :], hp[r][:, :], T.b1[:, q:q + 1], 0.0, ALU.add, ALU.max)\
                            .then_inc(S.h[r], 1)
                    if q == 0 and ok(i + 1):
                        norm_stats(i + 1)
                    if r == 0 and ok(i if q else i - 1):
                        last, c, b = HR - 1, i if q else i - 1, q - 1 if q else NQ - 1
                        dve.wait_ge(S.h_hi[last], due(m(c, b)))
                        dve.tensor_tensor(h_lo[last][:, :], h[last][:, :], h_hi[last][:, :].bitcast(F32),
                                          ALU.subtract).then_inc(S.h_lo[last], 1)
                    if q in ADD_SLOTS:
                        off, e = ADD_SLOTS[q]
                        if ok(i + off):
                            add_expert(i + off, e, (par + off) % 2)
                    if q == 8 and ok(i - 1):
                        finish(i - 1)
                    if q == 5 and ok(i + 1):
                        norm(i + 1)
                    if q == 7 and ok(i + 1):
                        weigh(i + 1)
                    if q == 11 and ok(i + 1):
                        choose(i + 1, 1 - par)

            run(dve, iteration)

        @block.tensor
        def _(pe):
            def block_in(c, q, buf):
                r = q % HR
                if q == 0:
                    pe.wait_ge(S.x_hi, due(n(c)))
                pe.wait_ge(S.h[r], due(m(c, q) - 1))
                w = slice(q * P, (q + 1) * P)
                pe.matmul(hp[r][:, :], T.w1_lo[:, w], x_hi[buf][:, :], start=True, stop=False)
                pe.matmul(hp[r][:, :], T.w1_hi[:, w], x_hi[buf][:, :], start=False, stop=False)
                if q == 0:
                    pe.wait_ge(S.x_lo, due(n(c)))
                pe.matmul(hp[r][:, :], T.w1_hi[:, w], x_lo[buf][:, :], start=False, stop=True)\
                    .then_inc(S.h_full[r], 1)

            def block_out(c, q):
                r = q % HR
                e, part = divmod(q, HC)
                if part == 0:
                    pe.wait_ge(S.y_sb, due(ne(c, e) - 2))
                pe.wait_ge(S.h_hi[r], due(m(c, q)))
                y = yp[e % 2]
                w = slice(q * P, (q + 1) * P)
                pe.matmul(y[:, :], T.w2_lo[:, w], h_hi[r][:, :], start=(part == 0), stop=False)
                pe.matmul(y[:, :], T.w2_hi[:, w], h_hi[r][:, :], start=False, stop=False)
                pe.wait_ge(S.h_lo[r], due(m(c, q)))
                pe.matmul(y[:, :], T.w2_hi[:, w], h_lo[r][:, :], start=False, stop=(part == HC - 1))\
                    .then_inc(S.h_used[r], 1)

            def iteration(i, par):
                for q in range(NQ):
                    if ok(i):
                        block_in(i, q, par)
                    if q < LAGQ and ok(i - 1):
                        block_out(i - 1, q + NQ - LAGQ)
                    if q >= LAGQ and ok(i):
                        block_out(i, q - LAGQ)
                    if q == 6 and ok(i + 1):
                        c = i + 1
                        pe.wait_ge(S.xn, due(n(c)))
                        pe.wait_ge(S.pick, due((c + base - 1) * PICK + 1))
                        for k in range(CT):
                            ins = pe.transpose(amid[:, k * P:(k + 1) * P], xn[:, k, :], T.ident[:, :])
                        ins.then_inc(S.xt_ready, 1)
                    if q == 9 and ok(i + 1):
                        c = i + 1
                        pe.wait_ge(S.xt, due(n(c)))
                        for k in range(CT):
                            ins = pe.matmul(amid[:, k * NE:(k + 1) * NE], xT[:, k * P:(k + 1) * P], T.gate[:, :],
                                            start=True, stop=True)
                        ins.then_inc(S.lg_ready, 1)

                    if q in BACK_SLOTS:
                        off, e = BACK_SLOTS[q]
                        if ok(i + off):
                            c = i + off
                            pe.wait_ge(S.y_sb, due(ne(c, e)))
                            pe.wait_ge(S.acc, due(ne(c, e) - 1))
                            for k in range(CT):
                                ins = pe.transpose(yt[:, k * P:(k + 1) * P], y_sb[e % 2][:, k * P:(k + 1) * P],
                                                   T.ident[:, :])
                            ins.then_inc(S.yt_ready, 1)
            run(pe, iteration)


PR4 = 4
PT_LAG = 2
Q_SLOTS = {3: 0, 5: 1, 6: 2, 7: 3}
PAIR_SLOTS = {4: (0, 0), 6: (0, 1), 0: (-1, 2), 2: (-1, 3)}
MULTI_MISC = {0: ("xt", 1), 2: ("kv", 1), 4: ("wo", -1)}
MISC_ORDER = [MULTI_MISC[s] for s in sorted(MULTI_MISC)]


class MqaSems:

    def __init__(self, sem):
        self.bn = sem("mqa_bn")
        self.stats = sem("mqa_stats")
        self.sum_eps = sem("mqa_sum_eps")
        self.veps = sem("mqa_veps")
        self.rnorm = sem("mqa_rnorm")
        self.xn = sem("mqa_xn")
        self.turn = {k: sem(f"mqa_{k}_ready") for k, _ in MISC_ORDER}
        self.taken = {k: sem(f"mqa_{k}_taken") for k, _ in MISC_ORDER}
        self.k_hi = sem("mqa_k_hi")
        self.vals = sem("mqa_vals")
        self.q_ready = sem("mqa_q_ready")
        self.q_hi = sem("mqa_q_hi")
        self.q = sem("mqa_q")
        self.s_full = [sem(f"mqa_s_full{n}") for n in range(2)]
        self.mx = [sem(f"mqa_mx{n}") for n in range(2)]
        self.exp = [sem(f"mqa_exp{n}") for n in range(2)]
        self.pt_full = [sem(f"mqa_pt_full{n}") for n in range(2)]
        self.pt_sb = [sem(f"mqa_pt_sb{n}") for n in range(2)]
        self.ov_full = [sem(f"mqa_ov_full{n}") for n in range(2)]
        self.ov_sb = [sem(f"mqa_ov_sb{n}") for n in range(2)]
        self.rec = [sem(f"mqa_rec{n}") for n in range(2)]
        self.pn = [sem(f"mqa_pn{n}") for n in range(2)]
        self.o_bn = sem("mqa_o_bn")
        self.o_stats = sem("mqa_o_stats")
        self.o_veps = sem("mqa_o_veps")
        self.o_rnorm = sem("mqa_o_rnorm")
        self.o_norm = sem("mqa_o_norm")
        self.o_w = sem("mqa_o_w")
        self.o_b = sem("mqa_o_b")
        self.x = sem("mqa_x")


def mqa_phase(nc, T, S):
    tiles = ExitStack()
    with tiles:
        def sb(name, shape, dt=F32):
            return tiles.enter_context(nc.sbuf_tensor(f"mqa_{name}", shape, dt))

        def pb(name):
            return tiles.enter_context(nc.psum_tensor(f"mqa_{name}", [P, 512], F32))

        st6 = sb("st6", [P, KT, 6])
        mv = sb("mv", [P, KT, 2])
        veps = sb("veps", [P, 2, KT])
        rs = sb("rs", [P, KT])
        xn = sb("xn", [P, KT, D])
        xT = sb("xT", [D, SEQ])
        k_hi = [sb(f"k_hi{n}", [P, SEQ], F32R) for n in range(2)]
        k_lo = [sb(f"k_lo{n}", [P, SEQ], F32R) for n in range(2)]
        vals = [sb(f"vals{n}", [P, KT, AD]) for n in range(2)]
        q_all = [sb(f"q_all{n}", [AD, 2 * SEQ]) for n in range(2)]
        qst = [sb(f"qst{n}", [P, AH * SEQ], F32R) for n in range(2)]
        nmax = sb("nmax", [P, AH, KT])
        sums = sb("sums", [P, AH, KT])
        recs = sb("recs", [P, AH, KT])
        pr = sb("pr", [P, PR4, KT, SEQ])
        pt = sb("pt", [P, PR4, KT, SEQ])
        oT = sb("oT", [P, PAIRS, SEQ])
        o_sb = sb("o_sb", [P, KT, D])
        ost6 = sb("ost6", [P, KT, 6])
        omv = sb("omv", [P, KT, 2])
        oveps = sb("oveps", [P, KT])
        ors = sb("ors", [P, KT])
        o_n = sb("o_n", [P, KT, D])
        o_w = sb("o_w", [P, KT, D])
        o_b = sb("o_b", [P, KT, D])

        sp_ = [pb(f"s{n}") for n in range(2)]
        ptp = pb("ptp")
        ovp = [pb(f"ov{n}") for n in range(2)]
        qp = [pb(f"q{n}") for n in range(2)]
        misc = pb("misc")
        block = tiles.enter_context(nc.Block("mqa"))
        X = T.X

        def ok(b):
            return not is_int(b) or 0 <= b < NB

        def n(b):
            return b + 1

        def nh(b, h):
            return b * (AH // 2) + (h // 2 + 1)

        def nq(b, p):
            return b * PAIRS + (p + 1)

        def np_(b, p):
            return b * (PAIRS // 2) + (p // 2 + 1)

        def before(i, kind):
            here = [(k, i + o) for k, o in MISC_ORDER if ok(i + o)]
            at = [k for k, _ in here].index(kind)
            if at:
                return here[at - 1]
            if is_int(i):
                old = [(k, i - 1 + o) for k, o in MISC_ORDER if ok(i - 1 + o)]
                return old[-1] if old else None
            return MISC_ORDER[-1][0], i + (MISC_ORDER[-1][1] - 1)

        def run(eng, iteration):
            first = 3
            for i in range(-2, first):
                iteration(i, i % 2)
            pairs = (NB - 2 - first) // 2
            with eng.Fori(0, pairs) as j:
                iteration(j * 2 + first, 1)
                iteration(j * 2 + (first + 1), 0)
            for i in range(2 * pairs + first, NB + 2):
                iteration(i, i % 2)

        def take(eng, copy, b, h):
            eng.wait_ge(S.pt_full[h % 2], due(nh(b, h)))
            if h >= PR4:
                eng.wait_ge(S.ov_full[(h - PR4) // 2 % 2], due(np_(b, (h - PR4) // 2)))
            else:
                eng.wait_ge(S.ov_full[(h + AH - PR4) // 2 % 2], due(np_(b - 1, (h + AH - PR4) // 2)))
            copy(pt[:, h % PR4, :, :].rearrange("p t q -> p (t q)"), ptp[:, :]).then_inc(S.pt_sb[h % 2], 1)

        @block.gpsimd
        def _(pool):
            def row_factors(b):
                count0 = value(pool, n(b))
                count1 = value(pool, n(b - 1))
                pool.wait_ge(T.made, 1)
                pool.wait_ge(S.stats, count0)
                pool.wait_ge(S.xn, count1)
                pool.tensor_scalar(veps[:, 0, :], mv[:, :, 1], EPS5, EPS5 * EPS5, ALU.mult, ALU.add)\
                    .then_inc(S.sum_eps, 1)
                pool.wait_ge(S.sum_eps, due(n(b)))
                pool.tensor_tensor(veps[:, 1, :], veps[:, 0, :], mv[:, :, 1], ALU.add).then_inc(S.veps, 1)
                pool.wait_ge(S.veps, due(n(b)))
                pool.tensor_tensor(rs[:, :], veps[:, 1, :], T.neghalf[:, 0, 0:KT], ALU.pow).then_inc(S.rnorm, 1)

            def out_factors(b):
                count0 = value(pool, n(b))
                pool.wait_ge(T.made, 1)
                pool.wait_ge(S.o_stats, count0)
                pool.tensor_scalar(oveps[:, :], omv[:, :, 1], EPS5, None, ALU.add).then_inc(S.o_veps, 1)
                pool.wait_ge(S.o_veps, due(n(b)))
                pool.tensor_tensor(ors[:, :], oveps[:, :], T.neghalf[:, 0, 0:KT], ALU.pow).then_inc(S.o_rnorm, 1)

            def finish(b):
                pool.wait_ge(S.o_norm, due(n(b)))
                row = lambda t: t[:, :].unsqueeze(1).to_broadcast([P, KT, D])
                pool.tensor_tensor(o_w[:, :, :], o_n[:, :, :], row(T.out_w), ALU.mult).then_inc(S.o_w, 1)
                pool.wait_ge(S.o_w, due(n(b)))
                pool.tensor_tensor(o_b[:, :, :], o_w[:, :, :], row(T.out_b), ALU.add).then_inc(S.o_b, 1)
                pool.wait_ge(S.o_b, due(n(b)))
                at = cols(b * SEQ, SEQ)
                pool.tensor_tensor(X[:, at], X[:, at], o_b[:, :, :].rearrange("p k d -> p (k d)"), ALU.add)\
                    .then_inc(S.x, 1)

            def lower_queries(b, p, buf):
                pool.wait_ge(S.q_hi, due(nq(b, p)))
                low = qst[buf][0:AD, 2 * p * SEQ:(2 * p + 2) * SEQ]
                pool.tensor_tensor(low, q_all[p % 2][:, :], low.bitcast(F32), ALU.subtract).then_inc(S.q, 1)

            def iteration(i, par):
                for s in range(AH):
                    if s == 2 and ok(i):
                        lower_queries(i, PAIRS - 1, par)
                    if s - 1 in Q_SLOTS and ok(i + 1):
                        lower_queries(i + 1, Q_SLOTS[s - 1], 1 - par)
                    if s == 1 and ok(i - 2):
                        finish(i - 2)

                    if s == 2 and ok(i + 2):
                        row_factors(i + 2)
                    if s == 5 and ok(i - 1):
                        out_factors(i - 1)
            run(pool, iteration)

        @block.scalar
        def _(act):
            def exponentials(b, h):
                s = h % 2
                act.wait_ge(S.mx[s], due(nh(b, h)))
                if h >= PR4:
                    act.wait_ge(S.pt_full[s], due(nh(b, h - PR4)))
                else:
                    act.wait_ge(S.pt_full[s], due(nh(b - 1, h + AH - PR4)))
                for t in range(KT):
                    ins = act.activation(pr[:, h % PR4, t, :], sp_[s][:, t * SEQ:(t + 1) * SEQ], ACT.Exp,
                                         bias=nmax[:, h, t:t + 1], accum_out=sums[:, h, t:t + 1])
                ins.then_inc(S.exp[s], 1)

            def take_transposes(b, h):
                take(act, lambda dst, src: act.activation(dst, src, ACT.Copy), b, h)

            def upper_queries(b, p, buf):
                act.wait_ge(S.q_ready, due(nq(b, p)))
                act.wait_ge(S.s_full[1], due(nh(b - 2, 2 * p + 1)))
                act.activation(qst[buf][:, 2 * p * SEQ:(2 * p + 2) * SEQ], qp[p % 2][:, :], ACT.Copy)
                act.wait_ge(S.q, due(nq(b, p) - 2))
                act.activation(q_all[p % 2][:, :], qp[p % 2][0:AD, :], ACT.Copy).then_inc(S.q_hi, 1)

            def take_pair(b, p):
                act.wait_ge(S.ov_full[p % 2], due(np_(b, p)))
                act.wait_ge(S.turn["wo"], due(n(b - 1)))
                act.activation(oT[:, p, :], ovp[p % 2][:, 0:SEQ], ACT.Copy).then_inc(S.ov_sb[p % 2], 1)

            def iteration(i, par):
                for s in range(AH):
                    if s == 0 and ok(i):
                        upper_queries(i, PAIRS - 1, par)
                    if s - 1 in Q_SLOTS and ok(i + 1):
                        upper_queries(i + 1, Q_SLOTS[s - 1], 1 - par)
                    h = s - PT_LAG
                    if h % 2 == 1:
                        if h >= 0 and ok(i):
                            take_transposes(i, h)
                        if h < 0 and ok(i - 1):
                            take_transposes(i - 1, h + AH)
                    if ok(i):
                        exponentials(i, s)
                    if s == 0 and ok(i + 1):
                        b = i + 1
                        act.wait_ge(S.turn["xt"], due(n(b)))
                        act.wait_ge(S.q_ready, due(nq(b - 1, PAIRS - 1)))
                        act.activation(xT[:, :], misc[:, 0:SEQ], ACT.Identity, scale=T.norm_w[:, 0:1],
                                       bias=T.norm_b[:, 0:1]).then_inc(S.taken["xt"], 1)
                    if s in PAIR_SLOTS:
                        off, p = PAIR_SLOTS[s]
                        if ok(i + off):
                            take_pair(i + off, p)

                    if s == 2 and ok(i + 1):
                        b, buf = i + 1, 1 - par
                        act.wait_ge(S.turn["kv"], due(n(b)))
                        act.wait_ge(S.s_full[1], due(nh(b - 2, AH - 1)))
                        act.wait_ge(S.ov_full[1], due(np_(b - 2, PAIRS - 1)))
                        act.activation(k_hi[buf][:, :], misc[:, 0:SEQ], ACT.Copy, scale=ASCALE)\
                            .then_inc(S.k_hi, 1)
                        act.activation(vals[buf][:, :, :].rearrange("p k d -> p (k d)"),
                                       misc[:, SEQ:SEQ + KT * AD], ACT.Copy).then_inc(S.vals, 1)
            run(act, iteration)

        @block.vector
        def _(dve):
            def row_stats(b):
                for k in range(KT):
                    ins = dve.bn_stats(st6[:, k, :], X[:, cols(b * SEQ + k * D, D)])
                ins.then_inc(S.bn, 1)
                count0 = value(dve, n(b))
                dve.wait_ge(T.made, 1)
                dve.wait_ge(S.bn, count0)
                for k in range(KT):
                    ins = dve.bn_aggr(mv[:, k, :], st6[:, k, :])
                ins.then_inc(S.stats, 1)

            def norm_rows(b):
                dve.wait_ge(S.rnorm, due(n(b)))
                dve.wait_ge(S.turn["xt"], due(n(b - 1)))
                for k in range(KT):
                    ins = dve.tensor_scalar(xn[:, k, :], X[:, cols(b * SEQ + k * D, D)], mv[:, k, 0:1],
                                            rs[:, k:k + 1], ALU.subtract, ALU.mult)
                ins.then_inc(S.xn, 1)

            def maximum(b, h):
                s = h % 2
                dve.wait_ge(S.s_full[s], due(nh(b, h)))
                dve.wait_ge(S.exp[s], due(nh(b, h) - (AH // 2)))
                dve.tensor_reduce(nmax[:, h, :], sp_[s][:, :].rearrange("p (t k) -> p t k", t=KT), AX.X, ALU.max,
                                  negate=True).then_inc(S.mx[s], 1)

            def probabilities(b, h):
                s = h % 2
                dve.wait_ge(S.exp[s], due(nh(b, h)))
                dve.reciprocal(recs[:, h, :], sums[:, h, :]).then_inc(S.rec[s], 1)
                dve.wait_ge(S.rec[s], due(nh(b, h)))
                for t in range(KT):
                    ins = dve.tensor_scalar(pr[:, h % PR4, t, :], pr[:, h % PR4, t, :], recs[:, h, t:t + 1], None,
                                            ALU.mult)
                ins.then_inc(S.pn[s], 1)

            def out_rows(b):
                dve.wait_ge(S.turn["wo"], due(n(b)))
                dve.tensor_copy(o_sb[:, :, :].rearrange("p k d -> p (k d)"), misc[:, 0:KT * D])\
                    .then_inc(S.taken["wo"], 1)
                dve.wait_ge(S.taken["wo"], due(n(b)))
                for k in range(KT):
                    ins = dve.bn_stats(ost6[:, k, :], o_sb[:, k, :])
                ins.then_inc(S.o_bn, 1)
                count0 = value(dve, n(b))
                dve.wait_ge(T.made, 1)
                dve.wait_ge(S.o_bn, count0)
                for k in range(KT):
                    ins = dve.bn_aggr(omv[:, k, :], ost6[:, k, :])
                ins.then_inc(S.o_stats, 1)

            def out_norm(b):
                dve.wait_ge(S.o_rnorm, due(n(b)))
                dve.wait_ge(S.o_w, due(n(b - 1)))
                for k in range(KT):
                    ins = dve.tensor_scalar(o_n[:, k, :], o_sb[:, k, :], omv[:, k, 0:1], ors[:, k:k + 1],
                                            ALU.subtract, ALU.mult)
                ins.then_inc(S.o_norm, 1)

            def iteration(i, par):
                for s in range(AH):
                    if ok(i):
                        maximum(i, s)
                    if s == 3 and ok(i + 1):
                        b, buf = i + 1, 1 - par
                        dve.wait_ge(S.k_hi, due(n(b)))
                        dve.wait_ge(S.vals, due(n(b)))
                        dve.scalar_tensor_tensor(k_lo[buf][:, :], misc[:, 0:SEQ], ASCALE,
                                                 k_hi[buf][:, :].bitcast(F32), op0=ALU.mult, op1=ALU.subtract)\
                            .then_inc(S.taken["kv"], 1)
                    if s and ok(i):
                        probabilities(i, s - 1)
                    if s == 0 and ok(i - 1):
                        probabilities(i - 1, AH - 1)
                    h = s - PT_LAG
                    if s == 4 and ok(i - 1):
                        out_rows(i - 1)
                    if s == 7 and ok(i - 1):
                        out_norm(i - 1)
                    if h % 2 == 0:
                        if h >= 0 and ok(i):
                            take(dve, dve.tensor_copy, i, h)
                        if h < 0 and ok(i - 1):
                            take(dve, dve.tensor_copy, i - 1, h + AH)
                    if s == 5 and ok(i + 2):
                        norm_rows(i + 2)

                    if s == 4 and ok(i + 2):
                        row_stats(i + 2)
            run(dve, iteration)

        @block.tensor
        def _(pe):
            def scores(b, h, buf):
                s = h % 2
                pe.wait_ge(S.q, due(nq(b, h // 2)))
                if h == 0:
                    pe.wait_ge(S.taken["kv"], due(n(b)))
                pe.wait_ge(S.exp[s], due(nh(b, h) - 1))
                for t in range(KT):
                    q = qst[buf][:, h * SEQ + t * P:h * SEQ + (t + 1) * P]
                    out = sp_[s][:, t * SEQ:(t + 1) * SEQ]
                    pe.matmul(out, q, k_lo[buf][:, :], start=(t == 0), stop=False, skip_group_check=True)
                    ins = pe.matmul(out, q, k_hi[buf][:, :], start=False, stop=(t == KT - 1),
                                    skip_group_check=True)
                ins.then_inc(S.s_full[s], 1)

            def transposes(b, h):
                s = h % 2
                pe.wait_ge(S.pn[s], due(nh(b, h)))
                pe.wait_ge(S.pt_sb[1 - s], due(nh(b, h - 1) if h else nh(b - 1, AH - 1)))
                for kt in range(KT):
                    for t in range(KT):
                        at = kt * SEQ + t * P
                        ins = pe.transpose(ptp[:, at:at + P], pr[:, h % PR4, t, kt * P:(kt + 1) * P],
                                           T.ident[:, :])
                ins.then_inc(S.pt_full[s], 1)

            def value_products(b, p, buf):
                for s in range(2):
                    pe.wait_ge(S.pt_sb[s], due(nh(b, 2 * p + s)))
                pe.wait_ge(S.ov_sb[p % 2], due(np_(b, p) - 1))
                for kt in range(KT):
                    for m in range(2):
                        ins = pe.matmul(ovp[p % 2][AD * m:AD * (m + 1), 0:SEQ], vals[buf][:, kt, :],
                                        pt[:, (2 * p + m) % PR4, kt, :], start=(kt == 0), stop=(kt == KT - 1),
                                        skip_group_check=True)
                ins.then_inc(S.ov_full[p % 2], 1)

            def turn(kind, b):
                if kind == "xt":
                    pe.wait_ge(S.xn, due(n(b)))
                    for k in range(KT):
                        ins = pe.transpose(misc[:, k * P:(k + 1) * P], xn[:, k, :], T.ident[:, :])
                elif kind == "kv":
                    pe.matmul(misc[:, 0:SEQ], T.awk[:, :], xT[:, :], start=True, stop=True)
                    for k in range(KT):
                        ins = pe.matmul(misc[:, SEQ + k * AD:SEQ + (k + 1) * AD], xT[:, k * P:(k + 1) * P],
                                        T.awv[:, :], start=True, stop=True)
                else:
                    for r in range(2):
                        pe.wait_ge(S.ov_sb[r], due(np_(b, PAIRS - 2 + r)))
                    for k in range(KT):
                        for p in range(PAIRS):
                            ins = pe.matmul(misc[:, k * D:(k + 1) * D], oT[:, p, k * P:(k + 1) * P],
                                            T.awo[:, p * D:(p + 1) * D], start=(p == 0), stop=(p == PAIRS - 1))
                return ins

            def iteration(i, par):
                for s in range(AH):
                    if ok(i):
                        scores(i, s, par)
                    if s in MULTI_MISC:
                        kind, off = MULTI_MISC[s]
                        if ok(i + off):
                            prev = before(i, kind)
                            if prev:
                                pe.wait_ge(S.taken[prev[0]], due(n(prev[1])))
                            turn(kind, i + off).then_inc(S.turn[kind], 1)
                    if s in Q_SLOTS and ok(i + 1):
                        b, p = i + 1, Q_SLOTS[s]
                        pe.wait_ge(S.taken["xt"], due(n(b)))
                        pe.wait_ge(S.q_hi, due(nq(b, p) - 2))
                        for m in range(2):
                            h2 = 2 * p + m
                            ins = pe.matmul(qp[p % 2][:, m * SEQ:(m + 1) * SEQ], T.awq[:, h2 * P:(h2 + 1) * P],
                                            xT[:, :], start=True, stop=True)
                        ins.then_inc(S.q_ready, 1)
                    h = s - PT_LAG
                    if h < 0 and ok(i - 1):
                        transposes(i - 1, h + AH)
                    if s in PAIR_SLOTS:
                        off, p = PAIR_SLOTS[s]
                        if ok(i + off):
                            value_products(i + off, p, (par + off) % 2)

                    if h >= 0 and ok(i):
                        transposes(i, h)
            run(pe, iteration)


def rotary_tables():
    half = MD // 2
    inv_freq = (np.float32(1.0) / np.float32(10000.0) ** (np.arange(half, dtype=np.float32) / np.float32(half)))
    angle = np.arange(SEQ, dtype=np.float32)[:, None] * inv_freq[None, :].astype(np.float32)
    cos, sin = np.cos(angle).T, np.sin(angle).T
    cos8 = np.concatenate([cos, cos])
    sin8 = np.concatenate([-sin, sin])
    rows = lambda a: np.ascontiguousarray(np.tile(np.repeat(a, HH, axis=0), (2, 1)), dtype=np.float32)
    return rows(cos8), rows(sin8)


def by_dim(w, swap=False):
    w = w.reshape(MH, MD, w.shape[1])
    if swap:
        w = np.concatenate([w[:, MD // 2:], w[:, :MD // 2]], axis=1)
    w = w.reshape(2, HH, MD, w.shape[2])
    return np.ascontiguousarray(w.transpose(3, 0, 2, 1).reshape(w.shape[3], MH * MD))


def laid_out(v):
    v = {k: np.asarray(a) for k, a in v.items()}
    cos, sin = rotary_tables()
    col = lambda a: np.ascontiguousarray(a.reshape(-1, 1))
    a = {
        "x": v["L0_attn_x"],
        "wq": by_dim(v["L0_ffn_Wq"]), "wq_swap": by_dim(v["L0_ffn_Wq"], True),
        "wuk": by_dim(v["L0_ffn_Wuk"]), "wuk_swap": by_dim(v["L0_ffn_Wuk"], True),
        "wuv": np.ascontiguousarray(v["L0_ffn_Wuv"].T), "wo": np.ascontiguousarray(v["L0_ffn_Wo"].T),
        "wdkv": np.ascontiguousarray(v["L0_ffn_Wdkv"].T), "cos": cos, "sin": sin,
        "norm2": col(v["L0_ffn_norm2_w"]), "gate": np.ascontiguousarray(v["L0_ffn_gate_w"].T),
        "gate_b": v["L0_ffn_gate_b"].reshape(1, NE),
        "b1": np.ascontiguousarray(v["L0_ffn_b1"].reshape(NE * HC, P).T), "b2": np.ascontiguousarray(v["L0_ffn_b2"].T),
        "w1": np.ascontiguousarray(v["L0_ffn_W1"].transpose(2, 0, 1).reshape(D, NE * HID)),
        "w2": np.ascontiguousarray(v["L0_ffn_W2"].reshape(NE, D, HC, P).transpose(3, 0, 2, 1).reshape(P, NE * HC * D)),
        "awq": np.ascontiguousarray(np.repeat(v["L0_attn_Wq"].reshape(D, AH, 1, AD), 2, axis=2).reshape(D, AH * P)),
        "awk": np.ascontiguousarray(np.concatenate([v["L0_attn_Wkv"][:, :AD]] * 2, axis=1)),
        "awv": np.ascontiguousarray(v["L0_attn_Wkv"][:, AD:]),
        "awo": np.ascontiguousarray(v["L0_attn_Wo"].reshape(PAIRS, P, D).transpose(1, 0, 2).reshape(P, PAIRS * D)),
        "norm_w": col(v["L0_attn_norm_w"]), "norm_b": col(v["L0_attn_norm_b"]),
        "out_w": v["L0_attn_out_norm_w"].reshape(1, D), "out_b": v["L0_attn_out_norm_b"].reshape(1, D),
        "norm1": col(v["L0_ffn_norm1_w"]), "ln_g": col(v["L0_ffn_ln_g"]), "ln_b": col(v["L0_ffn_ln_b"]),
    }
    pack = lambda widths: np.ascontiguousarray(np.concatenate([a[key] for key in widths], axis=1))
    return {
        "x": a["x"], "w1": a["w1"], "w2": a["w2"],
        "latent_weights": pack(LATENT_WEIGHTS), "latent_rows": pack(LATENT_ROWS), "weights": pack(WEIGHTS),
        "spread": pack(SPREAD),
    }


def build(nc, A, out):
    ctx = ExitStack()
    with ctx:
        def sb(name, shape, dt=F32):
            return ctx.enter_context(nc.sbuf_tensor(name, shape, dt))

        def sem(name):
            return ctx.enter_context(nc.semaphore(name))

        T = Tiles()
        T.made = sem("made")
        T.X = sb("X", [P, NT * D])
        T.U = sb("U", [P, NT * D])
        def packed(name, rows, widths):
            tile = sb(name, [rows, sum(widths.values())])
            at, views = 0, {}
            for key, width in widths.items():
                views[key] = tile[:, at:at + width]
                at += width
            return tile, views

        T.latent_weights, lw = packed("latent_weights", P, LATENT_WEIGHTS)
        T.latent_rows, lr = packed("latent_rows", LAT, LATENT_ROWS)
        T.weights, w = packed("weights", P, WEIGHTS)
        T.spread, sw = packed("spread", P, SPREAD)
        T.wdkv, T.wq, T.wq_swap, T.wo = lw["wdkv"], lw["wq"], lw["wq_swap"], lw["wo"]
        T.cos, T.sin, T.norm1 = lw["cos"], lw["sin"], lw["norm1"]
        T.wuk, T.wuk_swap, T.wuv, T.ln_g, T.ln_b = lr["wuk"], lr["wuk_swap"], lr["wuv"], lr["ln_g"], lr["ln_b"]
        T.norm2, T.gate, T.gate_b, T.b1, T.b2 = w["norm2"], w["gate"], sw["gate_b"], w["b1"], w["b2"]
        T.awq, T.awk, T.awv, T.awo = w["awq"], w["awk"], w["awv"], w["awo"]
        T.norm_w, T.norm_b, T.out_w, T.out_b = w["norm_w"], w["norm_b"], sw["out_w"], sw["out_b"]
        T.stack = [sb(f"stack{n}", [P, MH * 2 * SEQ], F32R) for n in range(2)]
        T.va = [sb(f"va{n}", [P, KT, MH, MW]) for n in range(2)]
        T.w1_raw = T.U[:, NT * D - NQ * P:NT * D]
        T.w1_hi, T.w1_lo = sb("w1_hi", [D, NQ * P], F32R), sb("w1_lo", [D, NQ * P], F32R)
        T.w2_hi, T.w2_lo = sb("w2_hi", [P, NQ * D], F32R), sb("w2_lo", [P, NQ * D], F32R)
        T.neghalf = sb("neghalf", [P, 2, KT])
        T.ident, T.ident_bf = sb("ident", [P, P]), sb("ident_bf", [P, P], BF16)
        T.neg = sb("neg", [P, 4, P], BF16)

        mla, moe, mqa = MlaSems(sem), MoeSems(sem), MqaSems(sem)
        L = LoadSems(sem)
        setup_phase(nc, T, A, L)
        mla_phase(nc, T, mla, 0, L, A)
        moe_phase(nc, T, moe, 0)
        mqa_phase(nc, T, mqa)
        mla_phase(nc, T, mla, NB)
        moe_phase(nc, T, moe, NC, out)


def kernel(**inputs):
    import concourse.bacc as bacc
    from concourse.bass_utils import run_bass_kernel_spmd

    arrays = laid_out(inputs)
    nc = bacc.Bacc("TRN2", target_bir_lowering=False, num_devices=1)
    dram = {name: nc.dram_tensor(f"in_{name}", a.shape, mybir.dt.from_np(a.dtype), kind="ExternalInput").ap()
            for name, a in arrays.items()}
    out = nc.dram_tensor("out", (NB, SEQ, D), F32, kind="ExternalOutput").ap()
    build(nc, dram, out)
    result = run_bass_kernel_spmd(nc, [{f"in_{name}": a for name, a in arrays.items()}], core_ids=[0])
    return result.results[0]["out"]
```
